# Optimizing a Trainium2 kernel written in Bass

```python
import numpy as np
import jax
import jax.numpy as jnp

def _softmax(x, axis=-1):
    return jax.nn.softmax(x, axis=axis)

def _gelu(x):
    return jax.nn.gelu(x, approximate=True)

def _silu(x):
    return jax.nn.silu(x)

def _sigmoid(x):
    return jax.nn.sigmoid(x)

def _layernorm(x, axis=-1, eps=1e-05):
    m = jnp.mean(x, axis=axis, keepdims=True)
    v = jnp.var(x, axis=axis, keepdims=True)
    return (x - m) / jnp.sqrt(v + eps)

def _scatter_add(tgt, idx, src, axis=0):
    return tgt.at[idx].add(src)

def _segment_sum(src, seg, n):
    return jax.ops.segment_sum(src, seg, n)
kernel_name = 'mk_early_fusion_d1_tok_img1024_r4_e53ca8'

def setup_inputs(seed: int=0):
    np.random.seed(seed)
    _w = jnp.asarray

    def _rec_inputs():
        import jax
        import jax.numpy as jnp
        _rk = jax.random.key(seed)
        x = -0.00016672 + 0.999947 * jax.random.normal(jax.random.fold_in(_rk, 1), (16, 3, 96, 96), jnp.float32)
        txt = 0.434251 + 1.14597 * jax.random.normal(jax.random.fold_in(_rk, 2), (16, 32, 256), jnp.float32)
        return (x, txt)
    x, txt = _rec_inputs()

    def _L0_tok_setup():
        import jax, jax.numpy as jnp
        import numpy as np
        DIM = 256
        IMG = 96
        P = 16
        C = 3
        TEMP = 10000.0
        EPS = 1e-05
        PATCH_DIM = C * P * P
        HP = IMG // P

        def layernorm(x, gamma, beta):
            mu = jnp.mean(x, axis=-1, keepdims=True)
            var = jnp.var(x, axis=-1, keepdims=True)
            return (x - mu) * jax.lax.rsqrt(var + EPS) * gamma + beta

        def posemb_sincos_2d(h, w, dim, dtype):
            y, x = jnp.meshgrid(jnp.arange(h), jnp.arange(w), indexing='ij')
            omega = jnp.arange(dim // 4, dtype=jnp.float32) / (dim // 4 - 1)
            omega = 1.0 / TEMP ** omega
            y = y.reshape(-1)[:, None] * omega[None, :]
            x = x.reshape(-1)[:, None] * omega[None, :]
            pe = jnp.concatenate((jnp.sin(x), jnp.cos(x), jnp.sin(y), jnp.cos(y)), axis=1)
            return pe.astype(dtype)
        key = jax.random.key(seed)
        ks = jax.random.split(key, 8)
        B = 64
        img = jax.random.normal(ks[0], (B, C, IMG, IMG), dtype=jnp.float32)
        cls_token = jax.random.normal(ks[1], (1, 1, DIM), dtype=jnp.float32)
        cls_pos_embedding = jax.random.normal(ks[2], (1, 1, DIM), dtype=jnp.float32)
        ln1_g = jnp.ones((PATCH_DIM,), jnp.float32)
        ln1_b = jnp.zeros((PATCH_DIM,), jnp.float32)
        W = jax.random.normal(ks[3], (PATCH_DIM, DIM), dtype=jnp.float32) / np.sqrt(PATCH_DIM)
        bias = jnp.zeros((DIM,), jnp.float32)
        ln2_g = jnp.ones((DIM,), jnp.float32)
        ln2_b = jnp.zeros((DIM,), jnp.float32)
        return {'img': img, 'cls_token': cls_token, 'cls_pos_embedding': cls_pos_embedding, 'ln1_g': ln1_g, 'ln1_b': ln1_b, 'W': W, 'bias': bias, 'ln2_g': ln2_g, 'ln2_b': ln2_b}
    _L0_tok_all = _L0_tok_setup()
    _L0_tok_in = {k: v for k, v in _L0_tok_all.items() if k in ('cls_token', 'cls_pos_embedding', 'ln1_g', 'ln1_b', 'W', 'bias', 'ln2_g', 'ln2_b')}
    del _L0_tok_all

    def _L0_attn_setup():
        import math
        import jax, jax.numpy as jnp
        import numpy as np
        N_HEADS = 16
        ROPE_BASE = 10000.0

        def rotate_half(x):
            x_even = x[..., ::2]
            x_odd = x[..., 1::2]
            return jnp.stack((-x_odd, x_even), axis=-1).reshape(x.shape)

        def rope_cache(seq_len, head_dim, dtype):
            pos = jnp.arange(seq_len, dtype=jnp.float32)
            freqs = 1.0 / ROPE_BASE ** (jnp.arange(0, head_dim, 2, dtype=jnp.float32) / head_dim)
            angles = pos[:, None] * freqs[None, :]
            cos = jnp.repeat(jnp.cos(angles), 2, axis=-1).astype(dtype)
            sin = jnp.repeat(jnp.sin(angles), 2, axis=-1).astype(dtype)
            return (cos, sin)
        key = jax.random.key(seed)
        ks = jax.random.split(key, 5)
        B, S, D = (2, 512, 256)
        scale = 1.0 / math.sqrt(D)
        return {'x': jax.random.normal(ks[0], (B, S, D), dtype=jnp.float32), 'wq': jax.random.normal(ks[1], (D, D), dtype=jnp.float32) * scale, 'wk': jax.random.normal(ks[2], (D, D), dtype=jnp.float32) * scale, 'wv': jax.random.normal(ks[3], (D, D), dtype=jnp.float32) * scale, 'wo': jax.random.normal(ks[4], (D, D), dtype=jnp.float32) * scale}
    _L0_attn_all = _L0_attn_setup()
    _L0_attn_in = {k: v for k, v in _L0_attn_all.items() if k in ('wq', 'wk', 'wv', 'wo')}
    del _L0_attn_all

    def _L0_ffn_setup():
        import jax, jax.numpy as jnp
        import numpy as np
        E = 8
        H = 256
        M = 512
        K = 2
        SE = 1
        BSZ, SEQ = (2, 256)
        W_SCALE = 0.02
        key = jax.random.key(seed)
        ks = jax.random.split(key, 9)
        return {'x': jax.random.normal(ks[0], (BSZ, SEQ, H), jnp.float32), 'gate_w': jax.random.normal(ks[1], (E, H), jnp.float32) * W_SCALE, 'beta': jnp.zeros((E,), jnp.float32), 'gate_proj_w': jax.random.normal(ks[2], (E, H, M), jnp.float32) * W_SCALE, 'up_proj_w': jax.random.normal(ks[3], (E, H, M), jnp.float32) * W_SCALE, 'down_proj_w': jax.random.normal(ks[4], (E, M, H), jnp.float32) * W_SCALE, 'shared_gate_w': jax.random.normal(ks[5], (SE, H, M), jnp.float32) * W_SCALE, 'shared_up_w': jax.random.normal(ks[6], (SE, H, M), jnp.float32) * W_SCALE, 'shared_down_w': jax.random.normal(ks[7], (SE, M, H), jnp.float32) * W_SCALE}
    _L0_ffn_all = _L0_ffn_setup()
    _L0_ffn_in = {k: v for k, v in _L0_ffn_all.items() if k in ('gate_w', 'beta', 'gate_proj_w', 'up_proj_w', 'down_proj_w', 'shared_gate_w', 'shared_up_w', 'shared_down_w')}
    del _L0_ffn_all
    return {'x': x, 'txt': txt, 'L0_tok_cls_token': _L0_tok_in['cls_token'], 'L0_tok_cls_pos_embedding': _L0_tok_in['cls_pos_embedding'], 'L0_tok_ln1_g': _L0_tok_in['ln1_g'], 'L0_tok_ln1_b': _L0_tok_in['ln1_b'], 'L0_tok_W': _L0_tok_in['W'], 'L0_tok_bias': _L0_tok_in['bias'], 'L0_tok_ln2_g': _L0_tok_in['ln2_g'], 'L0_tok_ln2_b': _L0_tok_in['ln2_b'], 'L0_attn_wq': _L0_attn_in['wq'], 'L0_attn_wk': _L0_attn_in['wk'], 'L0_attn_wv': _L0_attn_in['wv'], 'L0_attn_wo': _L0_attn_in['wo'], 'L0_ffn_gate_w': _L0_ffn_in['gate_w'], 'L0_ffn_beta': _L0_ffn_in['beta'], 'L0_ffn_gate_proj_w': _L0_ffn_in['gate_proj_w'], 'L0_ffn_up_proj_w': _L0_ffn_in['up_proj_w'], 'L0_ffn_down_proj_w': _L0_ffn_in['down_proj_w'], 'L0_ffn_shared_gate_w': _L0_ffn_in['shared_gate_w'], 'L0_ffn_shared_up_w': _L0_ffn_in['shared_up_w'], 'L0_ffn_shared_down_w': _L0_ffn_in['shared_down_w']}

def reference(x, txt, L0_tok_cls_token, L0_tok_cls_pos_embedding, L0_tok_ln1_g, L0_tok_ln1_b, L0_tok_W, L0_tok_bias, L0_tok_ln2_g, L0_tok_ln2_b, L0_attn_wq, L0_attn_wk, L0_attn_wv, L0_attn_wo, L0_ffn_gate_w, L0_ffn_beta, L0_ffn_gate_proj_w, L0_ffn_up_proj_w, L0_ffn_down_proj_w, L0_ffn_shared_gate_w, L0_ffn_shared_up_w, L0_ffn_shared_down_w):
    import jax
    import jax.numpy as jnp

    def _L0_tok_ref(img, cls_token, cls_pos_embedding, ln1_g, ln1_b, W, bias, ln2_g, ln2_b):
        import jax, jax.numpy as jnp
        import numpy as np
        DIM = 256
        IMG = 96
        P = 16
        C = 3
        TEMP = 10000.0
        EPS = 1e-05
        PATCH_DIM = C * P * P
        HP = IMG // P

        def layernorm(x, gamma, beta):
            mu = jnp.mean(x, axis=-1, keepdims=True)
            var = jnp.var(x, axis=-1, keepdims=True)
            return (x - mu) * jax.lax.rsqrt(var + EPS) * gamma + beta

        def posemb_sincos_2d(h, w, dim, dtype):
            y, x = jnp.meshgrid(jnp.arange(h), jnp.arange(w), indexing='ij')
            omega = jnp.arange(dim // 4, dtype=jnp.float32) / (dim // 4 - 1)
            omega = 1.0 / TEMP ** omega
            y = y.reshape(-1)[:, None] * omega[None, :]
            x = x.reshape(-1)[:, None] * omega[None, :]
            pe = jnp.concatenate((jnp.sin(x), jnp.cos(x), jnp.sin(y), jnp.cos(y)), axis=1)
            return pe.astype(dtype)
        b = img.shape[0]
        x = img.reshape(b, C, HP, P, HP, P)
        x = jnp.transpose(x, (0, 2, 4, 3, 5, 1))
        x = x.reshape(b, HP, HP, PATCH_DIM)
        x = layernorm(x, ln1_g, ln1_b)
        x = jnp.einsum('bhwp,pd->bhwd', x, W) + bias
        x = layernorm(x, ln2_g, ln2_b)
        pe = posemb_sincos_2d(HP, HP, DIM, x.dtype)
        x = x.reshape(b, HP * HP, DIM) + pe[None]
        cls_tokens = jnp.broadcast_to(cls_token + cls_pos_embedding, (b, 1, DIM))
        return jnp.concatenate((cls_tokens, x), axis=1)

    def _L0_attn_ref(x, wq, wk, wv, wo):
        import math
        import jax, jax.numpy as jnp
        import numpy as np
        N_HEADS = 16
        ROPE_BASE = 10000.0

        def rotate_half(x):
            x_even = x[..., ::2]
            x_odd = x[..., 1::2]
            return jnp.stack((-x_odd, x_even), axis=-1).reshape(x.shape)

        def rope_cache(seq_len, head_dim, dtype):
            pos = jnp.arange(seq_len, dtype=jnp.float32)
            freqs = 1.0 / ROPE_BASE ** (jnp.arange(0, head_dim, 2, dtype=jnp.float32) / head_dim)
            angles = pos[:, None] * freqs[None, :]
            cos = jnp.repeat(jnp.cos(angles), 2, axis=-1).astype(dtype)
            sin = jnp.repeat(jnp.sin(angles), 2, axis=-1).astype(dtype)
            return (cos, sin)
        B, S, D = x.shape
        H = N_HEADS
        hd = D // H

        def split_heads(t):
            return t.reshape(B, S, H, hd).transpose(0, 2, 1, 3)
        q = split_heads(x @ wq.T)
        k = split_heads(x @ wk.T)
        v = split_heads(x @ wv.T)
        cos, sin = rope_cache(S, hd, x.dtype)
        cos = cos[None, None]
        sin = sin[None, None]
        q = q * cos + rotate_half(q) * sin
        k = k * cos + rotate_half(k) * sin
        scores = jnp.einsum('bhqd,bhkd->bhqk', q, k) / math.sqrt(hd)
        causal_mask = jnp.triu(jnp.ones((S, S), dtype=bool), k=1)
        scores = jnp.where(causal_mask, jnp.finfo(scores.dtype).min, scores)
        pattern = jax.nn.softmax(scores, axis=-1)
        head_out = jnp.einsum('bhqk,bhkd->bhqd', pattern, v)
        merged = head_out.transpose(0, 2, 1, 3).reshape(B, S, D)
        out = merged @ wo.T
        return out

    def _L0_ffn_ref(x, gate_w, beta, gate_proj_w, up_proj_w, down_proj_w, shared_gate_w, shared_up_w, shared_down_w):
        import jax, jax.numpy as jnp
        import numpy as np
        E = 8
        H = 256
        M = 512
        K = 2
        SE = 1
        BSZ, SEQ = (2, 256)
        W_SCALE = 0.02
        B0, S0, H0 = x.shape
        xt = x.reshape(-1, H0)
        B = xt.shape[0]
        logits = xt @ gate_w.T
        _, idx = jax.lax.top_k(logits + beta, K)
        probs = jax.nn.sigmoid(jnp.take_along_axis(logits, idx, axis=-1))
        c = jnp.zeros((B, E), xt.dtype).at[jnp.arange(B)[:, None], idx].add(probs)
        g = jnp.einsum('bh,ehm->bem', xt, gate_proj_w)
        u = jnp.einsum('bh,ehm->bem', xt, up_proj_w)
        h = jax.nn.silu(g) * u
        eo = jnp.einsum('bem,emh->beh', h, down_proj_w)
        combined = jnp.einsum('beh,be->bh', eo, c)
        sg = jnp.einsum('bh,ehm->bem', xt, shared_gate_w)
        su = jnp.einsum('bh,ehm->bem', xt, shared_up_w)
        sh = jax.nn.silu(sg) * su
        shared_out = jnp.einsum('bem,emh->beh', sh, shared_down_w).sum(axis=1)
        return (combined + shared_out).reshape(B0, S0, H0)
    h = _L0_tok_ref(x, L0_tok_cls_token, L0_tok_cls_pos_embedding, L0_tok_ln1_g, L0_tok_ln1_b, L0_tok_W, L0_tok_bias, L0_tok_ln2_g, L0_tok_ln2_b)
    h = jnp.concatenate([h, txt], axis=1)
    h = h + _L0_attn_ref(_layernorm(h, axis=-1), L0_attn_wq, L0_attn_wk, L0_attn_wv, L0_attn_wo)
    h = h + _L0_ffn_ref(_layernorm(h, axis=-1), L0_ffn_gate_w, L0_ffn_beta, L0_ffn_gate_proj_w, L0_ffn_up_proj_w, L0_ffn_down_proj_w, L0_ffn_shared_gate_w, L0_ffn_shared_up_w, L0_ffn_shared_down_w)
    return h

_drawn_inputs = setup_inputs


def setup_inputs(seed=0):
    import zlib

    import numpy as np

    out = dict(_drawn_inputs(seed))
    spreads = {'L0_tok_ln1_g': (1.0, 0.2),
     'L0_tok_ln1_b': (0.0, 0.1),
     'L0_tok_bias': (0.0, 0.1),
     'L0_tok_ln2_g': (1.0, 0.2),
     'L0_tok_ln2_b': (0.0, 0.1),
     'L0_ffn_beta': (0.0, 0.799)}
    factors = {'L0_ffn_gate_w': 4.318,
     'L0_ffn_gate_proj_w': 3.729,
     'L0_ffn_up_proj_w': 3.673,
     'L0_ffn_down_proj_w': 3.677,
     'L0_ffn_shared_gate_w': 3.184,
     'L0_ffn_shared_up_w': 3.112,
     'L0_ffn_shared_down_w': 3.12}
    for name, (base, spread) in spreads.items():
        noise = np.random.default_rng([zlib.crc32(name.encode()), seed]).standard_normal(out[name].shape)
        drawn = base * np.exp(spread * noise) if base else spread * noise
        out[name] = jnp.asarray(drawn.astype(out[name].dtype))
    for name, factor in factors.items():
        out[name] = (out[name] * factor).astype(out[name].dtype)
    return out
```

```python
from contextlib import ExitStack

import numpy as np

import concourse.bass as bass
from concourse import mybir

F32 = mybir.dt.float32
BF16 = mybir.dt.bfloat16
I32 = mybir.dt.int32
ALU = mybir.AluOpType
ACT = mybir.ActivationFunctionType
AX_X = mybir.AxisListType.X

P = 128
B = 16
C, IMG, PS = 3, 96, 16
HP = IMG // PS
NPATCH = HP * HP
PD = C * PS * PS
PDC = PD // P
TXT = 32
S = 1 + NPATCH + TXT
D = 256
DC = D // P
NH, HD = 16, 16
HPT = P // HD
TOK = B * S
PAIRS = B // 2
PT = 96
NPT = B * NPATCH // PT
E, M, K = 8, 512, 2
MC = M // P
NT = -(-TOK // P)
LAST = TOK - (NT - 1) * P
NB = (K * TOK + E * (P - 1)) // P
NU = NT + NB
EPS = 1e-5
FAR = -1.0e30
QH = 4
QC = QH * S


def shape_constants():
    f = np.float32
    omega = (np.arange(D // 4, dtype=f) / f(D // 4 - 1)).astype(f)
    omega = (f(1.0) / np.power(f(10000.0), omega)).astype(f)
    yy, xx = np.meshgrid(np.arange(HP), np.arange(HP), indexing="ij")
    y = yy.reshape(-1)[:, None].astype(f) * omega[None]
    x = xx.reshape(-1)[:, None].astype(f) * omega[None]
    pe = np.concatenate((np.sin(x), np.cos(x), np.sin(y), np.cos(y)), axis=1).astype(f)
    pe = np.tile(pe, (B, 1)).reshape(NPT, PT, D).transpose(1, 0, 2).reshape(PT, NPT * D)
    freqs = (f(1.0) / np.power(f(10000.0), np.arange(0, HD, 2, dtype=f) / f(HD))).astype(f)
    ang = np.arange(S, dtype=f)[:, None] * freqs[None]
    cos = np.repeat(np.cos(ang), 2, axis=1).T
    sin = np.repeat(np.sin(ang), 2, axis=1).T * np.where(np.arange(HD) % 2 == 0, -1, 1)[:, None]
    rope = np.stack([np.tile(t, (HPT, 2 * DC)) for t in (cos, sin)], axis=1).astype(f)
    rope = rope.reshape(P, 2 * DC * 2 * S)
    heads = (np.arange(P)[:, None] // HD == np.arange(HPT)[None]).astype(f)
    ident = np.eye(P, dtype=f)
    causal = np.where(np.arange(S)[None] > np.arange(S)[:, None], FAR, 0.0).astype(f)
    before = (np.arange(P)[:, None] < np.arange(P)[None]).astype(f)
    first = np.tile(E - np.arange(E, dtype=f), NT)
    valid = (np.arange(NT * P) < TOK).astype(f).reshape(NT, P).T
    valid = np.repeat(valid, E, axis=1)
    steps = np.tile(np.arange(NT, dtype=f) * P, E)
    lower = (np.arange(E)[:, None] > np.arange(E)[None]).astype(f).reshape(-1)
    blocks = np.repeat(np.arange(NB, dtype=f), E)
    rows = np.concatenate([first, steps, lower, blocks])
    route = np.concatenate([np.tile(rows, (P, 1)), valid], axis=1).astype(f)
    return {"c_pe": pe.astype(f), "c_rope": rope, "c_heads": heads, "c_ident": ident,
            "c_causal": causal, "c_before": before, "c_route": route}


class Chain:

    def __init__(self, eng, sem):
        self.eng, self.sem, self.base, self.n = eng, sem, 0, 0

    def enter(self, round_, per):
        self.start, self.per = self.n, per
        self.base = round_ * per

    def leave(self, rounds):
        assert self.n - self.start == self.per, (self.n - self.start, self.per)
        self.n = self.start + rounds * self.per
        self.base = 0

    def __call__(self, ins):
        ins.then_inc(self.sem, 1)
        self.n += 1
        self.eng.wait_ge(self.sem, self.base + self.n)


def build(nc, a, out):
    ctx = ExitStack()
    with ctx:
        def sb(name, shape, dt=F32):
            return ctx.enter_context(nc.sbuf_tensor(name, shape, dt))

        def sem(name):
            return ctx.enter_context(nc.semaphore(name))

        def sems(name, n):
            return [sem(f"{name}{i}") for i in range(n)]

        patches_d = nc.dram_tensor("patches_d", [B * NPATCH, D], F32).ap()
        rows_d = nc.dram_tensor("rows_d", [NB * P, D], F32).ap()
        y_d = nc.dram_tensor("y_d", [NB * P, D], F32).ap()
        h1_d = nc.dram_tensor("h1_d", [TOK, D], F32).ap()

        wqk = sb("wqk", [P, DC * 2 * D])
        wv = sb("wv", [P, DC * D])
        wo = sb("wo", [P, DC * D])
        wgate = sb("wgate", [P, DC * E])
        wgu = sb("wgu", [P, (E + 1) * DC * 2 * M])
        wdn = sb("wdn", [P, (E + 1) * MC * D])
        ln1gb = sb("ln1gb", [P, 2 * PDC])
        rowp = sb("rowp", [PT, 3 * D])
        rope = sb("rope", [P, 2 * 2 * DC * S])
        heads = sb("heads", [P, HPT])
        ident = sb("ident", [P, P])
        identb = sb("identb", [P, P], BF16)
        causalb = sb("causalb", [S, S], BF16)
        beforeb = sb("beforeb", [P, P], BF16)
        onesb = sb("onesb", [P, P], BF16)
        zero = sb("zero", [P, D])
        TE = NT * E
        NR = 2 * TE + E * E + NB * E
        route = sb("route", [P, NR + TE])
        beta = sb("beta", [P, E])
        cls = sb("cls", [1, 2 * D])
        stats = sb("stats", [P, 12])
        stats_all = sb("stats_all", [P, 6 * B])
        mv = sb("mv", [P, 2 * 2])
        dev = sb("dev", [P, 2])
        rstd = sb("rstd", [P, 2])
        mv_all = sb("mv_all", [P, 2 * B])
        dev_all = sb("dev_all", [P, B])
        rstd_all = sb("rstd_all", [P, B])
        eps = sb("eps", [P, 1])
        mx = sb("mx", [S, NH])
        rs = sb("rs", [S, NH])
        m12z = sb("m12z", [P, 2 * TE - E], BF16)
        m12 = m12z[:, TE - E:]
        rsm = sb("rsm", [P, 6 * NT])
        nb = sb("nb", [P, 4 * E])
        eidf = sb("eidf", [P, NB])
        eid = sb("eid", [P, NB], I32)
        slot = [sb(f"slot{i}", [P, NT], I32) for i in range(K)]
        csel = sb("csel", [P, K * NT])
        stream = sb("stream", [P, B * D])
        h_all = stream[0:S, :]
        acc = stream[:, 0:NT * D]

        class Arena:

            def __init__(self, name, words):
                self.whole, self.words, self.at = sb(name, [P, words]), words, 0

            def take(self, rows, words):
                part = self.whole[0:rows, self.at:self.at + words]
                self.at += words
                assert self.at <= self.words
                return part

            def again(self):
                self.at = 0

        early = Arena("early", 2 * PD * 2 + 3 * PDC * PT + 2 * D + NPT * D + PDC * D)
        wpatch = early.take(P, PDC * D)
        pe = early.take(PT, NPT * D)
        xp = [early.take(PT, PD) for _ in range(2)]
        xn = [early.take(PT, PD) for _ in range(2)]
        xnT = [early.take(P, PDC * PT) for _ in range(2)]
        yt = [early.take(PT, D) for _ in range(2)]
        ln1b = early.take(P, PDC * PT)
        early.again()
        n_t = early.take(S, 2 * D)
        W2 = DC * 2 * S
        nT, qc, kc, qs, ks, qr, kr = (early.take(P, W2) for _ in range(7))
        v_sb = early.take(S, 2 * NH * (HD + 1))
        on = early.take(S, D)
        oT = early.take(P, DC * S)
        m_all = early.take(P, NT * D)
        lg = early.take(P, TE)
        rt = early.take(P, 6 * TE)
        wide = early.take(P, NB * E)

        late = Arena("late", max(DC * HPT * 2 * S + 3 * NH * S, NT * D + 4 * D + 4 * M + D))
        kbd = late.take(P, DC * HPT * 2 * S)
        prob = [late.take(S, NH * S) for _ in range(2)]
        probT = late.take(S, NH * S)
        late.again()
        xT_all = late.take(P, NT * D)
        xin = [late.take(P, D) for _ in range(2)]
        xT = late.take(P, D)
        sg = [late.take(P, M) for _ in range(2)]
        hb = late.take(P, M)
        hT = late.take(P, M)
        yb = [late.take(P, D) for _ in range(2)]
        late.again()
        gath = [[late.take(P, D) for _ in range(K)] for _ in range(3)]

        ps = ctx.enter_context(nc.psum_tensor("ps", [P, 8, 512], F32))

        s_c = sem("const_in")
        s_cb = sem("bf16_const_in")
        s_w1 = sem("patch_weights_in")
        s_w2 = sem("attn_weights_in")
        s_w3 = sem("ffn_weights_in")
        s_cls = sem("cls_in")
        s_clsadd = sem("cls_added")
        s_txt = sem("txt_in")
        s_const = sem("const_made")
        s_zero = sem("zero_made")
        s_rows0 = sem("rows_cleared")
        xp_in = sems("xp_in", 2)
        x_normed = sem("x_normed")
        patch_T = sem("patch_T")
        affine_done = sem("affine_done")
        patch_mm = sem("patch_mm")
        patch_read = sem("patch_read")
        patch_out = sem("patch_out")
        patch_stored = sems("patch_stored", 2)
        h_in = sem("h_in")
        n_ready = sem("n_ready")
        nT_psum = sem("nT_psum")
        nT_ready = sem("nT_ready")
        qk_done = sem("qk_done")
        rope_in = sem("rope_in")
        qk_ready = sem("qk_ready")
        scores_done = sem("scores_done")
        shifted = sem("shifted")
        exp_done = sem("exp_done")
        probT_psum = sem("probT_psum")
        probT_ready = sem("probT_ready")
        v_done = sem("v_done")
        v_ready = sem("v_ready")
        pv_done = sem("pv_done")
        o_normed = sem("o_normed")
        oT_psum = sem("oT_psum")
        oT_ready = sem("oT_ready")
        wo_done = sem("wo_done")
        resid_done = sem("resid_done")
        moved = sem("moved")
        deviated = sem("deviated")
        image_moved = sem("image_moved")
        h1_stored = sem("h1_stored")
        h1_in = sem("h1_in")
        m_ready = sem("m_ready")
        rT_psum = sem("rT_psum")
        rT_ready = sem("rT_ready")
        logits_done = sem("logits_done")
        chosen = sem("chosen")
        ranked = sem("ranked")
        picked = sem("picked")
        c_ready = sem("c_ready")
        slots_ready = sem("slots_ready")
        scattered = sem("scattered")
        x_in = sems("x_in", 2)
        xT_psum = sem("xT_psum")
        xT_ready = sem("xT_ready")
        g_done = sem("g_done")
        u_done = sem("u_done")
        silu_done = sem("silu_done")
        h_ready = sem("h_ready")
        hT_psum = sem("hT_psum")
        hT_ready = sem("hT_ready")
        d_done = sem("d_done")
        y_ready = sem("y_ready")
        y_stored = sems("y_stored", 2)
        ln1b_ready = sem("ln1b_ready")
        ln1b_done = sem("ln1b_done")
        gained = sem("gained")
        gathered = sems("gathered", 3)
        tile_out = sem("tile_out")
        out_stored = sem("out_stored")
        dve_step = sem("dve_step")
        pool_step = sem("pool_step")

        def bc(ap, shape):
            return ap.broadcast_to(shape)

        ps_s = ps[0:S, 0:4, 0:QC].rearrange("p b (h k) -> p b h k", k=S)
        ps_pt = [ps[:, 4 + i, 0:QC] for i in range(2)]
        ps_oT = ps[:, 5, QC:QC + DC * S]
        ps_q = ps[:, 6, 0:DC * 2 * S]
        ps_k = ps[:, 7, 0:DC * 2 * S]
        ps_o = ps[0:S, 7, 0:NH * (HD + 1)]
        ps_wo = ps[0:S, 6, 0:D]
        ps_v = ps[0:S, 6, 0:2 * D]
        v_v = v_sb[:, :].rearrange("p (b h d) -> p b h d", b=2, d=HD + 1)

        var_all = mv_all[:, :].rearrange("p (i k) -> p i k", k=2)[:, :, 1]
        GROUPS = ((0, 4), (4, B))

        block = ctx.enter_context(nc.Block())
        NSTEP1 = NPT // 2 - 1

        @block.sync
        def _(sp):
            def load_patch(i, par):
                sp.dma_start(xp[par][:, :], a["patches"][bass.ds(i * PT, PT), :]).then_inc(xp_in[par], 16)

            load_patch(0, 0)
            sp.dma_start(ln1gb[:, :], a["ln1gb"]).then_inc(s_w1, 16)
            sp.dma_start(ident[:, :], a["c_ident"]).then_inc(s_w1, 16)
            load_patch(1, 1)
            sp.dma_start(wpatch[:, :].rearrange("p (c n) -> p c n", c=PDC),
                         a["W"].rearrange("(c p) n -> p c n", p=P)).then_inc(s_w1, 16)
            for i, n in enumerate(("bias", "ln2_g", "ln2_b")):
                sp.dma_start(rowp[:, i * D:(i + 1) * D], a[n].partition_broadcast(PT)).then_inc(s_c, 16)
            sp.dma_start(pe[:, :], a["c_pe"]).then_inc(s_c, 16)

            def stage1(i, par):
                sp.wait_ge(x_normed, i + 1)
                load_patch(i + 2, par)
                sp.wait_ge(patch_out, i + 1)
                sp.dma_start(patches_d[bass.ds(i * PT, PT), :], yt[par][:, :]).then_inc(patch_stored[par], 16)

            with sp.Fori(0, NSTEP1) as r:
                for par in range(2):
                    stage1(r * 2 + par, par)
            for i in (NPT - 2, NPT - 1):
                sp.wait_ge(patch_out, i + 1)
                sp.dma_start(patches_d[i * PT:(i + 1) * PT, :], yt[i % 2][:, :]).then_inc(patch_stored[i % 2], 16)
            for par in range(2):
                sp.wait_ge(patch_stored[par], 16 * (NPT // 2))
            sp.dma_start(h_all[1:1 + NPATCH, :].rearrange("p (b d) -> p b d", b=B),
                         patches_d.rearrange("(b p) d -> p b d", b=B)).then_inc(h_in, 16)

            with sp.Fori(0, PAIRS) as p:
                for b in range(2):
                    n = p * 2 + b
                    sp.wait_ge(resid_done, n + 1)
                    sp.dma_start(h1_d[bass.ds(n * S, S), :], h_all[:, bass.ds(n * D, D)]).then_inc(h1_stored, 16)
            sp.wait_ge(h1_stored, 16 * B)
            sp.dma_start(acc[:, 0:(NT - 1) * D].rearrange("p (t d) -> p t d", t=NT - 1),
                         h1_d[0:(NT - 1) * P, :].rearrange("(t p) d -> p t d", p=P)).then_inc(h1_in, 16)
            sp.dma_start(acc[0:LAST, (NT - 1) * D:], h1_d[(NT - 1) * P:TOK, :]).then_inc(h1_in, 16)

            def load_x(j, par, first=False):
                if not first:
                    sp.wait_ge(xT_psum, j - 1)
                sp.dma_start(xin[par][:, :], rows_d[bass.ds(j * P, P), :]).then_inc(x_in[par], 16)

            def store_y(j, par):
                sp.wait_ge(y_ready, j + (NT + 1))
                sp.dma_start(y_d[bass.ds(j * P, P), :], yb[par][:, :]).then_inc(y_stored[par], 16)

            sp.wait_ge(scattered, 16 * K * NT)
            load_x(0, 0, True)
            load_x(1, 1, True)
            load_x(2, 0)
            rounds = (NB - 3) // 2
            with sp.Fori(0, rounds) as r:
                for o in range(2):
                    load_x(r * 2 + (3 + o), (3 + o) % 2)
                    store_y(r * 2 + o, o)
            for j in range(2 * rounds, NB):
                if j + 3 < NB:
                    load_x(j + 3, (j + 3) % 2)
                store_y(j, j % 2)

            for t in range(NT):
                rows = P if t < NT - 1 else LAST
                sp.wait_ge(tile_out, t + 1)
                sp.dma_start(out[t * P:t * P + rows, :], acc[0:rows, t * D:(t + 1) * D]).then_inc(out_stored, 16)
            sp.wait_ge(out_stored, 16 * NT)

        @block.gpsimd
        def _(pool):
            link = Chain(pool, pool_step)
            pool.dma_start(identb[:, :], a["c_ident"]).then_inc(s_cb, 16)
            pool.dma_start(causalb[:, :], a["c_causal"]).then_inc(s_cb, 16)
            pool.dma_start(beforeb[:, :], a["c_before"]).then_inc(s_cb, 16)
            nc.gpsimd.memset(onesb[:, :], 1.0).then_inc(s_const, 1)

            gu_v = wgu[:, :].rearrange("p (e c x m) -> p e c x m", e=E + 1, c=DC, x=2)
            dn_v = wdn[:, :].rearrange("p (e c n) -> p e c n", e=E + 1, c=MC)
            for e in (E, *range(E)):
                for x, (all_w, shared) in enumerate((("gate_w", "sgate_w"), ("up_w", "sup_w"))):
                    src = a[shared][0] if e == E else a[all_w][e]
                    pool.dma_start(gu_v[:, e, :, x, :], src.rearrange("(c p) m -> p c m", p=P)).then_inc(s_w3, 16)
                src = a["sdown_w"][0] if e == E else a["down_w"][e]
                pool.dma_start(dn_v[:, e, :, :], src.rearrange("(c p) n -> p c n", p=P)).then_inc(s_w3, 16)

            def rope_pool(p):
                pool.wait_ge(rope_in, p + 1)
                nc.gpsimd.tensor_tensor(qs[:, :], qs[:, :], rope[:, W2:2 * W2], ALU.mult)
                link(nc.gpsimd.tensor_tensor(ks[:, :], ks[:, :], rope[:, W2:2 * W2], ALU.mult))
                pool.wait_ge(scores_done, p * 2)
                nc.gpsimd.tensor_tensor(qr[:, :], qc[:, :], qs[:, :], ALU.add)
                link(nc.gpsimd.tensor_tensor(kr[:, :], kc[:, :], ks[:, :], ALU.add))
                for t in range(DC):
                    o = kbd[:, t * HPT * 2 * S:(t + 1) * HPT * 2 * S].rearrange("p (h k) -> p h k", h=HPT)
                    k_in = kr[:, t * 2 * S:(t + 1) * 2 * S].unsqueeze(1)
                    i = nc.gpsimd.tensor_tensor(o, bc(k_in, [P, HPT, 2 * S]),
                                                bc(heads[:, :].unsqueeze(2), [P, HPT, 2 * S]), ALU.mult)
                i.then_inc(qk_ready, 1)

            pool.wait_ge(h_in, 16)
            nc.gpsimd.memset(v_sb[:, :], 1.0).then_inc(s_const, 1)
            pool.wait_ge(s_w2, 16 * 9)
            rope_pool(0)
            with pool.Fori(1, PAIRS) as p:
                link.enter(p - 1, 2)
                rope_pool(p)
                link.leave(PAIRS - 1)

            pool.wait_ge(slots_ready, 2)
            pool.wait_ge(s_rows0, 16)
            for t in range(NT):
                rows = P if t < NT - 1 else LAST
                for k in range(K):
                    nc.gpsimd.indirect_dma_start(
                        out=rows_d, out_offset=bass.IndirectOffsetOnAxis(ap=slot[k][0:rows, t:t + 1], axis=0),
                        in_=m_all[0:rows, t * D:(t + 1) * D], in_offset=None).then_inc(scattered, 16)

            for par in range(2):
                pool.wait_ge(y_stored[par], 16 * ((NB + 1 - par) // 2))
            pool.wait_ge(xT_ready, NT)
            for t in range(NT):
                rows = P if t < NT - 1 else LAST
                if t >= 3:
                    pool.wait_ge(tile_out, t - 2)
                for k in range(K):
                    nc.gpsimd.indirect_dma_start(
                        out=gath[t % 3][k][0:rows, :], out_offset=None, in_=y_d,
                        in_offset=bass.IndirectOffsetOnAxis(ap=slot[k][0:rows, t:t + 1], axis=0)
                    ).then_inc(gathered[t % 3], 16)

        @block.scalar
        def _(act):
            act.dma_start(cls[0:1, 0:D], a["cls_token"]).then_inc(s_cls, 16)
            act.dma_start(cls[0:1, D:2 * D], a["cls_pos"]).then_inc(s_cls, 16)
            act.dma_start(h_all[1 + NPATCH:S, :].rearrange("p (b d) -> p b d", b=B),
                          a["txt"].rearrange("b p d -> p b d")).then_inc(s_txt, 16)
            act.dma_start(rope[:, :], a["c_rope"]).then_inc(s_w2, 16)
            act.dma_start(heads[:, :], a["c_heads"]).then_inc(s_w2, 16)
            for i, n in enumerate(("wqT", "wkT")):
                act.dma_start(wqk[:, :].rearrange("p (c x n) -> p c x n", c=DC, x=2)[:, :, i, :],
                              a[n].rearrange("(c p) n -> p c n", p=P)).then_inc(s_w2, 16)
            for w, n in ((wv, "wvT"), (wo, "woT"), (wgate, "gateT")):
                act.dma_start(w[:, :].rearrange("p (c n) -> p c n", c=DC),
                              a[n].rearrange("(c p) n -> p c n", p=P)).then_inc(s_w2, 16)
            act.dma_start(route[:, :], a["c_route"]).then_inc(s_w2, 16)
            act.dma_start(beta[:, :], a["beta"].partition_broadcast(P)).then_inc(s_w2, 16)
            act.wait_ge(s_zero, 1)
            act.dma_start(rows_d.rearrange("(j p) d -> p j d", p=P),
                          bc(zero[:, :].unsqueeze(1), [P, NB, D])).then_inc(s_rows0, 16)

            def deviation(count):
                act.wait_ge(moved, count)
                nc.scalar.activation(dev[0:PT, :], mv[0:PT, :].rearrange("p (i k) -> p i k", k=2)[:, :, 1], ACT.Sqrt,
                                     bias=eps[0:PT, :]).then_inc(deviated, 1)

            def xnT_copy(i, par, first=False):
                act.wait_ge(patch_T, i + 1)
                if not first:
                    act.wait_ge(patch_mm, i - 1)
                nc.scalar.activation(xnT[par].rearrange("p (b n) -> p b n", b=2), ps[:, 0:2, 0:3 * PT],
                                     ACT.Copy).then_inc(affine_done, 1)

            deviation(1)
            xnT_copy(0, 0, True)
            xnT_copy(1, 1, True)
            act.wait_ge(s_clsadd, 1)
            act.dma_start(h_all[0:1, :].rearrange("p (b d) -> p b d", b=B),
                          bc(cls[0:1, 0:D].unsqueeze(1), [1, B, D])).then_inc(s_txt, 16)
            with act.Fori(0, NPT // 2 - 1) as r:
                for par in range(2):
                    deviation(r * 2 + (par + 2))
                    xnT_copy(r * 2 + (par + 2), par)
            for i in (NPT - 2, NPT - 1):
                deviation(i + 2)
            for g, (b0, b1) in enumerate(GROUPS):
                act.wait_ge(image_moved, g + 1)
                nc.scalar.activation(dev_all[0:S, b0:b1], var_all[0:S, b0:b1], ACT.Sqrt,
                                     bias=eps[0:S, :]).then_inc(deviated, 1)

            def nT_copy(p):
                act.wait_ge(nT_psum, p + 1)
                nc.scalar.activation(nT[:, :], ps_q, ACT.Copy).then_inc(nT_ready, 1)

            def v_copy(p):
                act.wait_ge(v_done, p + 1)
                for b in range(2):
                    ins = nc.scalar.activation(v_v[:, b, :, 0:HD],
                                               ps_v[:, b * D:(b + 1) * D].rearrange("p (h d) -> p h d", h=NH), ACT.Copy)
                ins.then_inc(v_ready, 1)

            def expo(n, b):
                act.wait_ge(shifted, n + 1)
                nc.scalar.activation(prob[b][:, :], prob[b][:, :], ACT.Exp, scale=HD ** -0.5).then_inc(exp_done, 1)

            def probT_copy(n, k, first):
                act.wait_ge(probT_psum, n * 4 + (k + 1))
                if not first:
                    act.wait_ge(pv_done, n * 4 + k - 3)
                nc.scalar.activation(probT[:, k * QC:(k + 1) * QC], ps_pt[k % 2][0:S, :], ACT.Copy).then_inc(probT_ready, 1)

            def oT_copy(n):
                act.wait_ge(oT_psum, n + 1)
                nc.scalar.activation(oT[:, :], ps_oT, ACT.Copy).then_inc(oT_ready, 1)

            def attn(p, following, first=False):
                if following:
                    nT_copy(p + 1)
                for b in range(2):
                    n = p * 2 + b
                    expo(n, b)
                    for k in range(4):
                        probT_copy(n, k, first and b == 0)
                oT_copy(p * 2)
                if following:
                    v_copy(p + 1)
                oT_copy(p * 2 + 1)

            act.wait_ge(s_const, 2)
            nT_copy(0)
            v_copy(0)
            attn(0, True, True)
            with act.Fori(1, PAIRS - 1) as p:
                attn(p, True)
            attn(PAIRS - 1, False)

            act.wait_ge(moved, NPT + 2)
            nc.scalar.activation(dev_all[:, 0:NT], var_all[:, 0:NT], ACT.Sqrt, bias=eps[:, :]).then_inc(deviated, 1)
            for t in range(NT):
                act.wait_ge(rT_psum, t + 1)
                nc.scalar.activation(xT_all[:, t * D:(t + 1) * D], ps[:, t % 2, 0:D], ACT.Copy).then_inc(rT_ready, 1)
            act.wait_ge(picked, 1)
            nc.scalar.activation(csel[:, :], rsm[:, 4 * NT:6 * NT], ACT.Sigmoid).then_inc(c_ready, 1)

            def xT_copy(j, shared):
                act.wait_ge(u_done, j)
                if shared:
                    nc.scalar.activation(xT[:, :], xT_all[:, bass.ds(j * D, D)], ACT.Copy).then_inc(xT_ready, 1)
                else:
                    act.wait_ge(xT_psum, j - (NT - 1))
                    nc.scalar.activation(xT[:, :], ps[:, 4, 0:D], ACT.Copy).then_inc(xT_ready, 1)

            def silu(j, par, first):
                act.wait_ge(g_done, j + 1)
                if not first:
                    act.wait_ge(h_ready, j - 1)
                nc.scalar.activation(sg[par][:, :], ps[:, 2 * par, :], ACT.Silu).then_inc(silu_done, 1)

            def y_copy(j, par, first):
                act.wait_ge(d_done, j + 1)
                if not first:
                    act.wait_ge(y_stored[par], (j - (NT + par)) * 8)
                nc.scalar.activation(yb[par][:, :], ps[:, 6, 0:D], ACT.Copy).then_inc(y_ready, 1)

            def run(first, n):
                shared = first == 0

                def step(j, k, t=True, g=True, d=True):
                    if g:
                        silu(j, (first + k) % 2, shared and k < 2)
                    if t:
                        xT_copy(j + 1, shared)
                    if d and not shared:
                        y_copy(j - 2, k % 2, k < 4)

                xT_copy(first, shared)
                for k in range(4):
                    step(first + k, k, d=k >= 2)
                rounds = (n - 5) // 2
                with act.Fori(0, rounds) as r:
                    for o in range(2):
                        step(r * 2 + (first + 4 + o), 4 + o)
                for k in range(4 + 2 * rounds, n + 2):
                    step(first + k, k, t=k + 1 < n, g=k < n)

            run(0, NT)
            run(NT, NB)

        @block.tensor
        def _(pe_):
            def patch_transpose(i, par, first=False):
                pe_.wait_ge(x_normed, i + 1)
                if not first:
                    pe_.wait_ge(affine_done, i)
                for c in range(PDC):
                    ins = nc.tensor.transpose(ps[:, c // 3, (c % 3) * PT:(c % 3 + 1) * PT],
                                              xn[par][:, c * P:(c + 1) * P], ident[0:PT, 0:PT])
                ins.then_inc(patch_T, 1)

            def patch_product(i, par, first=False):
                pe_.wait_ge(affine_done, i + 1)
                if not first:
                    pe_.wait_ge(patch_read, i)
                for c in range(PDC):
                    ins = nc.tensor.matmul(ps[0:PT, 2, 0:D], xnT[par][:, c * PT:(c + 1) * PT],
                                           wpatch[:, c * D:(c + 1) * D], start=(c == 0), stop=(c == PDC - 1))
                ins.then_inc(patch_mm, 1)

            pe_.wait_ge(s_w1, 16 * 3)
            pe_.wait_ge(ln1b_ready, 1)
            for c in range(PDC):
                ins = nc.tensor.matmul(ps[0:PT, 3, 0:D], ln1b[:, c * PT:(c + 1) * PT], wpatch[:, c * D:(c + 1) * D],
                                       start=(c == 0), stop=(c == PDC - 1))
            ins.then_inc(ln1b_done, 1)
            patch_transpose(0, 0, True)
            patch_transpose(1, 1)
            pe_.wait_ge(gained, 1)
            patch_product(0, 0, True)
            with pe_.Fori(0, NPT // 2 - 1) as r:
                patch_product(r * 2 + 1, 1)
                patch_transpose(r * 2 + 2, 0)
                patch_product(r * 2 + 2, 0)
                patch_transpose(r * 2 + 3, 1)
            patch_product(NPT - 1, 1)

            def nT_of(p, free=None, following=True):
                pe_.wait_ge(n_ready, p * 2 + 2)
                if free is not None:
                    pe_.wait_ge(resid_done, free)
                if following:
                    pe_.wait_ge(v_ready, p)
                for b in range(2):
                    for c in range(DC):
                        ins = nc.tensor.transpose(ps_q[:, (c * 2 + b) * S:(c * 2 + b + 1) * S],
                                                  n_t[:, b * D + c * P:b * D + (c + 1) * P], ident[0:S, 0:S])
                ins.then_inc(nT_psum, 1)

            def qk_of(p, free=None):
                pe_.wait_ge(nT_ready, p + 1)
                if free is not None:
                    pe_.wait_ge(o_normed, free)
                for x, dst in enumerate((ps_q, ps_k)):
                    for t in range(DC):
                        for c in range(DC):
                            ins = nc.tensor.matmul(dst[:, t * 2 * S:(t + 1) * 2 * S],
                                                   wqk[:, c * 2 * D + x * D + t * P:c * 2 * D + x * D + (t + 1) * P],
                                                   nT[:, c * 2 * S:(c + 1) * 2 * S], start=(c == 0), stop=(c == DC - 1))
                ins.then_inc(qk_done, 1)

            def v_of(p, free=None):
                pe_.wait_ge(rope_in, p + 1)
                if free is not None:
                    pe_.wait_ge(resid_done, free)
                for b in range(2):
                    for c in range(DC):
                        ins = nc.tensor.matmul(ps_v[:, b * D:(b + 1) * D], nT[:, (c * 2 + b) * S:(c * 2 + b + 1) * S],
                                               wv[:, c * D:(c + 1) * D], start=(c == 0), stop=(c == DC - 1))
                ins.then_inc(v_done, 1)

            def scores(p, b, first=False):
                n = p * 2 + b
                pe_.wait_ge(qk_ready, p + 1)
                if not first:
                    pe_.wait_ge(shifted, n)
                kv = kbd[:, :].rearrange("p (g h b k) -> p g h b k", g=4, h=QH, b=2)
                for g in range(4):
                    t = g // 2
                    nc.tensor.matmul(ps_s[:, g, :, :], qr[:, (t * 2 + b) * S:(t * 2 + b + 1) * S],
                                     kv[:, g, :, b, :], start=True, stop=False)
                    ins = nc.tensor.matmul(ps_s[:, g, :, :], identb[0:S, 0:S],
                                           bc(causalb[:, :].unsqueeze(1), [S, QH, S]), start=False, stop=True)
                ins.then_inc(scores_done, 1)

            def probT_of(n, b, k, first):
                if k == 0:
                    pe_.wait_ge(exp_done, n + 1)
                if not first:
                    pe_.wait_ge(probT_ready, n * 4 + k - 1)
                for h in range(QH):
                    ins = nc.tensor.transpose(ps_pt[k % 2][0:S, h * S:(h + 1) * S],
                                              prob[b][:, (k * QH + h) * S:(k * QH + h + 1) * S], ident[0:S, 0:S])
                ins.then_inc(probT_psum, 1)

            def pv_of(n, b, k):
                pe_.wait_ge(probT_ready, n * 4 + k + 1)
                for h in range(k * QH, (k + 1) * QH):
                    ins = nc.tensor.matmul(ps_o[:, h * (HD + 1):(h + 1) * (HD + 1)], probT[:, h * S:(h + 1) * S],
                                           v_v[:, b, h, :], start=True, stop=True)
                ins.then_inc(pv_done, 1)

            def context(p, b, rope_n, first):
                n = p * 2 + b
                probT_of(n, b, 0, first)
                probT_of(n, b, 1, first)
                pe_.wait_ge(v_ready, p + 1)
                if rope_n is not None:
                    pe_.wait_ge(rope_in, rope_n)
                if not first:
                    pe_.wait_ge(o_normed, n)
                pv_of(n, b, 0)
                probT_of(n, b, 2, False)
                pv_of(n, b, 1)
                probT_of(n, b, 3, False)
                pv_of(n, b, 2)
                pv_of(n, b, 3)

            def oT_of(n, first=False):
                pe_.wait_ge(o_normed, n + 1)
                if not first:
                    pe_.wait_ge(oT_ready, n)
                for c in range(DC):
                    ins = nc.tensor.transpose(ps_oT[:, c * S:(c + 1) * S], on[:, c * P:(c + 1) * P], ident[0:S, 0:S])
                ins.then_inc(oT_psum, 1)

            def wo_of(n):
                pe_.wait_ge(oT_ready, n + 1)
                for c in range(DC):
                    ins = nc.tensor.matmul(ps_wo, oT[:, c * S:(c + 1) * S], wo[:, c * D:(c + 1) * D],
                                           start=(c == 0), stop=(c == DC - 1))
                ins.then_inc(wo_done, 1)

            def attn(p, following, first=False):
                scores(p, 0, first)
                if following:
                    nT_of(p + 1, None if first else p * 2)
                scores(p, 1)
                if following:
                    qk_of(p + 1, None if first else p * 2)
                context(p, 0, p + 2 if following else None, first)
                context(p, 1, None, False)
                oT_of(p * 2, first)
                wo_of(p * 2)
                if following:
                    v_of(p + 1, p * 2 + 1)
                oT_of(p * 2 + 1)
                if following:
                    pe_.wait_ge(v_ready, p + 2)
                else:
                    pe_.wait_ge(resid_done, p * 2 + 1)
                wo_of(p * 2 + 1)

            pe_.wait_ge(s_w2, 16 * 9)
            pe_.wait_ge(s_cb, 16 * 3)
            pe_.wait_ge(patch_read, NPT)
            nT_of(0, following=False)
            qk_of(0)
            v_of(0)
            attn(0, True, True)
            with pe_.Fori(1, PAIRS - 1) as p:
                attn(p, True)
            attn(PAIRS - 1, False)

            pe_.wait_ge(resid_done, B)
            pe_.wait_ge(s_const, 2)
            ps_lg = ps[:, 7, 0:NT * E]

            def logits(t):
                pe_.wait_ge(rT_ready, t + 1)
                for c in range(DC):
                    ins = nc.tensor.matmul(ps_lg[:, t * E:(t + 1) * E], xT_all[:, t * D + c * P:t * D + (c + 1) * P],
                                           wgate[:, c * E:(c + 1) * E], start=(c == 0), stop=(c == DC - 1))
                ins.then_inc(logits_done, 1)

            for t in range(NT):
                pe_.wait_ge(m_ready, t + 1)
                if t >= 2:
                    pe_.wait_ge(rT_ready, t - 1)
                for c in range(DC):
                    ins = nc.tensor.transpose(ps[:, t % 2, c * P:(c + 1) * P],
                                              m_all[:, t * D + c * P:t * D + (c + 1) * P], ident[:, :])
                ins.then_inc(rT_psum, 1)
                if t >= 1:
                    logits(t - 1)
            logits(NT - 1)
            pe_.wait_ge(chosen, 1)
            ps_rank = ps[:, 7, 128:128 + NT * E]
            nc.tensor.matmul(ps_rank, beforeb[:, :], m12[:, :], start=True, stop=False)
            for s in range(1, NT):
                ins = nc.tensor.matmul(ps_rank, onesb[:, :], m12z[:, TE - (s + 1) * E:2 * TE - (s + 1) * E],
                                       start=False, stop=(s == NT - 1))
            for t in range(NT):
                ins = nc.tensor.matmul(ps[:, 7, 256:256 + E], onesb[:, :], m12[:, t * E:(t + 1) * E],
                                       start=(t == 0), stop=(t == NT - 1))
            ins.then_inc(ranked, 1)

            def x_transpose(j, par, n_in):
                pe_.wait_ge(x_in[par], n_in)
                pe_.wait_ge(xT_ready, j)
                for c in range(DC):
                    ins = nc.tensor.transpose(ps[:, 4, c * P:(c + 1) * P], xin[par][:, c * P:(c + 1) * P], ident[:, :])
                ins.then_inc(xT_psum, 1)

            def gate_up(j, par, e, first):
                pe_.wait_ge(xT_ready, j + 1)
                if not first:
                    pe_.wait_ge(h_ready, j - 1)
                for x, done in enumerate((g_done, u_done)):
                    for c in range(DC):
                        at = (c * 2 + x) * M
                        ins = nc.tensor.matmul(ps[:, 2 * par + x, :], xT[:, c * P:(c + 1) * P],
                                               wgu[:, bass.ds(e * (DC * 2 * M) + at, M)],
                                               start=(c == 0), stop=(c == DC - 1))
                    ins.then_inc(done, 1)

            def h_transpose(j):
                pe_.wait_ge(h_ready, j + 1)
                pe_.wait_ge(hT_ready, j)
                for c in range(MC):
                    ins = nc.tensor.transpose(ps[:, 5, c * P:(c + 1) * P], hb[:, c * P:(c + 1) * P], ident[:, :])
                ins.then_inc(hT_psum, 1)

            def down(j, e):
                pe_.wait_ge(hT_ready, j + 1)
                pe_.wait_ge(y_ready, j)
                for c in range(MC):
                    ins = nc.tensor.matmul(ps[:, 6, 0:D], hT[:, c * P:(c + 1) * P],
                                           wdn[:, bass.ds(e * (MC * D) + c * D, D)],
                                           start=(c == 0), stop=(c == MC - 1))
                ins.then_inc(d_done, 1)

            def expert_of(j, first):
                if first == 0:
                    return E
                return pe_.value_load(eid[0:1, bass.ds(j - NT, 1)], min_val=0, max_val=E - 1)

            def run(first, n):
                def x_T(j, k):
                    if first:
                        x_transpose(j, k % 2, (j - (first + k % 2)) * 8 + 16)

                def full(j, k, t=True, g=True, h=True, d=True):
                    if t:
                        x_T(j + 1, k + 1)
                    if g:
                        gate_up(j, (first + k) % 2, expert_of(j, first), first == 0 and k < 2)
                    if h:
                        h_transpose(j - 1)
                    if d:
                        down(j - 2, expert_of(j - 2, first))

                x_T(first, 0)
                full(first, 0, h=False, d=False)
                full(first + 1, 1, d=False)
                rounds = (n - 3) // 2
                with pe_.Fori(0, rounds) as r:
                    for o in range(2):
                        full(r * 2 + (first + 2 + o), 2 + o)
                for k in range(2 + 2 * rounds, n + 2):
                    full(first + k, k, t=k + 1 < n, g=k < n, h=k - 1 < n)

            pe_.wait_ge(s_w3, 16 * 3 * (E + 1))
            run(0, NT)
            pe_.wait_ge(slots_ready, 2)
            run(NT, NB)

        @block.vector
        def _(dve):
            link = Chain(dve, dve_step)

            def moments(src, rows, width, st, out_mv):
                half = width // 512 + 1
                w = width // half
                for i in range(half):
                    ins = nc.vector.bn_stats(st[0:rows, 6 * i:6 * i + 6], src[:, i * w:(i + 1) * w])
                link(ins)
                return nc.vector.bn_aggr(out_mv, st[0:rows, 0:6 * half])

            def normed(dst, src, mean, inv):
                return nc.vector.tensor_scalar(dst, src, mean, inv, ALU.subtract, ALU.mult)

            nc.vector.memset(eps[:, :], EPS)
            nc.vector.memset(m12z[:, 0:TE - E], 0.0)
            link(nc.vector.memset(mv_all[:, :], 1.0))
            nc.vector.memset(zero[:, :], 0.0).then_inc(s_zero, 1)
            dve.wait_ge(s_w1, 16 * 3)
            nc.vector.tensor_copy(ln1b.rearrange("p (c n) -> p c n", c=PDC),
                                  bc(ln1gb[:, PDC:].unsqueeze(2), [P, PDC, PT])).then_inc(ln1b_ready, 1)
            for par in range(2):
                dve.wait_ge(xp_in[par], 16)
                ins = moments(xp[par], PT, PD, stats, mv[0:PT, 2 * par:2 * par + 2])
                if par == 0:
                    link(ins)
            ins.then_inc(moved, 1)
            dve.wait_ge(ln1b_done, 1)
            wp_v = wpatch.rearrange("p (c n) -> p c n", c=PDC)
            nc.vector.tensor_tensor(wp_v, wp_v, bc(ln1gb[:, 0:PDC].unsqueeze(2), [P, PDC, D]),
                                    ALU.mult).then_inc(gained, 1)
            dve.wait_ge(deviated, 1)
            link(nc.vector.reciprocal(rstd[0:PT, :], dev[0:PT, :]))
            for par in range(2):
                normed(xn[par], xp[par], mv[0:PT, 2 * par:2 * par + 1], rstd[0:PT, par:par + 1]).then_inc(x_normed, 1)
            dve.wait_ge(s_c, 16 * 4)
            link(nc.vector.tensor_tensor(rowp[:, 0:D], rowp[:, 0:D], ps[0:PT, 3, 0:D], ALU.add))
            link(nc.vector.tensor_tensor(pe.rearrange("p (t d) -> p t d", t=NPT),
                                         pe.rearrange("p (t d) -> p t d", t=NPT),
                                         bc(rowp[:, 2 * D:3 * D].unsqueeze(1), [PT, NPT, D]), ALU.add))
            dve.wait_ge(s_cls, 32)
            nc.vector.tensor_tensor(cls[0:1, 0:D], cls[0:1, 0:D], cls[0:1, D:2 * D], ALU.add).then_inc(s_clsadd, 1)

            def patch_step(i, par, n_in, following=True, first=False):
                y = yt[par]
                if following:
                    dve.wait_ge(xp_in[par], n_in)
                    link(moments(xp[par], PT, PD, stats, mv[0:PT, 2:4]))
                dve.wait_ge(patch_mm, i + 1)
                if not first:
                    dve.wait_ge(patch_stored[par], (i - par) * 8)
                nc.vector.tensor_tensor(y, ps[0:PT, 2, 0:D], rowp[:, 0:D], ALU.add).then_inc(patch_read, 1)
                dve.wait_ge(patch_read, i + 1)
                moments(y, PT, D, stats, mv[0:PT, 0:2]).then_inc(moved, 1)
                dve.wait_ge(deviated, i + 2)
                link(nc.vector.reciprocal(rstd[0:PT, :], dev[0:PT, :]))
                if following:
                    normed(xn[par], xp[par], mv[0:PT, 2:3], rstd[0:PT, 1:2]).then_inc(x_normed, 1)
                link(normed(y, y, mv[0:PT, 0:1], rstd[0:PT, 0:1]))
                link(nc.vector.tensor_tensor(y, y, rowp[:, D:2 * D], ALU.mult))
                nc.vector.tensor_tensor(y, y, pe[:, bass.ds(i * D, D)], ALU.add).then_inc(patch_out, 1)

            patch_step(0, 0, 32, True, True)
            patch_step(1, 1, 32, True, True)
            with dve.Fori(1, NPT // 2 - 1) as r:
                link.enter(r - 1, 12)
                for par in range(2):
                    patch_step(r * 2 + par, par, r * 16 + 32)
                link.leave(NPT // 2 - 2)
            for i in (NPT - 2, NPT - 1):
                patch_step(i, i % 2, 0, False)

            def image_moments(g):
                b0, b1 = GROUPS[g]
                for b in range(b0, b1):
                    ins = nc.vector.bn_stats(stats_all[0:S, 6 * b:6 * b + 6], h_all[:, b * D:(b + 1) * D])
                link(ins)
                for b in range(b0, b1):
                    ins = nc.vector.bn_aggr(mv_all[0:S, 2 * b:2 * b + 2], stats_all[0:S, 6 * b:6 * b + 6])
                ins.then_inc(image_moved, 1)

            def image_rstd(g):
                b0, b1 = GROUPS[g]
                dve.wait_ge(deviated, NPT + 2 + g)
                link(nc.vector.reciprocal(rstd_all[0:S, b0:b1], dev_all[0:S, b0:b1]))

            def ln_pair(p, first=False):
                if not first:
                    dve.wait_ge(nT_psum, p)
                for b in range(2):
                    n = p * 2 + b
                    normed(n_t[:, b * D:(b + 1) * D], h_all[:, bass.ds(n * D, D)], mv_all[0:S, bass.ds(n * 2, 1)],
                           rstd_all[0:S, bass.ds(n, 1)]).then_inc(n_ready, 1)

            swap = [i ^ 1 for i in range(32)]

            def rope_dve(p, first=False):
                dve.wait_ge(qk_done, p + 1)
                if not first:
                    dve.wait_ge(qk_ready, p)
                nc.vector.tensor_tensor(qc[:, :], ps_q, rope[:, 0:W2], ALU.mult)
                nc.vector.stream_shuffle(qs[:, :], ps_q, swap)
                nc.vector.tensor_tensor(kc[:, :], ps_k, rope[:, 0:W2], ALU.mult)
                nc.vector.stream_shuffle(ks[:, :], ps_k, swap).then_inc(rope_in, 1)

            def shift(n, b, first=False):
                dve.wait_ge(scores_done, n + 1)
                mx_v = mx[:, :].rearrange("p (g h) -> p g h", g=4)
                link(nc.vector.tensor_reduce(mx_v, ps_s, AX_X, ALU.max))
                if not first:
                    dve.wait_ge(probT_psum, n * 4 - 4)
                nc.vector.tensor_tensor(prob[b][:, :].rearrange("p (g h k) -> p g h k", g=4, h=QH), ps_s,
                                        bc(mx_v.unsqueeze(3), [S, 4, QH, S]), ALU.subtract).then_inc(shifted, 1)

            def norm_o(n, first=False):
                dve.wait_ge(pv_done, n * 4 + 4)
                o_v = ps_o.rearrange("p (h d) -> p h d", h=NH)
                link(nc.vector.reciprocal(rs[:, :], o_v[:, :, HD]))
                if not first:
                    dve.wait_ge(oT_psum, n)
                nc.vector.tensor_tensor(on[:, :].rearrange("p (h d) -> p h d", h=NH), o_v[:, :, 0:HD],
                                        bc(rs[:, :].unsqueeze(2), [S, NH, HD]), ALU.mult).then_inc(o_normed, 1)

            def resid(n, b, first=False):
                dve.wait_ge(wo_done, n + 1)
                h = h_all[:, bass.ds(n * D, D)]
                nc.vector.tensor_tensor(h, ps_wo, h, ALU.add).then_inc(resid_done, 1)

            def attn(p, following, first=False):
                if following:
                    ln_pair(p + 1)
                for b in range(2):
                    shift(p * 2 + b, b, first)
                if following:
                    rope_dve(p + 1)
                for b in range(2):
                    norm_o(p * 2 + b, first and b == 0)
                for b in range(2):
                    resid(p * 2 + b, b, first)

            dve.wait_ge(h_in, 16)
            dve.wait_ge(s_txt, 32)
            dve.wait_ge(s_w2, 16 * 9)
            image_moments(0)
            image_rstd(0)
            ln_pair(0, True)
            image_moments(1)
            image_rstd(1)
            rope_dve(0, True)
            attn(0, True, True)
            with dve.Fori(1, PAIRS - 1) as p:
                link.enter(p - 1, 4)
                attn(p, True)
                link.leave(PAIRS - 2)
            attn(PAIRS - 1, False)

            dve.wait_ge(h1_in, 32)
            for t in range(NT):
                rows = P if t < NT - 1 else LAST
                ins = nc.vector.bn_stats(stats_all[0:rows, 6 * t:6 * t + 6], acc[0:rows, t * D:(t + 1) * D])
            link(ins)
            for t in range(NT):
                rows = P if t < NT - 1 else LAST
                ins = nc.vector.bn_aggr(mv_all[0:rows, 2 * t:2 * t + 2], stats_all[0:rows, 6 * t:6 * t + 6])
            ins.then_inc(moved, 1)
            dve.wait_ge(deviated, NPT + 2 + len(GROUPS))
            link(nc.vector.reciprocal(rstd_all[:, 0:NT], dev_all[:, 0:NT]))
            link(nc.vector.memset(m_all[64:P, (NT - 1) * D:], 0.0))
            for t in range(NT):
                rows = P if t < NT - 1 else LAST
                at = slice(t * D, (t + 1) * D)
                normed(m_all[0:rows, at], acc[0:rows, at], mv_all[0:rows, 2 * t:2 * t + 1],
                       rstd_all[0:rows, t:t + 1]).then_inc(m_ready, 1)
            r_first, r_steps = route[:, 0:TE], route[:, TE:2 * TE]
            r_lower, r_blocks = route[:, 2 * TE:2 * TE + E * E], route[:, 2 * TE + E * E:NR]
            r_valid = route[:, NR:NR + TE]

            def te(ap):
                return ap.rearrange("p (t e) -> p t e", e=E)

            biased, eq, wt, one, two, tmp = (rt[:, i * TE:(i + 1) * TE] for i in range(6))
            top = rsm[:, 0:NT]
            dve.wait_ge(logits_done, NT)
            link(nc.vector.tensor_copy(lg[:, :], ps[:, 7, 0:TE]))
            link(nc.vector.tensor_tensor(te(biased), te(lg[:, :]), bc(beta[:, :].unsqueeze(1), [P, NT, E]), ALU.add))
            for sel in (one, two):
                link(nc.vector.tensor_reduce(top, te(biased), AX_X, ALU.max))
                link(nc.vector.tensor_tensor(te(eq), te(biased), bc(top.unsqueeze(2), [P, NT, E]), ALU.is_equal))
                link(nc.vector.tensor_tensor(wt, eq, r_first, ALU.mult))
                link(nc.vector.tensor_reduce(top, te(wt), AX_X, ALU.max))
                link(nc.vector.tensor_tensor(te(sel), te(r_first), bc(top.unsqueeze(2), [P, NT, E]), ALU.is_equal))
                link(nc.vector.scalar_tensor_tensor(out=biased, in0=sel, scalar=-3.0e38, in1=biased,
                                                    op0=ALU.mult, op1=ALU.add))
            link(nc.vector.tensor_tensor(tmp, one, two, ALU.add))
            nc.vector.tensor_tensor(m12[:, :], tmp, r_valid, ALU.mult).then_inc(chosen, 1)
            dve.wait_ge(chosen, 1)
            for i, sel in enumerate((one, two)):
                link(nc.vector.tensor_tensor(tmp, sel, lg[:, :], ALU.mult))
                ins = nc.vector.tensor_reduce(rsm[:, (4 + i) * NT:(5 + i) * NT], te(tmp), AX_X, ALU.add)
                if i == 0:
                    link(ins)
            ins.then_inc(picked, 1)
            dve.wait_ge(picked, 1)
            dve.wait_ge(ranked, 1)
            cnt, nblk, base, upto = (nb[:, i * E:(i + 1) * E] for i in range(4))
            link(nc.vector.tensor_copy(cnt, ps[:, 7, 256:256 + E]))
            en = wide[:, 0:TE].rearrange("p (e s) -> p e s", e=E)
            link(nc.vector.tensor_tensor(en, bc(cnt.unsqueeze(2), [P, E, NT]),
                                         r_steps.rearrange("p (e s) -> p e s", e=E), ALU.is_gt))
            link(nc.vector.tensor_reduce(nblk, en, AX_X, ALU.add))
            ee = wide[:, 0:E * E].rearrange("p (e s) -> p e s", e=E)
            link(nc.vector.tensor_tensor(ee, bc(nblk.unsqueeze(1), [P, E, E]),
                                         r_lower.rearrange("p (e s) -> p e s", e=E), ALU.mult))
            link(nc.vector.tensor_reduce(base, ee, AX_X, ALU.add))
            link(nc.vector.tensor_tensor(upto, base, nblk, ALU.add))
            be = wide[:, :].rearrange("p (j e) -> p j e", e=E)
            link(nc.vector.tensor_tensor(be, r_blocks.rearrange("p (j e) -> p j e", e=E),
                                         bc(upto.unsqueeze(1), [P, NB, E]), ALU.is_ge))
            link(nc.vector.tensor_reduce(eidf[:, :], be, AX_X, ALU.add))
            nc.vector.tensor_scalar(eid[:, :], eidf[:, :], float(E - 1), None, ALU.min).then_inc(slots_ready, 1)
            link(nc.vector.tensor_scalar(upto, base, float(P), None, ALU.mult))
            link(nc.vector.tensor_tensor(te(wt), te(ps[:, 7, 128:128 + TE]), bc(upto.unsqueeze(1), [P, NT, E]), ALU.add))
            for i, sel in enumerate((one, two)):
                link(nc.vector.tensor_tensor(tmp, sel, wt, ALU.mult))
                link(nc.vector.tensor_reduce(rsm[:, (2 + i) * NT:(3 + i) * NT], te(tmp), AX_X, ALU.add))
            nc.vector.tensor_copy(slot[0][:, :], rsm[:, 2 * NT:3 * NT])
            nc.vector.tensor_copy(slot[1][:, :], rsm[:, 3 * NT:4 * NT]).then_inc(slots_ready, 1)

            def h_mult(j, par):
                dve.wait_ge(silu_done, j + 1)
                dve.wait_ge(u_done, j + 1)
                dve.wait_ge(hT_psum, j)
                nc.vector.tensor_tensor(hb[:, :], sg[par][:, :], ps[:, 2 * par + 1, :], ALU.mult).then_inc(h_ready, 1)

            def hT_copy(j):
                dve.wait_ge(hT_psum, j + 1)
                dve.wait_ge(d_done, j)
                nc.vector.tensor_copy(hT[:, :], ps[:, 5, :]).then_inc(hT_ready, 1)

            def shared_y(j):
                dve.wait_ge(d_done, j + 1)
                rows = LAST if isinstance(j, int) and j == NT - 1 else P
                at = acc[0:rows, bass.ds(j * D, D)]
                nc.vector.tensor_tensor(at, ps[0:rows, 6, 0:D], at, ALU.add).then_inc(y_ready, 1)

            def run(first, n):
                shared = first == 0

                def step(j, k, g=True, h=True, d=True):
                    if g:
                        h_mult(j, (first + k) % 2)
                    if h:
                        hT_copy(j - 1)
                    if d and shared:
                        shared_y(j - 2)

                step(first, 0, h=False, d=False)
                step(first + 1, 1, d=False)
                rounds = (n - 2) // 2
                with dve.Fori(0, rounds) as r:
                    for o in range(2):
                        step(r * 2 + (first + 2 + o), 2 + o)
                for k in range(2 + 2 * rounds, n + 2):
                    step(first + k, k, g=k < n, h=k - 1 < n)

            run(0, NT)
            run(NT, NB)

            for t in range(NT):
                rows = P if t < NT - 1 else LAST
                at = slice(t * D, (t + 1) * D)
                dve.wait_ge(gathered[t % 3], 32 * (t // 3 + 1))
                g = gath[t % 3]
                link(nc.vector.scalar_tensor_tensor(out=acc[0:rows, at], in0=g[0][0:rows, :], scalar=csel[0:rows, t:t + 1],
                                                    in1=acc[0:rows, at], op0=ALU.mult, op1=ALU.add))
                nc.vector.scalar_tensor_tensor(out=acc[0:rows, at], in0=g[1][0:rows, :],
                                               scalar=csel[0:rows, NT + t:NT + t + 1],
                                               in1=acc[0:rows, at], op0=ALU.mult, op1=ALU.add).then_inc(tile_out, 1)


def kernel(**inputs):
    import concourse.bacc as bacc
    from concourse.bass_utils import run_bass_kernel_spmd

    x = np.asarray(inputs["x"])
    patches = x.reshape(B, C, HP, PS, HP, PS).transpose(0, 2, 4, 3, 5, 1).reshape(B * NPATCH, PD)
    cols = [np.asarray(inputs[n]).reshape(PDC, P).T for n in ("L0_tok_ln1_g", "L0_tok_ln1_b")]
    arrays = {
        "patches": patches, "ln1gb": np.concatenate(cols, axis=1), "txt": inputs["txt"],
        "cls_token": np.asarray(inputs["L0_tok_cls_token"]).reshape(1, D),
        "cls_pos": np.asarray(inputs["L0_tok_cls_pos_embedding"]).reshape(1, D),
        "W": inputs["L0_tok_W"],
        "bias": np.asarray(inputs["L0_tok_bias"]).reshape(1, D),
        "ln2_g": np.asarray(inputs["L0_tok_ln2_g"]).reshape(1, D),
        "ln2_b": np.asarray(inputs["L0_tok_ln2_b"]).reshape(1, D),
        "wqT": np.asarray(inputs["L0_attn_wq"]).T, "wkT": np.asarray(inputs["L0_attn_wk"]).T,
        "wvT": np.asarray(inputs["L0_attn_wv"]).T, "woT": np.asarray(inputs["L0_attn_wo"]).T,
        "gateT": np.asarray(inputs["L0_ffn_gate_w"]).T,
        "beta": np.asarray(inputs["L0_ffn_beta"]).reshape(1, E),
        "gate_w": inputs["L0_ffn_gate_proj_w"], "up_w": inputs["L0_ffn_up_proj_w"],
        "down_w": inputs["L0_ffn_down_proj_w"], "sgate_w": inputs["L0_ffn_shared_gate_w"],
        "sup_w": inputs["L0_ffn_shared_up_w"], "sdown_w": inputs["L0_ffn_shared_down_w"],
        **shape_constants(),
    }
    arrays = {n: np.ascontiguousarray(v) for n, v in arrays.items()}
    nc = bacc.Bacc("TRN2", target_bir_lowering=False, num_devices=1)
    aps = {n: nc.dram_tensor(f"in_{n}", v.shape, mybir.dt.from_np(v.dtype), kind="ExternalInput").ap()
           for n, v in arrays.items()}
    out = nc.dram_tensor("out", (TOK, D), F32, kind="ExternalOutput").ap()
    build(nc, aps, out)
    r = run_bass_kernel_spmd(nc, [{f"in_{n}": v for n, v in arrays.items()}], core_ids=[0])
    return r.results[0]["out"].reshape(B, S, D)
```

```python
from contextlib import ExitStack

import numpy as np

import concourse.bass as bass
from concourse import mybir

F32 = mybir.dt.float32
BF16 = mybir.dt.bfloat16
I32 = mybir.dt.int32
ALU = mybir.AluOpType
ACT = mybir.ActivationFunctionType
AX_X = mybir.AxisListType.X

P = 128
B = 16
C, IMG, PS = 3, 96, 16
HP = IMG // PS
NPATCH = HP * HP
PD = C * PS * PS
PDC = PD // P
TXT = 32
S = 1 + NPATCH + TXT
D = 256
DC = D // P
NH, HD = 16, 16
HPT = P // HD
TOK = B * S
PAIRS = B // 2
PT = 96
NPT = B * NPATCH // PT
E, M, K = 8, 512, 2
MC = M // P
NT = -(-TOK // P)
LAST = TOK - (NT - 1) * P
NB = (K * TOK + E * (P - 1)) // P
NU = NT + NB
EPS = 1e-5
FAR = -1.0e30
QH = 4
QC = QH * S


def shape_constants():
    f = np.float32
    omega = (np.arange(D // 4, dtype=f) / f(D // 4 - 1)).astype(f)
    omega = (f(1.0) / np.power(f(10000.0), omega)).astype(f)
    yy, xx = np.meshgrid(np.arange(HP), np.arange(HP), indexing="ij")
    y = yy.reshape(-1)[:, None].astype(f) * omega[None]
    x = xx.reshape(-1)[:, None].astype(f) * omega[None]
    pe = np.concatenate((np.sin(x), np.cos(x), np.sin(y), np.cos(y)), axis=1).astype(f)
    pe = np.tile(pe, (B, 1)).reshape(NPT, PT, D).transpose(1, 0, 2).reshape(PT, NPT * D)
    freqs = (f(1.0) / np.power(f(10000.0), np.arange(0, HD, 2, dtype=f) / f(HD))).astype(f)
    ang = np.arange(S, dtype=f)[:, None] * freqs[None]
    cos = np.repeat(np.cos(ang), 2, axis=1).T
    sin = np.repeat(np.sin(ang), 2, axis=1).T * np.where(np.arange(HD) % 2 == 0, -1, 1)[:, None]
    rope = np.stack([np.tile(t, (HPT, 2 * DC)) for t in (cos, sin)], axis=1).astype(f)
    rope = rope.reshape(P, 2 * DC * 2 * S)
    heads = (np.arange(P)[:, None] // HD == np.arange(HPT)[None]).astype(f)
    ident = np.eye(P, dtype=f)
    causal = np.where(np.arange(S)[None] > np.arange(S)[:, None], FAR, 0.0).astype(f)
    before = (np.arange(P)[:, None] < np.arange(P)[None]).astype(f)
    first = np.tile(E - np.arange(E, dtype=f), NT)
    valid = (np.arange(NT * P) < TOK).astype(f).reshape(NT, P).T
    valid = np.repeat(valid, E, axis=1)
    steps = np.tile(np.arange(NT, dtype=f) * P, E)
    lower = (np.arange(E)[:, None] > np.arange(E)[None]).astype(f).reshape(-1)
    blocks = np.repeat(np.arange(NB, dtype=f), E)
    rows = np.concatenate([first, steps, lower, blocks])
    route = np.concatenate([np.tile(rows, (P, 1)), valid], axis=1).astype(f)
    return {"c_pe": pe.astype(f), "c_rope": rope, "c_heads": heads, "c_ident": ident,
            "c_causal": causal, "c_before": before, "c_route": route}


class Chain:

    def __init__(self, eng, sem):
        self.eng, self.sem, self.base, self.n = eng, sem, 0, 0

    def enter(self, round_, per):
        self.start, self.per = self.n, per
        self.base = round_ * per

    def leave(self, rounds):
        assert self.n - self.start == self.per, (self.n - self.start, self.per)
        self.n = self.start + rounds * self.per
        self.base = 0

    def __call__(self, ins):
        ins.then_inc(self.sem, 1)
        self.n += 1
        self.eng.wait_ge(self.sem, self.base + self.n)


def build(nc, a, out):
    ctx = ExitStack()
    with ctx:
        def sb(name, shape, dt=F32):
            return ctx.enter_context(nc.sbuf_tensor(name, shape, dt))

        def sem(name):
            return ctx.enter_context(nc.semaphore(name))

        def sems(name, n):
            return [sem(f"{name}{i}") for i in range(n)]

        patches_d = nc.dram_tensor("patches_d", [B * NPATCH, D], F32).ap()
        rows_d = nc.dram_tensor("rows_d", [NB * P, D], F32).ap()
        y_d = nc.dram_tensor("y_d", [NB * P, D], F32).ap()
        h1_d = nc.dram_tensor("h1_d", [TOK, D], F32).ap()

        wqk = sb("wqk", [P, DC * 2 * D])
        wv = sb("wv", [P, DC * D])
        wo = sb("wo", [P, DC * D])
        wgate = sb("wgate", [P, DC * E])
        wgu = sb("wgu", [P, (E + 1) * DC * 2 * M])
        wdn = sb("wdn", [P, (E + 1) * MC * D])
        ln1gb = sb("ln1gb", [P, 2 * PDC])
        rowp = sb("rowp", [PT, 3 * D])
        rope = sb("rope", [P, 2 * 2 * DC * S])
        heads = sb("heads", [P, HPT])
        ident = sb("ident", [P, P])
        identb = sb("identb", [P, P], BF16)
        causalb = sb("causalb", [S, S], BF16)
        beforeb = sb("beforeb", [P, P], BF16)
        onesb = sb("onesb", [P, P], BF16)
        zero = sb("zero", [P, D])
        TE = NT * E
        NR = 2 * TE + E * E + NB * E
        route = sb("route", [P, NR + TE])
        beta = sb("beta", [P, E])
        cls = sb("cls", [1, 2 * D])
        stats = sb("stats", [P, 12])
        stats_all = sb("stats_all", [P, 6 * B])
        mv = sb("mv", [P, 2 * 2])
        dev = sb("dev", [P, 2])
        rstd = sb("rstd", [P, 2])
        mv_all = sb("mv_all", [P, 2 * B])
        dev_all = sb("dev_all", [P, B])
        rstd_all = sb("rstd_all", [P, B])
        eps = sb("eps", [P, 1])
        mx = sb("mx", [S, NH])
        rs = sb("rs", [S, NH])
        m12z = sb("m12z", [P, 2 * TE - E], BF16)
        m12 = m12z[:, TE - E:]
        rsm = sb("rsm", [P, 6 * NT])
        nb = sb("nb", [P, 4 * E])
        eidf = sb("eidf", [P, NB])
        eid = sb("eid", [P, NB], I32)
        slot = [sb(f"slot{i}", [P, NT], I32) for i in range(K)]
        csel = sb("csel", [P, K * NT])
        stream = sb("stream", [P, B * D])
        h_all = stream[0:S, :]
        acc = stream[:, 0:NT * D]

        class Arena:

            def __init__(self, name, words):
                self.whole, self.words, self.at = sb(name, [P, words]), words, 0

            def take(self, rows, words):
                part = self.whole[0:rows, self.at:self.at + words]
                self.at += words
                assert self.at <= self.words
                return part

            def again(self):
                self.at = 0

        early = Arena("early", 2 * PD + 3 * PDC * PT + 2 * D + NPT * D + 2 * PDC * D)
        wpatch = early.take(P, PDC * D)
        pe = early.take(PT, NPT * D)
        wgain = early.take(P, PDC * D)
        xn = [early.take(PT, PD) for _ in range(2)]
        xnT = [early.take(P, PDC * PT) for _ in range(2)]
        yt = [early.take(PT, D) for _ in range(2)]
        ln1b = early.take(P, PDC * PT)
        early.again()
        n_t = early.take(S, 2 * D)
        W2 = DC * 2 * S
        nT, qc, kc, qs, ks, qr, kr = (early.take(P, W2) for _ in range(7))
        VW = 2 * NH * (HD + 1)
        v_sb = early.take(S, 2 * VW)
        on = early.take(S, D)
        oT = early.take(P, DC * S)
        m_all = early.take(P, NT * D)
        lg = early.take(P, TE)
        rt = early.take(P, 6 * TE)
        wide = early.take(P, NB * E)

        late = Arena("late", max(DC * HPT * 2 * S + 3 * NH * S, NT * D + 5 * D + 4 * M, NPT * PD))
        xp = late.take(PT, NPT * PD)
        late.again()
        kbd = late.take(P, DC * HPT * 2 * S)
        prob = [late.take(S, NH * S) for _ in range(2)]
        probT = late.take(S, NH * S)
        late.again()
        xT_all = late.take(P, NT * D)
        xin = [late.take(P, D) for _ in range(2)]
        xT = late.take(P, D)
        sg = [late.take(P, M) for _ in range(2)]
        hb = late.take(P, M)
        hT = late.take(P, M)
        yb = [late.take(P, D) for _ in range(2)]
        late.again()
        gath = [[late.take(P, D) for _ in range(K)] for _ in range(3)]

        ps = ctx.enter_context(nc.psum_tensor("ps", [P, 8, 512], F32))

        s_c = sem("const_in")
        s_cb = sem("bf16_const_in")
        s_w1 = sem("patch_weights_in")
        s_w2 = sem("attn_weights_in")
        s_w3 = sem("ffn_weights_in")
        s_cls = sem("cls_in")
        s_clsadd = sem("cls_added")
        s_txt = sem("txt_in")
        s_const = sem("const_made")
        s_zero = sem("zero_made")
        s_rows0 = sem("rows_cleared")
        xp_in = sems("xp_in", NPT)
        x_normed = sem("x_normed")
        patch_T = sem("patch_T")
        affine_done = sem("affine_done")
        patch_mm = sem("patch_mm")
        patch_read = sem("patch_read")
        patch_out = sem("patch_out")
        y_normed = sem("y_normed")
        pe_made = sem("pe_made")
        patch_stored = sems("patch_stored", 2)
        h_in = sem("h_in")
        n_ready = sem("n_ready")
        nT_psum = sem("nT_psum")
        nT_ready = sem("nT_ready")
        qk_done = sem("qk_done")
        rope_in = sem("rope_in")
        qk_ready = sem("qk_ready")
        kr_ready = sem("kr_ready")
        kbd1_ready = sem("kbd1_ready")
        scores_done = sem("scores_done")
        shifted = sem("shifted")
        exp_done = sem("exp_done")
        probT_psum = sem("probT_psum")
        probT_ready = sem("probT_ready")
        v_done = sem("v_done")
        v_ready = sem("v_ready")
        pv_done = sem("pv_done")
        o_normed = sem("o_normed")
        oT_psum = sem("oT_psum")
        oT_ready = sem("oT_ready")
        wo_done = sem("wo_done")
        resid_done = sem("resid_done")
        moved = sem("moved")
        deviated = sem("deviated")
        image_moved = sem("image_moved")
        h1_stored = sem("h1_stored")
        h1_in = sem("h1_in")
        m_ready = sem("m_ready")
        rT_psum = sem("rT_psum")
        rT_ready = sem("rT_ready")
        logits_done = sem("logits_done")
        chosen = sem("chosen")
        ranked = sem("ranked")
        picked = sem("picked")
        c_ready = sem("c_ready")
        slots_ready = sem("slots_ready")
        scattered = sem("scattered")
        x_in = sems("x_in", 2)
        xT_psum = sem("xT_psum")
        xT_ready = sem("xT_ready")
        g_done = sem("g_done")
        u_done = sem("u_done")
        silu_done = sem("silu_done")
        h_ready = sem("h_ready")
        hT_psum = sem("hT_psum")
        hT_ready = sem("hT_ready")
        d_done = sem("d_done")
        y_ready = sem("y_ready")
        y_stored = sems("y_stored", 2)
        ln1b_ready = sem("ln1b_ready")
        ln1b_done = sem("ln1b_done")
        gained = sem("gained")
        gathered = sems("gathered", 3)
        tile_out = sem("tile_out")
        out_stored = sem("out_stored")
        dve_step = sem("dve_step")
        pool_step = sem("pool_step")

        def bc(ap, shape):
            return ap.broadcast_to(shape)

        ps_s = ps[0:S, 0:4, 0:QC].rearrange("p b (h k) -> p b h k", k=S)
        ps_pt = [ps[:, 4 + i, 0:QC] for i in range(2)]
        ps_oT = ps[:, 7, VW // 2:VW // 2 + DC * S]
        ps_q = ps[:, 4, 0:DC * 2 * S]
        ps_k = ps[:, 5, 0:DC * 2 * S]
        ps_nT = ps[:, 6, 0:DC * 2 * S]
        ps_o = ps[0:S, 7, 0:NH * (HD + 1)]
        ps_wo = ps[0:S, 6, 0:D]
        ps_v = ps[0:S, 6, 0:2 * D]

        var_all = mv_all[:, :].rearrange("p (i k) -> p i k", k=2)[:, :, 1]
        GROUPS = ((0, 4), (4, B))

        def spread_keys(engine, t):
            o = kbd[:, t * HPT * 2 * S:(t + 1) * HPT * 2 * S].rearrange("p (h k) -> p h k", h=HPT)
            return engine.tensor_tensor(o, bc(kr[:, t * 2 * S:(t + 1) * 2 * S].unsqueeze(1), [P, HPT, 2 * S]),
                                        bc(heads[:, :].unsqueeze(2), [P, HPT, 2 * S]), ALU.mult)

        block = ctx.enter_context(nc.Block())

        @block.sync
        def _(sp):
            for i in range(NPT):
                sp.dma_start(xp[:, i * PD:(i + 1) * PD], a["patches"][i * PT:(i + 1) * PT, :]).then_inc(xp_in[i], 16)
                if i == 0:
                    sp.dma_start(ln1gb[:, :], a["ln1gb"]).then_inc(s_w1, 16)
                    sp.dma_start(ident[:, :], a["c_ident"]).then_inc(s_w1, 16)
            for i, n in enumerate(("bias", "ln2_g", "ln2_b")):
                sp.dma_start(rowp[:, i * D:(i + 1) * D], a[n].partition_broadcast(PT)).then_inc(s_c, 16)
            sp.dma_start(pe[:, :], a["c_pe"]).then_inc(s_c, 16)

            def store_patches(i, par):
                sp.wait_ge(patch_out, i + 1)
                sp.dma_start(patches_d[bass.ds(i * PT, PT), :], yt[par][:, :]).then_inc(patch_stored[par], 16)

            with sp.Fori(0, NPT // 2) as r:
                for par in range(2):
                    store_patches(r * 2 + par, par)
            for par in range(2):
                sp.wait_ge(patch_stored[par], 16 * (NPT // 2))
            sp.dma_start(h_all[1:1 + NPATCH, :].rearrange("p (b d) -> p b d", b=B),
                         patches_d.rearrange("(b p) d -> p b d", b=B)).then_inc(h_in, 16)

            gu_v = wgu[:, :].rearrange("p (e c x m) -> p e c x m", e=E + 1, c=DC, x=2)
            dn_v = wdn[:, :].rearrange("p (e c n) -> p e c n", e=E + 1, c=MC)
            for e in (E, *range(E)):
                for x, (all_w, shared) in enumerate((("gate_w", "sgate_w"), ("up_w", "sup_w"))):
                    src = a[shared][0] if e == E else a[all_w][e]
                    sp.dma_start(gu_v[:, e, :, x, :], src.rearrange("(c p) m -> p c m", p=P)).then_inc(s_w3, 16)
                src = a["sdown_w"][0] if e == E else a["down_w"][e]
                sp.dma_start(dn_v[:, e, :, :], src.rearrange("(c p) n -> p c n", p=P)).then_inc(s_w3, 16)

            with sp.Fori(0, PAIRS) as p:
                for b in range(2):
                    n = p * 2 + b
                    sp.wait_ge(resid_done, n + 1)
                    sp.dma_start(h1_d[bass.ds(n * S, S), :], h_all[:, bass.ds(n * D, D)]).then_inc(h1_stored, 16)
            sp.wait_ge(h1_stored, 16 * B)
            sp.dma_start(acc[:, 0:(NT - 1) * D].rearrange("p (t d) -> p t d", t=NT - 1),
                         h1_d[0:(NT - 1) * P, :].rearrange("(t p) d -> p t d", p=P)).then_inc(h1_in, 16)
            sp.dma_start(acc[0:LAST, (NT - 1) * D:], h1_d[(NT - 1) * P:TOK, :]).then_inc(h1_in, 16)

            def load_x(j, par, first=False):
                if not first:
                    sp.wait_ge(xT_psum, j - 1)
                sp.dma_start(xin[par][:, :], rows_d[bass.ds(j * P, P), :]).then_inc(x_in[par], 16)

            sp.wait_ge(scattered, 16 * K * NT)
            load_x(0, 0, True)
            load_x(1, 1, True)
            rounds = (NB - 2) // 2
            with sp.Fori(0, rounds) as r:
                for o in range(2):
                    load_x(r * 2 + (2 + o), o)
            for j in range(2 + 2 * rounds, NB):
                load_x(j, j % 2)

            for t in range(NT):
                rows = P if t < NT - 1 else LAST
                sp.wait_ge(tile_out, t + 1)
                sp.dma_start(out[t * P:t * P + rows, :], acc[0:rows, t * D:(t + 1) * D]).then_inc(out_stored, 16)
            sp.wait_ge(out_stored, 16 * NT)

        @block.gpsimd
        def _(pool):
            link = Chain(pool, pool_step)
            pool.dma_start(identb[:, :], a["c_ident"]).then_inc(s_cb, 16)
            pool.dma_start(causalb[:, :], a["c_causal"]).then_inc(s_cb, 16)
            pool.dma_start(beforeb[:, :], a["c_before"]).then_inc(s_cb, 16)
            nc.gpsimd.memset(onesb[:, :], 1.0).then_inc(s_const, 1)

            def rope_pool(p, first=False):
                pool.wait_ge(rope_in, p + 1)
                nc.gpsimd.tensor_tensor(ks[:, :], ks[:, :], rope[:, W2:2 * W2], ALU.mult)
                link(nc.gpsimd.tensor_tensor(qs[:, :], qs[:, :], rope[:, W2:2 * W2], ALU.mult))
                if not first:
                    pool.wait_ge(kbd1_ready, p)
                nc.gpsimd.tensor_tensor(kr[:, :], kc[:, :], ks[:, :], ALU.add).then_inc(kr_ready, 1)
                pool.wait_ge(kr_ready, p + 1)
                if not first:
                    pool.wait_ge(scores_done, p * 2)
                nc.gpsimd.tensor_tensor(qr[:, :], qc[:, :], qs[:, :], ALU.add)
                spread_keys(nc.gpsimd, 0).then_inc(qk_ready, 1)

            pool.wait_ge(pe_made, 1)

            def patch_end(i, par):
                pool.wait_ge(y_normed, i + 1)
                y = yt[par]
                link(nc.gpsimd.tensor_tensor(y, y, rowp[:, D:2 * D], ALU.mult))
                nc.gpsimd.tensor_tensor(y, y, pe[:, bass.ds(i * D, D)], ALU.add).then_inc(patch_out, 1)

            with pool.Fori(0, NPT // 2) as r:
                link.enter(r, 2)
                for par in range(2):
                    patch_end(r * 2 + par, par)
                link.leave(NPT // 2)
            pool.wait_ge(h_in, 16)
            nc.gpsimd.memset(v_sb[:, :], 1.0).then_inc(s_const, 1)
            pool.wait_ge(s_w2, 16 * 9)
            rope_pool(0, True)
            with pool.Fori(1, PAIRS) as p:
                link.enter(p - 1, 1)
                rope_pool(p)
                link.leave(PAIRS - 1)

            pool.wait_ge(slots_ready, 2)
            pool.wait_ge(s_rows0, 16)
            for t in range(NT):
                rows = P if t < NT - 1 else LAST
                for k in range(K):
                    nc.gpsimd.indirect_dma_start(
                        out=rows_d, out_offset=bass.IndirectOffsetOnAxis(ap=slot[k][0:rows, t:t + 1], axis=0),
                        in_=m_all[0:rows, t * D:(t + 1) * D], in_offset=None).then_inc(scattered, 16)

            for par in range(2):
                pool.wait_ge(y_stored[par], 16 * ((NB + 1 - par) // 2))
            pool.wait_ge(xT_ready, NT)
            for t in range(NT):
                rows = P if t < NT - 1 else LAST
                if t >= 3:
                    pool.wait_ge(tile_out, t - 2)
                for k in range(K):
                    nc.gpsimd.indirect_dma_start(
                        out=gath[t % 3][k][0:rows, :], out_offset=None, in_=y_d,
                        in_offset=bass.IndirectOffsetOnAxis(ap=slot[k][0:rows, t:t + 1], axis=0)
                    ).then_inc(gathered[t % 3], 16)

        @block.scalar
        def _(act):
            act.dma_start(wpatch.rearrange("p (c n) -> p c n", c=PDC),
                          a["W"].rearrange("(c p) n -> p c n", p=P)).then_inc(s_w1, 16)
            act.dma_start(cls[0:1, 0:D], a["cls_token"]).then_inc(s_cls, 16)
            act.dma_start(cls[0:1, D:2 * D], a["cls_pos"]).then_inc(s_cls, 16)
            act.dma_start(h_all[1 + NPATCH:S, :].rearrange("p (b d) -> p b d", b=B),
                          a["txt"].rearrange("b p d -> p b d")).then_inc(s_txt, 16)
            act.dma_start(rope[:, :], a["c_rope"]).then_inc(s_w2, 16)
            act.dma_start(heads[:, :], a["c_heads"]).then_inc(s_w2, 16)
            for i, n in enumerate(("wqT", "wkT")):
                act.dma_start(wqk[:, :].rearrange("p (c x n) -> p c x n", c=DC, x=2)[:, :, i, :],
                              a[n].rearrange("(c p) n -> p c n", p=P)).then_inc(s_w2, 16)
            for w, n in ((wv, "wvT"), (wo, "woT"), (wgate, "gateT")):
                act.dma_start(w[:, :].rearrange("p (c n) -> p c n", c=DC),
                              a[n].rearrange("(c p) n -> p c n", p=P)).then_inc(s_w2, 16)
            act.dma_start(route[:, :], a["c_route"]).then_inc(s_w2, 16)
            act.dma_start(beta[:, :], a["beta"].partition_broadcast(P)).then_inc(s_w2, 16)
            def deviation(count):
                act.wait_ge(moved, count)
                nc.scalar.activation(dev[0:PT, :], mv[0:PT, :].rearrange("p (i k) -> p i k", k=2)[:, :, 1], ACT.Sqrt,
                                     bias=eps[0:PT, :]).then_inc(deviated, 1)

            def xnT_copy(i, par, first=False):
                act.wait_ge(patch_T, i + 1)
                if not first:
                    act.wait_ge(patch_mm, i - 1)
                nc.scalar.activation(xnT[par].rearrange("p (b n) -> p b n", b=2), ps[:, 0:2, 0:3 * PT],
                                     ACT.Copy).then_inc(affine_done, 1)

            deviation(1)
            xnT_copy(0, 0, True)
            xnT_copy(1, 1, True)
            act.wait_ge(s_clsadd, 1)
            act.dma_start(h_all[0:1, :].rearrange("p (b d) -> p b d", b=B),
                          bc(cls[0:1, 0:D].unsqueeze(1), [1, B, D])).then_inc(s_txt, 16)
            with act.Fori(0, NPT // 2 - 1) as r:
                for par in range(2):
                    deviation(r * 2 + (par + 2))
                    xnT_copy(r * 2 + (par + 2), par)
            for i in (NPT - 2, NPT - 1):
                deviation(i + 2)
            for g, (b0, b1) in enumerate(GROUPS):
                act.wait_ge(image_moved, g + 1)
                nc.scalar.activation(dev_all[0:S, b0:b1], var_all[0:S, b0:b1], ACT.Sqrt,
                                     bias=eps[0:S, :]).then_inc(deviated, 1)

            def nT_copy(p, first=False):
                act.wait_ge(nT_psum, p + 1)
                if not first:
                    act.wait_ge(v_done, p)
                nc.scalar.activation(nT[:, :], ps_nT, ACT.Copy).then_inc(nT_ready, 1)

            def v_copy(p, parity, first=False):
                act.wait_ge(v_done, p + 1)
                if not first:
                    act.wait_ge(pv_done, (p - 1) * 8)
                dst = v_sb[:, bass.ds(parity * VW, VW)].rearrange("p (b h d) -> p b h d", b=2, d=HD + 1)
                for b in range(2):
                    ins = nc.scalar.activation(dst[:, b, :, 0:HD],
                                               ps_v[:, b * D:(b + 1) * D].rearrange("p (h d) -> p h d", h=NH), ACT.Copy)
                ins.then_inc(v_ready, 1)

            def expo(n, b):
                act.wait_ge(shifted, n + 1)
                nc.scalar.activation(prob[b][:, :], prob[b][:, :], ACT.Exp, scale=HD ** -0.5).then_inc(exp_done, 1)

            def probT_copies(n, first=False):
                for k in range(4):
                    act.wait_ge(probT_psum, n * 4 + (k + 1))
                    if not first:
                        act.wait_ge(pv_done, n * 4 + k - 3)
                    nc.scalar.activation(probT[:, k * QC:(k + 1) * QC], ps_pt[k % 2][0:S, :],
                                         ACT.Copy).then_inc(probT_ready, 1)

            def oT_copy(n, first=False):
                act.wait_ge(oT_psum, n + 1)
                if not first:
                    act.wait_ge(wo_done, n)
                nc.scalar.activation(oT[:, :], ps_oT, ACT.Copy).then_inc(oT_ready, 1)

            def slot_even(p, parity, before=True, following=True):
                n = p * 2
                if before:
                    probT_copies(n - 1)
                if following:
                    nT_copy(p + 1)
                expo(n, 0)
                if before:
                    oT_copy(n - 1)

            def slot_odd(p, parity, first=False, following=True):
                n = p * 2 + 1
                probT_copies(n - 1, first)
                expo(n, 1)
                if following:
                    v_copy(p + 1, parity, first)
                oT_copy(n - 1, first)

            act.wait_ge(s_const, 2)
            act.wait_ge(s_zero, 1)
            act.dma_start(rows_d.rearrange("(j p) d -> p j d", p=P),
                          bc(zero[:, :].unsqueeze(1), [P, NB, D])).then_inc(s_rows0, 16)
            nT_copy(0, True)
            v_copy(0, 0, True)
            slot_even(0, 0, before=False)
            slot_odd(0, 1, first=True)
            with act.Fori(1, PAIRS - 1) as p:
                slot_even(p, None)
                slot_odd(p, (p + 1) % 2)
            slot_even(PAIRS - 1, None, following=False)
            slot_odd(PAIRS - 1, None, following=False)
            probT_copies(B - 1)
            oT_copy(B - 1)

            act.wait_ge(moved, NPT + 2)
            nc.scalar.activation(dev_all[:, 0:NT], var_all[:, 0:NT], ACT.Sqrt, bias=eps[:, :]).then_inc(deviated, 1)
            for t in range(NT):
                act.wait_ge(rT_psum, t + 1)
                nc.scalar.activation(xT_all[:, t * D:(t + 1) * D], ps[:, t % 2, 0:D], ACT.Copy).then_inc(rT_ready, 1)
            act.wait_ge(picked, 1)
            nc.scalar.activation(csel[:, :], rsm[:, 4 * NT:6 * NT], ACT.Sigmoid).then_inc(c_ready, 1)

            def xT_copy(j, shared):
                act.wait_ge(u_done, j)
                if shared:
                    nc.scalar.activation(xT[:, :], xT_all[:, bass.ds(j * D, D)], ACT.Copy).then_inc(xT_ready, 1)
                else:
                    act.wait_ge(xT_psum, j - (NT - 1))
                    nc.scalar.activation(xT[:, :], ps[:, 4, 0:D], ACT.Copy).then_inc(xT_ready, 1)

            def silu(j, par, first):
                act.wait_ge(g_done, j + 1)
                if not first:
                    act.wait_ge(h_ready, j - 1)
                nc.scalar.activation(sg[par][:, :], ps[:, 2 * par, :], ACT.Silu).then_inc(silu_done, 1)

            def y_copy(j, par, first):
                act.wait_ge(d_done, j + 1)
                if not first:
                    act.wait_ge(y_stored[par], (j - (NT + par)) * 8)
                nc.scalar.activation(yb[par][:, :], ps[:, 6, 0:D], ACT.Copy).then_inc(y_ready, 1)
                act.wait_ge(y_ready, j + 1)
                act.dma_start(y_d[bass.ds((j - NT) * P, P), :], yb[par][:, :]).then_inc(y_stored[par], 16)

            def run(first, n):
                shared = first == 0

                def step(j, k, t=True, g=True, d=True):
                    if g:
                        silu(j, (first + k) % 2, shared and k < 2)
                    if t:
                        xT_copy(j + 1, shared)
                    if d and not shared:
                        y_copy(j - 2, k % 2, k < 4)

                xT_copy(first, shared)
                for k in range(4):
                    step(first + k, k, d=k >= 2)
                rounds = (n - 5) // 2
                with act.Fori(0, rounds) as r:
                    for o in range(2):
                        step(r * 2 + (first + 4 + o), 4 + o)
                for k in range(4 + 2 * rounds, n + 2):
                    step(first + k, k, t=k + 1 < n, g=k < n)

            run(0, NT)
            run(NT, NB)

        @block.tensor
        def _(pe_):
            def patch_transpose(i, par, first=False):
                pe_.wait_ge(x_normed, i + 1)
                if not first:
                    pe_.wait_ge(affine_done, i)
                for c in range(PDC):
                    ins = nc.tensor.transpose(ps[:, c // 3, (c % 3) * PT:(c % 3 + 1) * PT],
                                              xn[par][:, c * P:(c + 1) * P], ident[0:PT, 0:PT])
                ins.then_inc(patch_T, 1)

            def patch_product(i, par, first=False):
                pe_.wait_ge(affine_done, i + 1)
                if not first:
                    pe_.wait_ge(patch_read, i)
                for c in range(PDC):
                    ins = nc.tensor.matmul(ps[0:PT, 2, 0:D], xnT[par][:, c * PT:(c + 1) * PT],
                                           wgain[:, c * D:(c + 1) * D], start=(c == 0), stop=(c == PDC - 1))
                ins.then_inc(patch_mm, 1)

            pe_.wait_ge(s_w1, 16 * 3)
            pe_.wait_ge(ln1b_ready, 1)
            for c in range(PDC):
                ins = nc.tensor.matmul(ps[0:PT, 3, 0:D], ln1b[:, c * PT:(c + 1) * PT], wpatch[:, c * D:(c + 1) * D],
                                       start=(c == 0), stop=(c == PDC - 1))
            ins.then_inc(ln1b_done, 1)
            patch_transpose(0, 0, True)
            patch_transpose(1, 1)
            pe_.wait_ge(gained, 1)
            patch_product(0, 0, True)
            with pe_.Fori(0, NPT // 2 - 1) as r:
                patch_product(r * 2 + 1, 1)
                patch_transpose(r * 2 + 2, 0)
                patch_product(r * 2 + 2, 0)
                patch_transpose(r * 2 + 3, 1)
            patch_product(NPT - 1, 1)

            def nT_of(p, free=None):
                pe_.wait_ge(n_ready, p * 2 + 2)
                if free is not None:
                    pe_.wait_ge(resid_done, free)
                for b in range(2):
                    for c in range(DC):
                        ins = nc.tensor.transpose(ps_nT[:, (c * 2 + b) * S:(c * 2 + b + 1) * S],
                                                  n_t[:, b * D + c * P:b * D + (c + 1) * P], ident[0:S, 0:S])
                ins.then_inc(nT_psum, 1)

            def qk_of(p):
                pe_.wait_ge(nT_ready, p + 1)
                for x, dst in enumerate((ps_q, ps_k)):
                    for t in range(DC):
                        for c in range(DC):
                            ins = nc.tensor.matmul(dst[:, t * 2 * S:(t + 1) * 2 * S],
                                                   wqk[:, c * 2 * D + x * D + t * P:c * 2 * D + x * D + (t + 1) * P],
                                                   nT[:, c * 2 * S:(c + 1) * 2 * S], start=(c == 0), stop=(c == DC - 1))
                ins.then_inc(qk_done, 1)

            def v_of(p, free=None):
                if free is not None:
                    pe_.wait_ge(resid_done, free)
                for b in range(2):
                    for c in range(DC):
                        ins = nc.tensor.matmul(ps_v[:, b * D:(b + 1) * D], nT[:, (c * 2 + b) * S:(c * 2 + b + 1) * S],
                                               wv[:, c * D:(c + 1) * D], start=(c == 0), stop=(c == DC - 1))
                ins.then_inc(v_done, 1)

            def scores(p, b, first=False):
                n = p * 2 + b
                pe_.wait_ge(qk_ready, p + 1)
                pe_.wait_ge(kbd1_ready, p + 1)
                if not first:
                    pe_.wait_ge(shifted, n)
                kv = kbd[:, :].rearrange("p (g h b k) -> p g h b k", g=4, h=QH, b=2)
                for g in range(4):
                    t = g // 2
                    nc.tensor.matmul(ps_s[:, g, :, :], qr[:, (t * 2 + b) * S:(t * 2 + b + 1) * S],
                                     kv[:, g, :, b, :], start=True, stop=False)
                    ins = nc.tensor.matmul(ps_s[:, g, :, :], identb[0:S, 0:S],
                                           bc(causalb[:, :].unsqueeze(1), [S, QH, S]), start=False, stop=True)
                ins.then_inc(scores_done, 1)

            def probT_of(n, b, k, first=False):
                if not first:
                    pe_.wait_ge(probT_ready, n * 4 + k - 1)
                for h in range(QH):
                    ins = nc.tensor.transpose(ps_pt[k % 2][0:S, h * S:(h + 1) * S],
                                              prob[b][:, (k * QH + h) * S:(k * QH + h + 1) * S], ident[0:S, 0:S])
                ins.then_inc(probT_psum, 1)

            def pv_of(n, b, k, parity):
                pe_.wait_ge(probT_ready, n * 4 + k + 1)
                for h in range(k * QH, (k + 1) * QH):
                    at = (b * NH + h) * (HD + 1)
                    ins = nc.tensor.matmul(ps_o[:, h * (HD + 1):(h + 1) * (HD + 1)], probT[:, h * S:(h + 1) * S],
                                           v_sb[:, bass.ds(parity * VW + at, HD + 1)], start=True, stop=True)
                ins.then_inc(pv_done, 1)

            def oT_of(n):
                pe_.wait_ge(o_normed, n + 1)
                for c in range(DC):
                    ins = nc.tensor.transpose(ps_oT[:, c * S:(c + 1) * S], on[:, c * P:(c + 1) * P], ident[0:S, 0:S])
                ins.then_inc(oT_psum, 1)

            def wo_of(n, first=False):
                pe_.wait_ge(oT_ready, n + 1)
                if not first:
                    pe_.wait_ge(resid_done, n)
                for c in range(DC):
                    ins = nc.tensor.matmul(ps_wo, oT[:, c * S:(c + 1) * S], wo[:, c * D:(c + 1) * D],
                                           start=(c == 0), stop=(c == DC - 1))
                ins.then_inc(wo_done, 1)

            def context(n, b, pair, parity, first=False, output=True, out_first=False, nT_next=None):
                pe_.wait_ge(exp_done, n + 1)
                probT_of(n, b, 0, first)
                probT_of(n, b, 1, first)
                pe_.wait_ge(v_ready, pair + 1)
                if output:
                    wo_of(n - 1, out_first)
                if not first:
                    pe_.wait_ge(oT_ready, n)
                pv_of(n, b, 0, parity)
                probT_of(n, b, 2)
                pv_of(n, b, 1, parity)
                probT_of(n, b, 3)
                if nT_next is not None:
                    nT_of(*nT_next)
                pv_of(n, b, 2, parity)
                pv_of(n, b, 3, parity)

            def slot_even(p, parity, following=True):
                n = p * 2
                scores(p, 0)
                context(n - 1, 1, p - 1, parity, nT_next=(p + 1, n - 1) if following else None)
                if following:
                    qk_of(p + 1)
                oT_of(n - 1)

            def slot_odd(p, parity, following=True, first=False):
                n = p * 2 + 1
                scores(p, 1)
                if following:
                    pe_.wait_ge(rope_in, p + 2)
                context(n - 1, 0, p, parity, first=first, output=not first)
                if following:
                    v_of(p + 1, None if first else n - 1)
                oT_of(n - 1)

            pe_.wait_ge(s_w2, 16 * 9)
            pe_.wait_ge(s_cb, 16 * 3)
            pe_.wait_ge(patch_read, NPT)
            nT_of(0)
            qk_of(0)
            v_of(0)
            scores(0, 0, True)
            pe_.wait_ge(v_ready, 1)
            nT_of(1)
            pe_.wait_ge(rope_in, 1)
            qk_of(1)
            slot_odd(0, 0, first=True)
            with pe_.Fori(1, PAIRS - 1) as p:
                slot_even(p, (p + 1) % 2)
                slot_odd(p, p % 2)
            slot_even(PAIRS - 1, (PAIRS - 2) % 2, following=False)
            slot_odd(PAIRS - 1, (PAIRS - 1) % 2, following=False)
            context(B - 1, 1, PAIRS - 1, (PAIRS - 1) % 2)
            oT_of(B - 1)
            wo_of(B - 1)

            pe_.wait_ge(resid_done, B)
            pe_.wait_ge(s_const, 2)
            ps_lg = ps[:, 7, 0:NT * E]

            def logits(t):
                pe_.wait_ge(rT_ready, t + 1)
                for c in range(DC):
                    ins = nc.tensor.matmul(ps_lg[:, t * E:(t + 1) * E], xT_all[:, t * D + c * P:t * D + (c + 1) * P],
                                           wgate[:, c * E:(c + 1) * E], start=(c == 0), stop=(c == DC - 1))
                ins.then_inc(logits_done, 1)

            for t in range(NT):
                pe_.wait_ge(m_ready, t + 1)
                if t >= 2:
                    pe_.wait_ge(rT_ready, t - 1)
                for c in range(DC):
                    ins = nc.tensor.transpose(ps[:, t % 2, c * P:(c + 1) * P],
                                              m_all[:, t * D + c * P:t * D + (c + 1) * P], ident[:, :])
                ins.then_inc(rT_psum, 1)
                if t >= 1:
                    logits(t - 1)
            logits(NT - 1)
            pe_.wait_ge(chosen, 1)
            ps_rank = ps[:, 7, 128:128 + NT * E]
            nc.tensor.matmul(ps_rank, beforeb[:, :], m12[:, :], start=True, stop=False)
            for s in range(1, NT):
                ins = nc.tensor.matmul(ps_rank, onesb[:, :], m12z[:, TE - (s + 1) * E:2 * TE - (s + 1) * E],
                                       start=False, stop=(s == NT - 1))
            for t in range(NT):
                ins = nc.tensor.matmul(ps[:, 7, 256:256 + E], onesb[:, :], m12[:, t * E:(t + 1) * E],
                                       start=(t == 0), stop=(t == NT - 1))
            ins.then_inc(ranked, 1)

            def x_transpose(j, par, n_in):
                pe_.wait_ge(x_in[par], n_in)
                pe_.wait_ge(xT_ready, j)
                for c in range(DC):
                    ins = nc.tensor.transpose(ps[:, 4, c * P:(c + 1) * P], xin[par][:, c * P:(c + 1) * P], ident[:, :])
                ins.then_inc(xT_psum, 1)

            def gate_up(j, par, e, first):
                pe_.wait_ge(xT_ready, j + 1)
                if not first:
                    pe_.wait_ge(h_ready, j - 1)
                for x, done in enumerate((g_done, u_done)):
                    for c in range(DC):
                        at = (c * 2 + x) * M
                        ins = nc.tensor.matmul(ps[:, 2 * par + x, :], xT[:, c * P:(c + 1) * P],
                                               wgu[:, bass.ds(e * (DC * 2 * M) + at, M)],
                                               start=(c == 0), stop=(c == DC - 1))
                    ins.then_inc(done, 1)

            def h_transpose(j):
                pe_.wait_ge(h_ready, j + 1)
                pe_.wait_ge(hT_ready, j)
                for c in range(MC):
                    ins = nc.tensor.transpose(ps[:, 5, c * P:(c + 1) * P], hb[:, c * P:(c + 1) * P], ident[:, :])
                ins.then_inc(hT_psum, 1)

            def down(j, e):
                pe_.wait_ge(hT_ready, j + 1)
                pe_.wait_ge(y_ready, j)
                for c in range(MC):
                    ins = nc.tensor.matmul(ps[:, 6, 0:D], hT[:, c * P:(c + 1) * P],
                                           wdn[:, bass.ds(e * (MC * D) + c * D, D)],
                                           start=(c == 0), stop=(c == MC - 1))
                ins.then_inc(d_done, 1)

            def expert_of(j, first):
                if first == 0:
                    return E
                return pe_.value_load(eid[0:1, bass.ds(j - NT, 1)], min_val=0, max_val=E - 1)

            def run(first, n):
                def x_T(j, k):
                    if first:
                        x_transpose(j, k % 2, (j - (first + k % 2)) * 8 + 16)

                def full(j, k, t=True, g=True, h=True, d=True):
                    if t:
                        x_T(j + 1, k + 1)
                    if g:
                        gate_up(j, (first + k) % 2, expert_of(j, first), first == 0 and k < 2)
                    if h:
                        h_transpose(j - 1)
                    if d:
                        down(j - 2, expert_of(j - 2, first))

                x_T(first, 0)
                full(first, 0, h=False, d=False)
                full(first + 1, 1, d=False)
                rounds = (n - 3) // 2
                with pe_.Fori(0, rounds) as r:
                    for o in range(2):
                        full(r * 2 + (first + 2 + o), 2 + o)
                for k in range(2 + 2 * rounds, n + 2):
                    full(first + k, k, t=k + 1 < n, g=k < n, h=k - 1 < n)

            pe_.wait_ge(s_w3, 16 * 3 * (E + 1))
            run(0, NT)
            pe_.wait_ge(slots_ready, 2)
            run(NT, NB)

        @block.vector
        def _(dve):
            link = Chain(dve, dve_step)

            def moments(src, rows, width, st, out_mv):
                half = width // 512 + 1
                w = width // half
                for i in range(half):
                    ins = nc.vector.bn_stats(st[0:rows, 6 * i:6 * i + 6], src[:, i * w:(i + 1) * w])
                link(ins)
                return nc.vector.bn_aggr(out_mv, st[0:rows, 0:6 * half])

            def normed(dst, src, mean, inv):
                return nc.vector.tensor_scalar(dst, src, mean, inv, ALU.subtract, ALU.mult)

            nc.vector.memset(eps[:, :], EPS)
            nc.vector.memset(m12z[:, 0:TE - E], 0.0)
            link(nc.vector.memset(mv_all[:, :], 1.0))
            nc.vector.memset(zero[:, :], 0.0).then_inc(s_zero, 1)
            dve.wait_ge(s_w1, 16 * 3)
            nc.vector.tensor_copy(ln1b.rearrange("p (c n) -> p c n", c=PDC),
                                  bc(ln1gb[:, PDC:].unsqueeze(2), [P, PDC, PT])).then_inc(ln1b_ready, 1)
            for par in range(2):
                dve.wait_ge(xp_in[par], 16)
                ins = moments(xp[:, par * PD:(par + 1) * PD], PT, PD, stats, mv[0:PT, 2 * par:2 * par + 2])
                if par == 0:
                    link(ins)
            ins.then_inc(moved, 1)
            nc.vector.tensor_tensor(wgain.rearrange("p (c n) -> p c n", c=PDC), wpatch.rearrange("p (c n) -> p c n", c=PDC),
                                    bc(ln1gb[:, 0:PDC].unsqueeze(2), [P, PDC, D]), ALU.mult).then_inc(gained, 1)
            dve.wait_ge(deviated, 1)
            link(nc.vector.reciprocal(rstd[0:PT, :], dev[0:PT, :]))
            for par in range(2):
                normed(xn[par], xp[:, par * PD:(par + 1) * PD], mv[0:PT, 2 * par:2 * par + 1], rstd[0:PT, par:par + 1]).then_inc(x_normed, 1)
            dve.wait_ge(s_c, 16 * 4)
            dve.wait_ge(ln1b_done, 1)
            link(nc.vector.tensor_tensor(rowp[:, 0:D], rowp[:, 0:D], ps[0:PT, 3, 0:D], ALU.add))
            nc.vector.tensor_tensor(pe.rearrange("p (t d) -> p t d", t=NPT), pe.rearrange("p (t d) -> p t d", t=NPT),
                                    bc(rowp[:, 2 * D:3 * D].unsqueeze(1), [PT, NPT, D]), ALU.add).then_inc(pe_made, 1)
            dve.wait_ge(s_cls, 32)
            nc.vector.tensor_tensor(cls[0:1, 0:D], cls[0:1, 0:D], cls[0:1, D:2 * D], ALU.add).then_inc(s_clsadd, 1)

            def patch_step(i, par, xp_at=None, first=False):
                y = yt[par]
                if xp_at is not None:
                    x_in_ = xp[:, bass.ds(xp_at, PD)]
                    link(moments(x_in_, PT, PD, stats, mv[0:PT, 2:4]))
                dve.wait_ge(patch_mm, i + 1)
                if not first:
                    dve.wait_ge(patch_stored[par], (i - par) * 8)
                nc.vector.tensor_tensor(y, ps[0:PT, 2, 0:D], rowp[:, 0:D], ALU.add).then_inc(patch_read, 1)
                dve.wait_ge(patch_read, i + 1)
                moments(y, PT, D, stats, mv[0:PT, 0:2]).then_inc(moved, 1)
                dve.wait_ge(deviated, i + 2)
                link(nc.vector.reciprocal(rstd[0:PT, :], dev[0:PT, :]))
                if xp_at is not None:
                    normed(xn[par], x_in_, mv[0:PT, 2:3], rstd[0:PT, 1:2]).then_inc(x_normed, 1)
                normed(y, y, mv[0:PT, 0:1], rstd[0:PT, 0:1]).then_inc(y_normed, 1)

            for i in range(2):
                dve.wait_ge(xp_in[i + 2], 16)
                patch_step(i, i, (i + 2) * PD, True)
            for i in range(4, NPT):
                dve.wait_ge(xp_in[i], 16)
            with dve.Fori(1, NPT // 2 - 1) as r:
                link.enter(r - 1, 8)
                for par in range(2):
                    patch_step(r * 2 + par, par, (r * 2 + (par + 2)) * PD)
                link.leave(NPT // 2 - 2)
            for i in (NPT - 2, NPT - 1):
                patch_step(i, i % 2)

            def image_moments(g):
                b0, b1 = GROUPS[g]
                for b in range(b0, b1):
                    ins = nc.vector.bn_stats(stats_all[0:S, 6 * b:6 * b + 6], h_all[:, b * D:(b + 1) * D])
                link(ins)
                for b in range(b0, b1):
                    ins = nc.vector.bn_aggr(mv_all[0:S, 2 * b:2 * b + 2], stats_all[0:S, 6 * b:6 * b + 6])
                ins.then_inc(image_moved, 1)

            def image_rstd(g):
                b0, b1 = GROUPS[g]
                dve.wait_ge(deviated, NPT + 2 + g)
                link(nc.vector.reciprocal(rstd_all[0:S, b0:b1], dev_all[0:S, b0:b1]))

            def ln_pair(p, first=False):
                if not first:
                    dve.wait_ge(nT_psum, p)
                for b in range(2):
                    n = p * 2 + b
                    normed(n_t[:, b * D:(b + 1) * D], h_all[:, bass.ds(n * D, D)], mv_all[0:S, bass.ds(n * 2, 1)],
                           rstd_all[0:S, bass.ds(n, 1)]).then_inc(n_ready, 1)

            swap = [i ^ 1 for i in range(32)]

            def rope_dve(p, first=False):
                dve.wait_ge(qk_done, p + 1)
                if not first:
                    dve.wait_ge(qk_ready, p)
                nc.vector.tensor_tensor(qc[:, :], ps_q, rope[:, 0:W2], ALU.mult)
                nc.vector.stream_shuffle(qs[:, :], ps_q, swap)
                nc.vector.tensor_tensor(kc[:, :], ps_k, rope[:, 0:W2], ALU.mult)
                nc.vector.stream_shuffle(ks[:, :], ps_k, swap).then_inc(rope_in, 1)

            mx_v = mx[:, :].rearrange("p (g h) -> p g h", g=4)

            def row_max(n):
                dve.wait_ge(scores_done, n + 1)
                link(nc.vector.tensor_reduce(mx_v, ps_s, AX_X, ALU.max))

            def shift(n, b, first=False):
                if not first:
                    dve.wait_ge(probT_psum, n * 4 - 4)
                nc.vector.tensor_tensor(prob[b][:, :].rearrange("p (g h k) -> p g h k", g=4, h=QH), ps_s,
                                        bc(mx_v.unsqueeze(3), [S, 4, QH, S]), ALU.subtract).then_inc(shifted, 1)

            def spread(p, first=False):
                dve.wait_ge(kr_ready, p + 1)
                if not first:
                    dve.wait_ge(scores_done, p * 2)
                spread_keys(nc.vector, 1).then_inc(kbd1_ready, 1)

            def norm_o(n, first=False):
                dve.wait_ge(pv_done, n * 4 + 4)
                o_v = ps_o.rearrange("p (h d) -> p h d", h=NH)
                link(nc.vector.reciprocal(rs[:, :], o_v[:, :, HD]))
                if not first:
                    dve.wait_ge(oT_psum, n)
                nc.vector.tensor_tensor(on[:, :].rearrange("p (h d) -> p h d", h=NH), o_v[:, :, 0:HD],
                                        bc(rs[:, :].unsqueeze(2), [S, NH, HD]), ALU.mult).then_inc(o_normed, 1)

            def resid(n):
                dve.wait_ge(wo_done, n + 1)
                h = h_all[:, bass.ds(n * D, D)]
                nc.vector.tensor_tensor(h, ps_wo, h, ALU.add).then_inc(resid_done, 1)

            def slot_even(p, following=True):
                n = p * 2
                row_max(n)
                resid(n - 2)
                shift(n, 0)
                norm_o(n - 1)
                if following:
                    rope_dve(p + 1)

            def slot_odd(p, following=True, ln=True, first=False):
                n = p * 2 + 1
                row_max(n)
                if not first:
                    resid(n - 2)
                shift(n, 1, first)
                if following:
                    spread(p + 1)
                norm_o(n - 1, first)
                if ln:
                    ln_pair(p + 2)

            dve.wait_ge(h_in, 16)
            dve.wait_ge(s_txt, 32)
            dve.wait_ge(s_w2, 16 * 9)
            image_moments(0)
            image_rstd(0)
            ln_pair(0, True)
            image_moments(1)
            image_rstd(1)
            rope_dve(0, True)
            ln_pair(1)
            spread(0, True)
            row_max(0)
            shift(0, 0, True)
            rope_dve(1)
            slot_odd(0, first=True)
            with dve.Fori(1, PAIRS - 2) as p:
                link.enter(p - 1, 4)
                slot_even(p)
                slot_odd(p)
                link.leave(PAIRS - 3)
            slot_even(PAIRS - 2)
            slot_odd(PAIRS - 2, ln=False)
            slot_even(PAIRS - 1, following=False)
            slot_odd(PAIRS - 1, following=False, ln=False)
            resid(B - 2)
            norm_o(B - 1)
            resid(B - 1)

            dve.wait_ge(h1_in, 32)
            for t in range(NT):
                rows = P if t < NT - 1 else LAST
                ins = nc.vector.bn_stats(stats_all[0:rows, 6 * t:6 * t + 6], acc[0:rows, t * D:(t + 1) * D])
            link(ins)
            for t in range(NT):
                rows = P if t < NT - 1 else LAST
                ins = nc.vector.bn_aggr(mv_all[0:rows, 2 * t:2 * t + 2], stats_all[0:rows, 6 * t:6 * t + 6])
            ins.then_inc(moved, 1)
            dve.wait_ge(deviated, NPT + 2 + len(GROUPS))
            link(nc.vector.reciprocal(rstd_all[:, 0:NT], dev_all[:, 0:NT]))
            link(nc.vector.memset(m_all[64:P, (NT - 1) * D:], 0.0))
            for t in range(NT):
                rows = P if t < NT - 1 else LAST
                at = slice(t * D, (t + 1) * D)
                normed(m_all[0:rows, at], acc[0:rows, at], mv_all[0:rows, 2 * t:2 * t + 1],
                       rstd_all[0:rows, t:t + 1]).then_inc(m_ready, 1)
            r_first, r_steps = route[:, 0:TE], route[:, TE:2 * TE]
            r_lower, r_blocks = route[:, 2 * TE:2 * TE + E * E], route[:, 2 * TE + E * E:NR]
            r_valid = route[:, NR:NR + TE]

            def te(ap):
                return ap.rearrange("p (t e) -> p t e", e=E)

            biased, eq, wt, one, two, tmp = (rt[:, i * TE:(i + 1) * TE] for i in range(6))
            top = rsm[:, 0:NT]
            dve.wait_ge(logits_done, NT)
            link(nc.vector.tensor_copy(lg[:, :], ps[:, 7, 0:TE]))
            link(nc.vector.tensor_tensor(te(biased), te(lg[:, :]), bc(beta[:, :].unsqueeze(1), [P, NT, E]), ALU.add))
            for sel in (one, two):
                link(nc.vector.tensor_reduce(top, te(biased), AX_X, ALU.max))
                link(nc.vector.tensor_tensor(te(eq), te(biased), bc(top.unsqueeze(2), [P, NT, E]), ALU.is_equal))
                link(nc.vector.tensor_tensor(wt, eq, r_first, ALU.mult))
                link(nc.vector.tensor_reduce(top, te(wt), AX_X, ALU.max))
                link(nc.vector.tensor_tensor(te(sel), te(r_first), bc(top.unsqueeze(2), [P, NT, E]), ALU.is_equal))
                link(nc.vector.scalar_tensor_tensor(out=biased, in0=sel, scalar=-3.0e38, in1=biased,
                                                    op0=ALU.mult, op1=ALU.add))
            link(nc.vector.tensor_tensor(tmp, one, two, ALU.add))
            nc.vector.tensor_tensor(m12[:, :], tmp, r_valid, ALU.mult).then_inc(chosen, 1)
            dve.wait_ge(chosen, 1)
            for i, sel in enumerate((one, two)):
                link(nc.vector.tensor_tensor(tmp, sel, lg[:, :], ALU.mult))
                ins = nc.vector.tensor_reduce(rsm[:, (4 + i) * NT:(5 + i) * NT], te(tmp), AX_X, ALU.add)
                if i == 0:
                    link(ins)
            ins.then_inc(picked, 1)
            dve.wait_ge(picked, 1)
            dve.wait_ge(ranked, 1)
            cnt, nblk, base, upto = (nb[:, i * E:(i + 1) * E] for i in range(4))
            link(nc.vector.tensor_copy(cnt, ps[:, 7, 256:256 + E]))
            en = wide[:, 0:TE].rearrange("p (e s) -> p e s", e=E)
            link(nc.vector.tensor_tensor(en, bc(cnt.unsqueeze(2), [P, E, NT]),
                                         r_steps.rearrange("p (e s) -> p e s", e=E), ALU.is_gt))
            link(nc.vector.tensor_reduce(nblk, en, AX_X, ALU.add))
            ee = wide[:, 0:E * E].rearrange("p (e s) -> p e s", e=E)
            link(nc.vector.tensor_tensor(ee, bc(nblk.unsqueeze(1), [P, E, E]),
                                         r_lower.rearrange("p (e s) -> p e s", e=E), ALU.mult))
            link(nc.vector.tensor_reduce(base, ee, AX_X, ALU.add))
            link(nc.vector.tensor_tensor(upto, base, nblk, ALU.add))
            be = wide[:, :].rearrange("p (j e) -> p j e", e=E)
            link(nc.vector.tensor_tensor(be, r_blocks.rearrange("p (j e) -> p j e", e=E),
                                         bc(upto.unsqueeze(1), [P, NB, E]), ALU.is_ge))
            link(nc.vector.tensor_reduce(eidf[:, :], be, AX_X, ALU.add))
            nc.vector.tensor_scalar(eid[:, :], eidf[:, :], float(E - 1), None, ALU.min).then_inc(slots_ready, 1)
            link(nc.vector.tensor_scalar(upto, base, float(P), None, ALU.mult))
            link(nc.vector.tensor_tensor(te(wt), te(ps[:, 7, 128:128 + TE]), bc(upto.unsqueeze(1), [P, NT, E]), ALU.add))
            for i, sel in enumerate((one, two)):
                link(nc.vector.tensor_tensor(tmp, sel, wt, ALU.mult))
                link(nc.vector.tensor_reduce(rsm[:, (2 + i) * NT:(3 + i) * NT], te(tmp), AX_X, ALU.add))
            nc.vector.tensor_copy(slot[0][:, :], rsm[:, 2 * NT:3 * NT])
            nc.vector.tensor_copy(slot[1][:, :], rsm[:, 3 * NT:4 * NT]).then_inc(slots_ready, 1)

            def h_mult(j, par):
                dve.wait_ge(silu_done, j + 1)
                dve.wait_ge(u_done, j + 1)
                dve.wait_ge(hT_psum, j)
                nc.vector.tensor_tensor(hb[:, :], sg[par][:, :], ps[:, 2 * par + 1, :], ALU.mult).then_inc(h_ready, 1)

            def hT_copy(j):
                dve.wait_ge(hT_psum, j + 1)
                dve.wait_ge(d_done, j)
                nc.vector.tensor_copy(hT[:, :], ps[:, 5, :]).then_inc(hT_ready, 1)

            def shared_y(j):
                dve.wait_ge(d_done, j + 1)
                rows = LAST if isinstance(j, int) and j == NT - 1 else P
                at = acc[0:rows, bass.ds(j * D, D)]
                nc.vector.tensor_tensor(at, ps[0:rows, 6, 0:D], at, ALU.add).then_inc(y_ready, 1)

            def run(first, n):
                shared = first == 0

                def step(j, k, g=True, h=True, d=True):
                    if g:
                        h_mult(j, (first + k) % 2)
                    if h:
                        hT_copy(j - 1)
                    if d and shared:
                        shared_y(j - 2)

                step(first, 0, h=False, d=False)
                step(first + 1, 1, d=False)
                rounds = (n - 2) // 2
                with dve.Fori(0, rounds) as r:
                    for o in range(2):
                        step(r * 2 + (first + 2 + o), 2 + o)
                for k in range(2 + 2 * rounds, n + 2):
                    step(first + k, k, g=k < n, h=k - 1 < n)

            run(0, NT)
            run(NT, NB)

            for t in range(NT):
                rows = P if t < NT - 1 else LAST
                at = slice(t * D, (t + 1) * D)
                dve.wait_ge(gathered[t % 3], 32 * (t // 3 + 1))
                g = gath[t % 3]
                link(nc.vector.scalar_tensor_tensor(out=acc[0:rows, at], in0=g[0][0:rows, :], scalar=csel[0:rows, t:t + 1],
                                                    in1=acc[0:rows, at], op0=ALU.mult, op1=ALU.add))
                nc.vector.scalar_tensor_tensor(out=acc[0:rows, at], in0=g[1][0:rows, :],
                                               scalar=csel[0:rows, NT + t:NT + t + 1],
                                               in1=acc[0:rows, at], op0=ALU.mult, op1=ALU.add).then_inc(tile_out, 1)


def kernel(**inputs):
    import concourse.bacc as bacc
    from concourse.bass_utils import run_bass_kernel_spmd

    x = np.asarray(inputs["x"])
    patches = x.reshape(B, C, HP, PS, HP, PS).transpose(0, 2, 4, 3, 5, 1).reshape(B * NPATCH, PD)
    cols = [np.asarray(inputs[n]).reshape(PDC, P).T for n in ("L0_tok_ln1_g", "L0_tok_ln1_b")]
    arrays = {
        "patches": patches, "ln1gb": np.concatenate(cols, axis=1), "txt": inputs["txt"],
        "cls_token": np.asarray(inputs["L0_tok_cls_token"]).reshape(1, D),
        "cls_pos": np.asarray(inputs["L0_tok_cls_pos_embedding"]).reshape(1, D),
        "W": inputs["L0_tok_W"],
        "bias": np.asarray(inputs["L0_tok_bias"]).reshape(1, D),
        "ln2_g": np.asarray(inputs["L0_tok_ln2_g"]).reshape(1, D),
        "ln2_b": np.asarray(inputs["L0_tok_ln2_b"]).reshape(1, D),
        "wqT": np.asarray(inputs["L0_attn_wq"]).T, "wkT": np.asarray(inputs["L0_attn_wk"]).T,
        "wvT": np.asarray(inputs["L0_attn_wv"]).T, "woT": np.asarray(inputs["L0_attn_wo"]).T,
        "gateT": np.asarray(inputs["L0_ffn_gate_w"]).T,
        "beta": np.asarray(inputs["L0_ffn_beta"]).reshape(1, E),
        "gate_w": inputs["L0_ffn_gate_proj_w"], "up_w": inputs["L0_ffn_up_proj_w"],
        "down_w": inputs["L0_ffn_down_proj_w"], "sgate_w": inputs["L0_ffn_shared_gate_w"],
        "sup_w": inputs["L0_ffn_shared_up_w"], "sdown_w": inputs["L0_ffn_shared_down_w"],
        **shape_constants(),
    }
    arrays = {n: np.ascontiguousarray(v) for n, v in arrays.items()}
    nc = bacc.Bacc("TRN2", target_bir_lowering=False, num_devices=1)
    aps = {n: nc.dram_tensor(f"in_{n}", v.shape, mybir.dt.from_np(v.dtype), kind="ExternalInput").ap()
           for n, v in arrays.items()}
    out = nc.dram_tensor("out", (TOK, D), F32, kind="ExternalOutput").ap()
    build(nc, aps, out)
    r = run_bass_kernel_spmd(nc, [{f"in_{n}": v for n, v in arrays.items()}], core_ids=[0])
    return r.results[0]["out"].reshape(B, S, D)
```

```python
import math
from contextlib import ExitStack

import numpy as np

import concourse.bass as bass
from concourse import mybir

F32 = mybir.dt.float32
BF16 = mybir.dt.bfloat16
F32R = mybir.dt.float32r
I32 = mybir.dt.int32
ALU = mybir.AluOpType
ACT = mybir.ActivationFunctionType
AX_X = mybir.AxisListType.X

P = 128
B = 16
C, IMG, PS = 3, 96, 16
HP = IMG // PS
NPATCH = HP * HP
PD = C * PS * PS
PDC = PD // P
TXT = 32
S = 1 + NPATCH + TXT
D = 256
DC = D // P
NH, HD = 16, 16
HPT = P // HD
TOK = B * S
PAIRS = B // 2
NPT = -(-B * NPATCH // P)
PLAST = B * NPATCH - (NPT - 1) * P
EARLY = 2 * P // NPATCH
E, M, K = 8, 512, 2
MC = M // P
NT = -(-TOK // P)
LAST = TOK - (NT - 1) * P
NB = (K * TOK + E * (P - 1)) // P
RW = D + 4
PIECES = 2 * DC
EPS = 1e-5
FAR = -1.0e30
QH = 4
QC = QH * S


def shape_constants():
    f = np.float32
    omega = (np.arange(D // 4, dtype=f) / f(D // 4 - 1)).astype(f)
    omega = (f(1.0) / np.power(f(10000.0), omega)).astype(f)
    yy, xx = np.meshgrid(np.arange(HP), np.arange(HP), indexing="ij")
    y = yy.reshape(-1)[:, None].astype(f) * omega[None]
    x = xx.reshape(-1)[:, None].astype(f) * omega[None]
    pe = np.concatenate((np.sin(x), np.cos(x), np.sin(y), np.cos(y)), axis=1).astype(f)
    pe = np.concatenate([np.tile(pe, (B, 1)), np.zeros((P - PLAST, D), f)])
    pe = pe.reshape(NPT, P, D).transpose(1, 0, 2).reshape(P, NPT * D)
    freqs = (f(1.0) / np.power(f(10000.0), np.arange(0, HD, 2, dtype=f) / f(HD))).astype(f)
    ang = np.arange(S, dtype=f)[:, None] * freqs[None]
    cos = np.repeat(np.cos(ang), 2, axis=1).T
    sin = np.repeat(np.sin(ang), 2, axis=1).T * np.where(np.arange(HD) % 2 == 0, -1, 1)[:, None]
    rope = np.stack([np.tile(t, (HPT, 2 * DC)) for t in (cos, sin)], axis=1).astype(f)
    rope = rope.reshape(P, 2 * DC * 2 * S)
    heads = (np.arange(P)[:, None] // HD == np.arange(HPT)[None]).astype(f)
    ident = np.eye(P, dtype=f)
    causal = np.where(np.arange(S)[None] > np.arange(S)[:, None], FAR, 0.0).astype(f)
    before = (np.arange(P)[:, None] < np.arange(P)[None]).astype(f)
    first = np.tile(E - np.arange(E, dtype=f), NT)
    valid = (np.arange(NT * P) < TOK).astype(f).reshape(NT, P).T
    valid = np.repeat(valid, E, axis=1)
    steps = np.tile(np.arange(NT, dtype=f) * P, E)
    lower = (np.arange(E)[:, None] > np.arange(E)[None]).astype(f).reshape(-1)
    blocks = np.repeat(np.arange(NB, dtype=f), E)
    rows = np.concatenate([first, steps, lower, blocks])
    token = np.arange(P)[:, None] + P * np.arange(NT)[None]
    unused = TOK + np.arange(P)[:, None]
    route = np.concatenate([np.tile(rows, (P, 1)), valid, token, unused], axis=1).astype(f)
    return {"c_pe": pe.astype(f), "c_rope": rope, "c_heads": heads, "c_ident": ident,
            "c_causal": causal, "c_before": before, "c_route": route}


class Chain:

    def __init__(self, eng, sem):
        self.eng, self.sem, self.base, self.n = eng, sem, 0, 0

    def enter(self, round_, per):
        self.start, self.per = self.n, per
        self.base = round_ * per

    def leave(self, rounds):
        assert self.n - self.start == self.per, (self.n - self.start, self.per)
        self.n = self.start + rounds * self.per
        self.base = 0

    def __call__(self, ins):
        ins.then_inc(self.sem, 1)
        self.n += 1
        self.eng.wait_ge(self.sem, self.base + self.n)


def build(nc, a, out):
    ctx = ExitStack()
    with ctx:
        def sb(name, shape, dt=F32):
            return ctx.enter_context(nc.sbuf_tensor(name, shape, dt))

        def sem(name):
            return ctx.enter_context(nc.semaphore(name))

        def sems(name, n):
            return [sem(f"{name}{i}") for i in range(n)]

        patches_d = nc.dram_tensor("patches_d", [B * NPATCH, D], F32).ap()
        rows_d = nc.dram_tensor("rows_d", [NB * P, RW], F32).ap()
        h1_d = nc.dram_tensor("h1_d", [TOK, D], F32).ap()

        wqk = sb("wqk", [P, DC * 2 * D])
        wv = sb("wv", [P, DC * D])
        wo = sb("wo", [P, DC * D])
        wgate = sb("wgate", [P, DC * E])
        wgu = sb("wgu", [P, (E + 1) * DC * 2 * M])
        wdn = sb("wdn", [P, (E + 1) * MC * D])
        ln1gb = sb("ln1gb", [P, 2 * PDC])
        rope = sb("rope", [P, 2 * 2 * DC * S])
        heads = sb("heads", [P, HPT])
        ident = sb("ident", [P, P])
        identb = sb("identb", [P, P], BF16)
        causalb = sb("causalb", [S, S], BF16)
        beforeb = sb("beforeb", [P, P], BF16)
        onesb = sb("onesb", [P, P], BF16)
        empty = sb("empty", [P, RW])
        TE = NT * E
        NR = 2 * TE + E * E + NB * E
        route = sb("route", [P, NR + TE + NT + 1])
        beta = sb("beta", [P, E])
        stats = sb("stats", [P, 12])
        stats_all = sb("stats_all", [P, 6 * B])
        mv = sb("mv", [P, 2 * 2])
        dev = sb("dev", [P, 2])
        rstd = sb("rstd", [P, 2])
        mv_all = sb("mv_all", [P, 2 * B])
        minus_half = sb("minus_half", [P, 1])
        mean_t = sb("mean_t", [P, NT])
        var_t = sb("var_t", [P, NT])
        rstd_t = sb("rstd_t", [P, NT])
        dev_all = sb("dev_all", [P, B])
        rstd_all = sb("rstd_all", [P, B])
        eps = sb("eps", [P, 1])
        mx = sb("mx", [S, NH])
        rs = sb("rs", [S, NH])
        m12z = sb("m12z", [P, 2 * TE - E], BF16)
        m12 = m12z[:, TE - E:]
        rsm = sb("rsm", [P, 6 * NT])
        nb = sb("nb", [P, 4 * E])
        eidf = sb("eidf", [P, NB])
        eid = sb("eid", [P, NB], I32)
        slot = [sb(f"slot{i}", [P, NT], I32) for i in range(K)]
        csel = sb("csel", [P, K * NT])
        recip_e = sb("recip_e", [P, 1])
        tok = sb("tok", [P, NB], I32)
        tokj = [sb(f"tokj{i}", [P, 1], I32) for i in range(2)]
        cblk = sb("cblk", [P, NB])
        stream = sb("stream", [P, B * D])
        h_all = stream[0:S, :]
        acc = stream[:, 0:NT * D]

        class Arena:

            def __init__(self, name, words):
                self.whole, self.words, self.at = sb(name, [P, words]), words, 0

            def take(self, rows, words):
                part = self.whole[0:rows, self.at:self.at + words]
                self.at += words
                assert self.at <= self.words
                return part

            def again(self):
                self.at = 0

        early = Arena("early", 2 * D + 7 * DC * 2 * S + 2 * 2 * NH * (HD + 1) + D + DC * S + NT * D + D)
        xn = [early.take(P, PD) for _ in range(2)]
        wpatch = early.take(P, PDC * D)
        pe = early.take(P, NPT * D)
        xnT = [early.take(P, PDC * P) for _ in range(2)]
        ln1b = xnT[1]
        yt = [early.take(P, D) for _ in range(2)]
        early.again()
        n_t = early.take(S, 2 * D)
        W2 = DC * 2 * S
        nT, qc, kc, qs, ks, qr, kr = (early.take(P, W2) for _ in range(7))
        VW = 2 * NH * (HD + 1)
        v_sb = early.take(S, 2 * VW)
        on = early.take(S, D)
        oT = early.take(P, DC * S)
        mT_all = early.take(P, NT * D)
        mc = early.take(P, D)
        after = NT * D
        lg, rt, wide, tags = (stream[:, after + a:after + b] for a, b in (
            (0, TE), (TE, 7 * TE), (7 * TE, 7 * TE + NB * E), (7 * TE + NB * E, 7 * TE + NB * (E + 4))))
        w_hi, w_lo = (sb(n, [P, PIECES * M], F32R) for n in ("w_hi", "w_lo"))
        x_hi, x_lo = (sb(n, [P, D], F32R) for n in ("x_hi", "x_lo"))

        late = Arena("late", max(DC * HPT * 2 * S + 3 * NH * S, NT * RW + 5 * D + 4 * M, NPT * PD + 5 * D))
        xp = late.take(P, NPT * PD)
        cls = late.take(1, 2 * D)
        rowp = late.take(P, 3 * D)
        late.again()
        kbd = late.take(P, DC * HPT * 2 * S)
        prob = [late.take(S, NH * S) for _ in range(2)]
        probT = late.take(S, NH * S)
        late.again()
        m_all = late.take(P, NT * RW)
        sg = [late.take(P, M)]
        xin = [late.take(P, D) for _ in range(2)]
        sg.append(late.take(P, M))
        hb = [late.take(P, M), stream[:, after + 7 * TE + NB * (E + 4):][:, 0:M]]
        hT = late.take(P, M)
        yb = [late.take(P, D) for _ in range(2)]

        ps = ctx.enter_context(nc.psum_tensor("ps", [P, 8, 512], F32))

        s_c = sem("const_in")
        s_cb = sem("bf16_const_in")
        s_w1 = sem("patch_weights_in")
        s_w2 = sem("attn_weights_in")
        s_w3 = sem("ffn_weights_in")
        s_shared = sem("shared_weights_in")
        s_cls = sem("cls_in")
        s_clsadd = sem("cls_added")
        s_txt = sem("txt_in")
        s_const = sem("const_made")
        s_zero = sem("zero_made")
        eps_made = sem("eps_made")
        s_table = sem("table_loaded")
        s_rows0 = sem("rows_cleared")
        xp_in = sems("xp_in", NPT)
        x_normed = sem("x_normed")
        patch_T = sem("patch_T")
        affine_done = sem("affine_done")
        patch_mm = sem("patch_mm")
        patch_read = sem("patch_read")
        patch_out = sem("patch_out")
        y_normed = sem("y_normed")
        pe_made = sem("pe_made")
        patch_stored = sems("patch_stored", 2)
        h_in = sems("h_in", 2)
        n_ready = sem("n_ready")
        nT_psum = sem("nT_psum")
        nT_ready = sem("nT_ready")
        qk_done = sem("qk_done")
        rope_in = sem("rope_in")
        qk_ready = sem("qk_ready")
        kr_ready = sem("kr_ready")
        kbd1_ready = sem("kbd1_ready")
        scores_done = sem("scores_done")
        shifted = sem("shifted")
        exp_done = sem("exp_done")
        probT_psum = sem("probT_psum")
        probT_ready = sem("probT_ready")
        v_done = sem("v_done")
        v_ready = sem("v_ready")
        pv_done = sem("pv_done")
        o_normed = sem("o_normed")
        oT_psum = sem("oT_psum")
        oT_ready = sem("oT_ready")
        wo_done = sem("wo_done")
        resid_done = sem("resid_done")
        moved = sem("moved")
        deviated = sem("deviated")
        image_moved = sem("image_moved")
        image_rstd = sem("image_rstd")
        h1_stored = sem("h1_stored")
        h1_in = sem("h1_in")
        centred = sem("centred")
        mT_psum = sem("mT_psum")
        mT_ready = sem("mT_ready")
        tile_moved = sem("tile_moved")
        tile_rstd = sem("tile_rstd")
        m_ready = sem("m_ready")
        logits_done = sem("logits_done")
        chosen = sem("chosen")
        ranked = sem("ranked")
        picked = sem("picked")
        c_ready = sem("c_ready")
        slots_ready = sem("slots_ready")
        experts_known = sem("experts_known")
        scattered = sem("scattered")
        x_in = sems("x_in", 2)
        xT_psum = sem("xT_psum")
        w_hi_ready = sem("w_hi_ready")
        w_lo_ready = sem("w_lo_ready")
        x_hi_ready = sem("x_hi_ready")
        x_lo_ready = sem("x_lo_ready")
        g_done = sem("g_done")
        u_done = sem("u_done")
        silu_done = sem("silu_done")
        h_ready = sem("h_ready")
        hT_psum = sem("hT_psum")
        hT_ready = sem("hT_ready")
        d_done = sem("d_done")
        y_ready = sem("y_ready")
        y_added = sem("y_added")
        tokens_set = sem("tokens_set")
        tags_in = sem("tags_in")
        weighed = sem("weighed")
        rows_tagged = sem("rows_tagged")
        ln1b_ready = sem("ln1b_ready")
        ln1b_done = sem("ln1b_done")
        gained = sem("gained")
        out_stored = sem("out_stored")
        dve_step = sem("dve_step")
        pool_step = sem("pool_step")

        def bc(ap, shape):
            return ap.broadcast_to(shape)

        ps_s = ps[0:S, 0:4, 0:QC].rearrange("p b (h k) -> p b h k", k=S)
        ps_pt = [ps[:, 4 + i, 0:QC] for i in range(2)]
        ps_oT = ps[:, 7, VW // 2:VW // 2 + DC * S]
        ps_q = ps[:, 4, 0:DC * 2 * S]
        ps_k = ps[:, 5, 0:DC * 2 * S]
        ps_nT = ps[:, 6, 0:DC * 2 * S]
        ps_o = ps[0:S, 7, 0:NH * (HD + 1)]
        ps_wo = ps[0:S, 6, 0:D]
        ps_v = ps[0:S, 6, 0:2 * D]

        var_all = mv_all[:, :].rearrange("p (i k) -> p i k", k=2)[:, :, 1]
        GROUPS = ((0, 4), (4, B))

        def spread_keys(engine, t):
            o = kbd[:, t * HPT * 2 * S:(t + 1) * HPT * 2 * S].rearrange("p (h k) -> p h k", h=HPT)
            return engine.tensor_tensor(o, bc(kr[:, t * 2 * S:(t + 1) * 2 * S].unsqueeze(1), [P, HPT, 2 * S]),
                                        bc(heads[:, :].unsqueeze(2), [P, HPT, 2 * S]), ALU.mult)

        def prows(i):
            return PLAST if i == NPT - 1 else P

        def w_piece(e, q):
            return wgu[:, bass.ds(e * (DC * 2 * M) + (q % DC * 2 + q // DC) * M, M)]

        def piece(q):
            return slice(q * M, (q + 1) * M)

        def block_expert(engine, j):
            return engine.value_load(eid[0:1, bass.ds(j - NT, 1)], min_val=0, max_val=E - 1)

        block = ctx.enter_context(nc.Block())

        @block.sync
        def _(sp):
            for i in range(NPT):
                rows = prows(i)
                sp.dma_start(xp[0:rows, i * PD:(i + 1) * PD], a["patches"][i * P:i * P + rows, :]).then_inc(xp_in[i], 16)
                if i == 0:
                    sp.dma_start(ln1gb[:, :], a["ln1gb"]).then_inc(s_w1, 16)
                    sp.dma_start(ident[:, :], a["c_ident"]).then_inc(s_w1, 16)
                if i == 1:
                    for k, n in enumerate(("bias", "ln2_g", "ln2_b")):
                        sp.dma_start(rowp[:, k * D:(k + 1) * D], a[n].partition_broadcast(P)).then_inc(s_c, 16)
                    sp.dma_start(pe[:, :], a["c_pe"]).then_inc(s_c, 16)

            gu_v = wgu[:, :].rearrange("p (e c x m) -> p e c x m", e=E + 1, c=DC, x=2)
            dn_v = wdn[:, :].rearrange("p (e c n) -> p e c n", e=E + 1, c=MC)
            FIRST, EACH = 3, 2

            def load_ffn(first, last):
                for i in range(first, last):
                    e, x = (i // 3 - 1) % (E + 1), i % 3
                    src = a[("sgate_w", "sup_w", "sdown_w")[x]][0] if e == E else a[("gate_w", "up_w", "down_w")[x]][e]
                    dst = dn_v[:, e, :, :] if x == 2 else gu_v[:, e, :, x, :]
                    sp.dma_start(dst, src.rearrange("(c p) n -> p c n", p=P)).then_inc(s_shared if e == E else s_w3, 16)

            load_ffn(0, FIRST)
            for i in range(NPT):
                sp.wait_ge(patch_out, i + 1)
                rows = prows(i)
                sp.dma_start(patches_d[i * P:i * P + rows, :], yt[i % 2][0:rows, :]).then_inc(patch_stored[i % 2], 16)
                if i in (1, NPT - 1):
                    part = i // (NPT - 1)
                    for par in range(2):
                        sp.wait_ge(patch_stored[par], 16 * ((i + 2 - par) // 2))
                    b0, b1 = ((0, EARLY), (EARLY, B))[part]
                    sp.dma_start(h_all[1:1 + NPATCH, b0 * D:b1 * D].rearrange("p (b d) -> p b d", b=b1 - b0),
                                 patches_d[b0 * NPATCH:b1 * NPATCH, :].rearrange("(b p) d -> p b d", b=b1 - b0)
                                 ).then_inc(h_in[part], 16)
                load_ffn(FIRST + i * EACH, FIRST + (i + 1) * EACH)

            load_ffn(FIRST + NPT * EACH, 3 * (E + 1))

            def store_h1(n):
                sp.wait_ge(resid_done, n + 1)
                sp.dma_start(h1_d[bass.ds(n * S, S), :], h_all[:, bass.ds(n * D, D)]).then_inc(h1_stored, 16)

            def load_h1(t, images, rows=P):
                sp.wait_ge(h1_stored, images * 16)
                sp.dma_start(acc[0:rows, bass.ds(t * D, D)], h1_d[bass.ds(t * P, rows), :]).then_inc(h1_in, 16)

            store_h1(0)
            store_h1(1)
            load_h1(0, 2)
            with sp.Fori(1, PAIRS - 1) as p:
                for b in range(2):
                    store_h1(p * 2 + b)
                load_h1(p, p * 2 + 2)
            for b in range(2):
                store_h1(B - 2 + b)
                sp.wait_ge(h1_in, 16 * (NT - 2 + b))
                load_h1(NT - 2 + b, B - 1 + b, (P, LAST)[b])

            def load_x(j, par, first=False):
                if not first:
                    sp.wait_ge(xT_psum, j - 1)
                sp.dma_start(xin[par][:, :], rows_d[bass.ds(j * P, P), 0:D]).then_inc(x_in[par], 16)

            def store_tile(t):
                rows = P if t < NT - 1 else LAST
                sp.wait_ge(y_ready, t + 1)
                sp.dma_start(out[t * P:t * P + rows, :], acc[0:rows, t * D:(t + 1) * D]).then_inc(out_stored, 16)

            for t in range(NT - 3):
                store_tile(t)
            sp.wait_ge(scattered, 16 * K * NT)
            load_x(0, 0, True)
            load_x(1, 1, True)
            sp.dma_start(tags.rearrange("p (j w) -> p j w", w=RW - D),
                         rows_d.rearrange("(j p) w -> p j w", p=P)[:, :, D:RW]).then_inc(tags_in, 16)
            load_x(2, 0)
            load_x(3, 1)
            for t in range(NT - 3, NT):
                store_tile(t)
            rounds = (NB - 4) // 2
            with sp.Fori(0, rounds) as r:
                for o in range(2):
                    load_x(r * 2 + (4 + o), o)
            for j in range(4 + 2 * rounds, NB):
                load_x(j, j % 2)

            sp.wait_ge(out_stored, 16 * NT)
            sp.wait_ge(y_added, 16 * NB)

        @block.gpsimd
        def _(pool):
            link = Chain(pool, pool_step)
            pool.dma_start(identb[:, :], a["c_ident"]).then_inc(s_cb, 16)
            pool.dma_start(causalb[:, :], a["c_causal"]).then_inc(s_cb, 16)
            pool.dma_start(beforeb[:, :], a["c_before"]).then_inc(s_cb, 16)
            nc.gpsimd.memset(minus_half[:, :], -0.5)
            nc.gpsimd.memset(recip_e[:, :], math.exp(-1.0))
            nc.gpsimd.memset(onesb[:, :], 1.0).then_inc(s_const, 1)
            pool.wait_ge(s_const, 1)

            def rope_pool(p, first=False):
                pool.wait_ge(rope_in, p + 1)
                nc.gpsimd.tensor_tensor(ks[:, :], ks[:, :], rope[:, W2:2 * W2], ALU.mult)
                link(nc.gpsimd.tensor_tensor(qs[:, :], qs[:, :], rope[:, W2:2 * W2], ALU.mult))
                if not first:
                    pool.wait_ge(kbd1_ready, p)
                nc.gpsimd.tensor_tensor(kr[:, :], kc[:, :], ks[:, :], ALU.add).then_inc(kr_ready, 1)
                pool.wait_ge(kr_ready, p + 1)
                if not first:
                    pool.wait_ge(scores_done, p * 2)
                nc.gpsimd.tensor_tensor(qr[:, :], qc[:, :], qs[:, :], ALU.add)
                spread_keys(nc.gpsimd, 0).then_inc(qk_ready, 1)

            pool.wait_ge(pe_made, 1)

            def patch_end(i, par, rows=P):
                pool.wait_ge(y_normed, i + 1)
                y = yt[par][0:rows, :]
                link(nc.gpsimd.tensor_tensor(y, y, rowp[0:rows, D:2 * D], ALU.mult))
                nc.gpsimd.tensor_tensor(y, y, pe[0:rows, i * D:(i + 1) * D], ALU.add).then_inc(patch_out, 1)

            def rstd_of_images(g):
                b0, b1 = GROUPS[g]
                pool.wait_ge(image_moved, g + 1)
                link(nc.gpsimd.tensor_scalar(dev_all[0:S, b0:b1], var_all[0:S, b0:b1], EPS, None, ALU.add))
                nc.gpsimd.tensor_tensor(rstd_all[0:S, b0:b1], dev_all[0:S, b0:b1],
                                        bc(minus_half[0:S, :], [S, b1 - b0]), ALU.pow).then_inc(image_rstd, 1)

            for i in range(NPT - 1):
                patch_end(i, i % 2)
                if i == NPT - 3:
                    rstd_of_images(0)
            patch_end(NPT - 1, (NPT - 1) % 2, PLAST)
            nc.gpsimd.memset(v_sb[:, :], 1.0).then_inc(s_const, 1)
            pool.wait_ge(s_w2, 16 * 9)
            rope_pool(0, True)

            def rstd_of_tile(t):
                pool.wait_ge(tile_moved, t + 1)
                nc.gpsimd.tensor_tensor(rstd_t[:, bass.ds(t, 1)], var_t[:, bass.ds(t, 1)], minus_half[:, :],
                                        ALU.pow).then_inc(tile_rstd, 1)

            rstd_of_images(1)
            rope_pool(1)
            rope_pool(2)
            with pool.Fori(3, PAIRS) as p:
                link.enter(p - 3, 1)
                rope_pool(p)
                rstd_of_tile(p - 3)
                link.leave(PAIRS - 3)
            for t in range(PAIRS - 3, NT - 2):
                rstd_of_tile(t)

            def m_of_tile(t, rows=P):
                nc.gpsimd.tensor_scalar(m_all[0:rows, t * RW:t * RW + D], acc[0:rows, t * D:(t + 1) * D],
                                        mean_t[0:rows, t:t + 1], rstd_t[0:rows, t:t + 1], ALU.subtract, ALU.mult).then_inc(m_ready, 1)

            pool.wait_ge(probT_psum, 4 * B)
            pool.wait_ge(pv_done, 4 * B)
            pool.wait_ge(tile_rstd, NT - 2)
            for t in range(NT - 2):
                m_of_tile(t)
            for t in (NT - 2, NT - 1):
                rstd_of_tile(t)
            pool.wait_ge(tile_rstd, NT)
            m_of_tile(NT - 2)
            m_of_tile(NT - 1, LAST)

            pool.wait_ge(picked, 1)
            link(nc.gpsimd.tensor_tensor(csel[:, :], bc(recip_e[:, :], [P, K * NT]), rsm[:, 4 * NT:6 * NT], ALU.pow))
            nc.gpsimd.tensor_scalar(csel[:, :], csel[:, :], 1.0, None, ALU.add).then_inc(c_ready, 1)

            pool.wait_ge(m_ready, NT)
            pool.wait_ge(rows_tagged, 1)
            pool.wait_ge(slots_ready, 1)
            pool.wait_ge(s_rows0, 32)
            for t in range(NT):
                rows = P if t < NT - 1 else LAST
                for k in range(K):
                    nc.gpsimd.indirect_dma_start(
                        out=rows_d, out_offset=bass.IndirectOffsetOnAxis(ap=slot[k][0:rows, t:t + 1], axis=0),
                        in_=m_all[0:rows, t * RW:(t + 1) * RW], in_offset=None).then_inc(scattered, 16)

            def tokens_of(j, par):
                nc.gpsimd.tensor_copy(tokj[par][:, :], tok[:, bass.ds(j, 1)]).then_inc(tokens_set, 1)

            def add_block(j, par, first=False, last=False):
                pool.wait_ge(tokens_set, j + 1)
                pool.wait_ge(y_ready, j + (NT + 1))
                if not first:
                    pool.wait_ge(y_added, j * 16)
                if not last:
                    tokens_of(j + 1, 1 - par)
                nc.gpsimd.indirect_dma_start(
                    out=out, out_offset=bass.IndirectOffsetOnAxis(ap=tokj[par][:, 0:1], axis=0),
                    in_=yb[par][:, :], in_offset=None, compute_op=ALU.add).then_inc(y_added, 16)

            pool.wait_ge(weighed, 1)
            pool.wait_ge(out_stored, 16 * NT)
            tokens_of(0, 0)
            add_block(0, 0, first=True)
            rounds = (NB - 2) // 2
            with pool.Fori(0, rounds) as r:
                for o in (1, 2):
                    add_block(r * 2 + o, o % 2)
            for j in range(1 + 2 * rounds, NB):
                add_block(j, j % 2, last=j == NB - 1)

        @block.scalar
        def _(act):
            act.dma_start(wpatch.rearrange("p (c n) -> p c n", c=PDC),
                          a["W"].rearrange("(c p) n -> p c n", p=P)).then_inc(s_w1, 16)
            act.dma_start(cls[0:1, 0:D], a["cls_token"]).then_inc(s_cls, 16)
            act.dma_start(cls[0:1, D:2 * D], a["cls_pos"]).then_inc(s_cls, 16)
            act.dma_start(h_all[1 + NPATCH:S, :].rearrange("p (b d) -> p b d", b=B),
                          a["txt"].rearrange("b p d -> p b d")).then_inc(s_txt, 16)
            def deviation(count):
                act.wait_ge(moved, count)
                nc.scalar.activation(dev[:, :], mv[:, :].rearrange("p (i k) -> p i k", k=2)[:, :, 1], ACT.Sqrt,
                                     bias=eps[:, :]).then_inc(deviated, 1)

            def xnT_copy(i, par, first=False):
                act.wait_ge(patch_T, i + 1)
                if not first:
                    act.wait_ge(patch_mm, i - 1)
                nc.scalar.activation(xnT[par].rearrange("p (b n) -> p b n", b=2), ps[:, 0:2, 0:3 * P],
                                     ACT.Copy).then_inc(affine_done, 1)

            act.wait_ge(eps_made, 1)
            nc.scalar.activation(dev[0:1, 0:1], eps[0:1, :], ACT.Sqrt).then_inc(s_table, 1)
            act.wait_ge(s_table, 1)
            deviation(1)
            xnT_copy(0, 0, True)
            xnT_copy(1, 1, True)
            act.dma_start(rope[:, :], a["c_rope"]).then_inc(s_w2, 16)
            act.dma_start(heads[:, :], a["c_heads"]).then_inc(s_w2, 16)
            for i, n in enumerate(("wqT", "wkT")):
                act.dma_start(wqk[:, :].rearrange("p (c x n) -> p c x n", c=DC, x=2)[:, :, i, :],
                              a[n].rearrange("(c p) n -> p c n", p=P)).then_inc(s_w2, 16)
            for w, n in ((wv, "wvT"), (wo, "woT"), (wgate, "gateT")):
                act.dma_start(w[:, :].rearrange("p (c n) -> p c n", c=DC),
                              a[n].rearrange("(c p) n -> p c n", p=P)).then_inc(s_w2, 16)
            act.dma_start(route[:, :], a["c_route"]).then_inc(s_w2, 16)
            act.dma_start(beta[:, :], a["beta"].partition_broadcast(P)).then_inc(s_w2, 16)
            act.wait_ge(s_clsadd, 1)
            act.dma_start(h_all[0:1, :].rearrange("p (b d) -> p b d", b=B),
                          bc(cls[0:1, 0:D].unsqueeze(1), [1, B, D])).then_inc(s_txt, 16)
            for i in range(NPT):
                deviation(i + 2)
                if i + 2 < NPT:
                    xnT_copy(i + 2, i % 2)

            def rows_hi(j, shared):
                act.wait_ge(u_done, j)
                if shared:
                    src = mT_all[:, bass.ds(j * D, D)]
                else:
                    act.wait_ge(xT_psum, j - (NT - 1))
                    src = ps[:, 4, 0:D]
                nc.scalar.activation(x_hi[:, :], src, ACT.Copy).then_inc(x_hi_ready, 1)

            def weights_hi(e, pieces):
                for q in pieces:
                    nc.scalar.activation(w_hi[:, piece(q)], w_piece(e, q), ACT.Copy).then_inc(w_hi_ready, 1)

            def nT_copy(p, first=False):
                act.wait_ge(nT_psum, p + 1)
                if not first:
                    act.wait_ge(v_done, p)
                nc.scalar.activation(nT[:, :], ps_nT, ACT.Copy).then_inc(nT_ready, 1)

            def v_copy(p, parity, first=False):
                act.wait_ge(v_done, p + 1)
                if not first:
                    act.wait_ge(pv_done, (p - 1) * 8)
                dst = v_sb[:, bass.ds(parity * VW, VW)].rearrange("p (b h d) -> p b h d", b=2, d=HD + 1)
                for b in range(2):
                    ins = nc.scalar.activation(dst[:, b, :, 0:HD],
                                               ps_v[:, b * D:(b + 1) * D].rearrange("p (h d) -> p h d", h=NH), ACT.Copy)
                ins.then_inc(v_ready, 1)

            def expo(n, b):
                act.wait_ge(shifted, n + 1)
                nc.scalar.activation(prob[b][:, :], prob[b][:, :], ACT.Exp, scale=HD ** -0.5).then_inc(exp_done, 1)

            def probT_copies(n, first=False):
                for k in range(4):
                    act.wait_ge(probT_psum, n * 4 + (k + 1))
                    if not first:
                        act.wait_ge(pv_done, n * 4 + k - 3)
                    nc.scalar.activation(probT[:, k * QC:(k + 1) * QC], ps_pt[k % 2][0:S, :],
                                         ACT.Copy).then_inc(probT_ready, 1)

            def oT_copy(n, first=False):
                act.wait_ge(oT_psum, n + 1)
                if not first:
                    act.wait_ge(wo_done, n)
                nc.scalar.activation(oT[:, :], ps_oT, ACT.Copy).then_inc(oT_ready, 1)

            def slot_even(p, parity, before=True, following=True):
                n = p * 2
                if before:
                    probT_copies(n - 1)
                if following:
                    nT_copy(p + 1)
                expo(n, 0)
                if before:
                    oT_copy(n - 1)

            def mT_copy(t):
                act.wait_ge(mT_psum, t + 1)
                nc.scalar.activation(mT_all[:, bass.ds(t * D, D)], ps[:, 4, 0:D], ACT.Copy).then_inc(mT_ready, 1)

            def slot_odd(p, parity, first=False, following=True, tile=True):
                n = p * 2 + 1
                probT_copies(n - 1, first)
                expo(n, 1)
                if tile:
                    mT_copy(p - 2)
                if following:
                    v_copy(p + 1, parity, first)
                oT_copy(n - 1, first)

            nT_copy(0, True)
            act.wait_ge(s_const, 2)
            v_copy(0, 0, True)
            slot_even(0, 0, before=False)
            act.wait_ge(s_zero, 1)
            act.dma_start(rows_d.rearrange("(j p) d -> p j d", p=P),
                          bc(empty[:, :].unsqueeze(1), [P, NB, RW])).then_inc(s_rows0, 16)
            act.dma_start(out[TOK:TOK + P, :], empty[:, 0:D]).then_inc(s_rows0, 16)
            slot_odd(0, 1, first=True, tile=False)
            act.wait_ge(s_shared, 16 * 3)
            weights_hi(E, range(PIECES))
            slot_even(1, None)
            slot_odd(1, 0, tile=False)
            with act.Fori(2, PAIRS - 1) as p:
                slot_even(p, None)
                slot_odd(p, (p + 1) % 2)
            rows_hi(0, True)
            slot_even(PAIRS - 1, None, following=False)
            def silu(j, par, first, shared):
                act.wait_ge(g_done, j + 1)
                if not first:
                    act.wait_ge(h_ready, j - 1)
                if shared:
                    act.wait_ge(tile_rstd, j + 1)
                scale = rstd_t[:, bass.ds(j, 1)] if shared else 1.0
                nc.scalar.activation(sg[par][:, :], ps[:, 2 * par, :], ACT.Silu, scale=scale).then_inc(silu_done, 1)

            def y_copy(j, par, first):
                act.wait_ge(d_done, j + 1)
                if not first:
                    act.wait_ge(y_added, (j - (NT + 1)) * 16)
                nc.scalar.activation(yb[par][:, :], ps[:, 6, 0:D], ACT.Copy,
                                     scale=cblk[:, bass.ds(j - NT, 1)]).then_inc(y_ready, 1)

            probT_copies(B - 2)
            expo(B - 1, 1)
            mT_copy(NT - 4)
            oT_copy(B - 2)
            rows_hi(1, True)
            probT_copies(B - 1)
            mT_copy(NT - 3)
            silu(0, 0, True, True)
            oT_copy(B - 1)
            silu(1, 1, True, True)
            rows_hi(2, True)
            silu(2, 0, False, True)
            rows_hi(3, True)
            mT_copy(NT - 2)
            mT_copy(NT - 1)

            def run(first, n):
                shared = first == 0

                def step(j, k, t=True, g=True, d=True):
                    if t and not shared:
                        e = block_expert(act, j + 1)
                        act.wait_ge(g_done, j + 1)
                        weights_hi(e, (0, 1))
                    if g:
                        silu(j, (first + k) % 2, shared and k < 2, shared)
                    if t:
                        rows_hi(j + 1, shared)
                    if t and not shared:
                        weights_hi(e, (2, 3))
                    if d and not shared:
                        y_copy(j - 2, k % 2, k < 4)

                if shared:
                    step(3, 3, d=False)
                else:
                    act.wait_ge(experts_known, 1)
                    act.wait_ge(u_done, first)
                    weights_hi(block_expert(act, first), range(PIECES))
                    rows_hi(first, shared)
                    for k in range(4):
                        if k == 2:
                            act.wait_ge(weighed, 1)
                        step(first + k, k, d=k >= 2)
                rounds = (n - 5) // 2
                with act.Fori(0, rounds) as r:
                    for o in range(2):
                        step(r * 2 + (first + 4 + o), 4 + o)
                for k in range(4 + 2 * rounds, n + 2):
                    step(first + k, k, t=k + 1 < n, g=k < n)

            run(0, NT)
            run(NT, NB)

        @block.tensor
        def _(pe_):
            def patch_transpose(i, par, first=False):
                rows = prows(i)
                pe_.wait_ge(x_normed, i + 1)
                if not first:
                    pe_.wait_ge(affine_done, i)
                for c in range(PDC):
                    ins = nc.tensor.transpose(ps[:, c // 3, (c % 3) * P:(c % 3) * P + rows],
                                              xn[par][0:rows, c * P:(c + 1) * P], ident[0:rows, 0:rows])
                ins.then_inc(patch_T, 1)

            def patch_product(i, par, first=False):
                pe_.wait_ge(affine_done, i + 1)
                if not first:
                    pe_.wait_ge(patch_read, i)
                for c in range(PDC):
                    ins = nc.tensor.matmul(ps[0:prows(i), 2, 0:D], xnT[par][:, c * P:c * P + prows(i)],
                                           wpatch[:, c * D:(c + 1) * D], start=(c == 0), stop=(c == PDC - 1))
                ins.then_inc(patch_mm, 1)

            pe_.wait_ge(s_w1, 16 * 3)
            pe_.wait_ge(ln1b_ready, 1)
            for c in range(PDC):
                ins = nc.tensor.matmul(ps[0:P, 3, 0:D], ln1b[:, c * P:(c + 1) * P], wpatch[:, c * D:(c + 1) * D],
                                       start=(c == 0), stop=(c == PDC - 1))
            ins.then_inc(ln1b_done, 1)
            patch_transpose(0, 0, True)
            patch_transpose(1, 1)
            pe_.wait_ge(gained, 1)
            patch_product(0, 0, True)
            for i in range(1, NPT):
                patch_product(i, i % 2)
                if i + 1 < NPT:
                    patch_transpose(i + 1, (i + 1) % 2)

            def nT_of(p, free=None):
                pe_.wait_ge(n_ready, p * 2 + 2)
                if free is not None:
                    pe_.wait_ge(resid_done, free)
                for b in range(2):
                    for c in range(DC):
                        ins = nc.tensor.transpose(ps_nT[:, (c * 2 + b) * S:(c * 2 + b + 1) * S],
                                                  n_t[:, b * D + c * P:b * D + (c + 1) * P], ident[0:S, 0:S])
                ins.then_inc(nT_psum, 1)

            def qk_of(p, parts=(0, 1)):
                pe_.wait_ge(nT_ready, p + 1)
                for x in parts:
                    dst = (ps_q, ps_k)[x]
                    for t in range(DC):
                        for c in range(DC):
                            ins = nc.tensor.matmul(dst[:, t * 2 * S:(t + 1) * 2 * S],
                                                   wqk[:, c * 2 * D + x * D + t * P:c * 2 * D + x * D + (t + 1) * P],
                                                   nT[:, c * 2 * S:(c + 1) * 2 * S], start=(c == 0), stop=(c == DC - 1))
                if 1 in parts:
                    ins.then_inc(qk_done, 1)

            def v_of(p, free=None):
                if free is not None:
                    pe_.wait_ge(resid_done, free)
                for b in range(2):
                    for c in range(DC):
                        ins = nc.tensor.matmul(ps_v[:, b * D:(b + 1) * D], nT[:, (c * 2 + b) * S:(c * 2 + b + 1) * S],
                                               wv[:, c * D:(c + 1) * D], start=(c == 0), stop=(c == DC - 1))
                ins.then_inc(v_done, 1)

            def scores(p, b, first=False):
                n = p * 2 + b
                pe_.wait_ge(qk_ready, p + 1)
                pe_.wait_ge(kbd1_ready, p + 1)
                if not first:
                    pe_.wait_ge(shifted, n)
                kv = kbd[:, :].rearrange("p (g h b k) -> p g h b k", g=4, h=QH, b=2)
                for g in range(4):
                    t = g // 2
                    nc.tensor.matmul(ps_s[:, g, :, :], qr[:, (t * 2 + b) * S:(t * 2 + b + 1) * S],
                                     kv[:, g, :, b, :], start=True, stop=False)
                    ins = nc.tensor.matmul(ps_s[:, g, :, :], identb[0:S, 0:S],
                                           bc(causalb[:, :].unsqueeze(1), [S, QH, S]), start=False, stop=True)
                ins.then_inc(scores_done, 1)

            def probT_of(n, b, k, first=False):
                if not first:
                    pe_.wait_ge(probT_ready, n * 4 + k - 1)
                for h in range(QH):
                    ins = nc.tensor.transpose(ps_pt[k % 2][0:S, h * S:(h + 1) * S],
                                              prob[b][:, (k * QH + h) * S:(k * QH + h + 1) * S], ident[0:S, 0:S])
                ins.then_inc(probT_psum, 1)

            def pv_of(n, b, k, parity):
                pe_.wait_ge(probT_ready, n * 4 + k + 1)
                for h in range(k * QH, (k + 1) * QH):
                    at = (b * NH + h) * (HD + 1)
                    ins = nc.tensor.matmul(ps_o[:, h * (HD + 1):(h + 1) * (HD + 1)], probT[:, h * S:(h + 1) * S],
                                           v_sb[:, bass.ds(parity * VW + at, HD + 1)], start=True, stop=True)
                ins.then_inc(pv_done, 1)

            def oT_of(n):
                pe_.wait_ge(o_normed, n + 1)
                for c in range(DC):
                    ins = nc.tensor.transpose(ps_oT[:, c * S:(c + 1) * S], on[:, c * P:(c + 1) * P], ident[0:S, 0:S])
                ins.then_inc(oT_psum, 1)

            def wo_of(n, first=False):
                pe_.wait_ge(oT_ready, n + 1)
                if not first:
                    pe_.wait_ge(resid_done, n)
                for c in range(DC):
                    ins = nc.tensor.matmul(ps_wo, oT[:, c * S:(c + 1) * S], wo[:, c * D:(c + 1) * D],
                                           start=(c == 0), stop=(c == DC - 1))
                ins.then_inc(wo_done, 1)

            def context(n, b, pair, parity, first=False, output=True, out_first=False, nT_next=None):
                pe_.wait_ge(exp_done, n + 1)
                probT_of(n, b, 0, first)
                probT_of(n, b, 1, first)
                pe_.wait_ge(v_ready, pair + 1)
                if output:
                    wo_of(n - 1, out_first)
                if not first:
                    pe_.wait_ge(oT_ready, n)
                pv_of(n, b, 0, parity)
                probT_of(n, b, 2)
                pv_of(n, b, 1, parity)
                probT_of(n, b, 3)
                if nT_next is not None:
                    nT_of(*nT_next)
                pv_of(n, b, 2, parity)
                pv_of(n, b, 3, parity)

            def mT_of(t):
                pe_.wait_ge(centred, t + 1)
                for c in range(DC):
                    ins = nc.tensor.transpose(ps[:, 4, c * P:(c + 1) * P], mc[:, c * P:(c + 1) * P], ident[:, :])
                ins.then_inc(mT_psum, 1)

            def slot_even(p, parity, following=True):
                n = p * 2
                scores(p, 0)
                pe_.wait_ge(v_ready, p + 1)
                context(n - 1, 1, p - 1, parity, nT_next=(p + 1, n - 1) if following else None)
                if following:
                    qk_of(p + 1)
                oT_of(n - 1)

            def slot_odd(p, parity, following=True, first=False, tile=True):
                n = p * 2 + 1
                scores(p, 1)
                if following:
                    pe_.wait_ge(rope_in, p + 2)
                context(n - 1, 0, p, parity, first=first, output=not first)
                if tile:
                    mT_of(p - 2)
                if following:
                    v_of(p + 1, None if first else n - 1)
                oT_of(n - 1)

            pe_.wait_ge(s_w2, 16 * 9)
            pe_.wait_ge(s_cb, 16 * 3)
            nT_of(0)
            qk_of(0)
            v_of(0)
            pe_.wait_ge(v_ready, 1)
            nT_of(1)
            pe_.wait_ge(patch_read, NPT)
            pe_.wait_ge(rope_in, 1)
            qk_of(1, (0,))
            scores(0, 0, True)
            qk_of(1, (1,))
            slot_odd(0, 0, first=True, tile=False)
            slot_even(1, 0)
            slot_odd(1, 1, tile=False)
            with pe_.Fori(2, PAIRS - 1) as p:
                slot_even(p, (p + 1) % 2)
                slot_odd(p, p % 2)
            slot_even(PAIRS - 1, (PAIRS - 2) % 2, following=False)
            ps_lg = ps[:, 7, 0:NT * E]
            ps_rank = ps[:, 7, P:P + TE]
            ps_count = ps[:, 7, 2 * P:2 * P + E]

            def logits(t):
                pe_.wait_ge(mT_ready, t + 1)
                for c in range(DC):
                    ins = nc.tensor.matmul(ps_lg[:, t * E:(t + 1) * E], mT_all[:, t * D + c * P:t * D + (c + 1) * P],
                                           wgate[:, c * E:(c + 1) * E], start=(c == 0), stop=(c == DC - 1))
                ins.then_inc(logits_done, 1)

            def ranks():
                pe_.wait_ge(chosen, 1)
                nc.tensor.matmul(ps_rank, beforeb[:, :], m12[:, :], start=True, stop=False)
                for s in range(1, NT):
                    nc.tensor.matmul(ps_rank, onesb[:, :], m12z[:, TE - (s + 1) * E:2 * TE - (s + 1) * E],
                                     start=False, stop=(s == NT - 1))
                for t in range(NT):
                    ins = nc.tensor.matmul(ps_count, onesb[:, :], m12[:, t * E:(t + 1) * E],
                                           start=(t == 0), stop=(t == NT - 1))
                ins.then_inc(ranked, 1)

            def x_transpose(j, par, n_in):
                pe_.wait_ge(x_in[par], n_in)
                pe_.wait_ge(x_lo_ready, j)
                for c in range(DC):
                    ins = nc.tensor.transpose(ps[:, 4, c * P:(c + 1) * P], xin[par][:, c * P:(c + 1) * P], ident[:, :])
                ins.then_inc(xT_psum, 1)

            def gate_up(j, par, shared, first=False, parts=(0, 1)):
                if 0 in parts:
                    pe_.wait_ge(x_lo_ready, j + 1)
                    if not first:
                        pe_.wait_ge(h_ready, j - 1)
                for x in parts:
                    for c in range(DC):
                        q = x * DC + c
                        pe_.wait_ge(w_lo_ready, q + 1 if shared else (j - (NT - 1)) * PIECES + (q + 1))
                        for i, (rows, w) in enumerate(((x_hi, w_hi), (x_lo, w_hi), (x_hi, w_lo))):
                            ins = nc.tensor.matmul(ps[:, 2 * par + x, :], rows[:, c * P:(c + 1) * P], w[:, piece(q)],
                                                   start=(c == 0 and i == 0), stop=(c == DC - 1 and i == 2))
                    ins.then_inc((g_done, u_done)[x], 1)

            def h_transpose(j, par):
                pe_.wait_ge(h_ready, j + 1)
                pe_.wait_ge(hT_ready, j)
                for c in range(MC):
                    ins = nc.tensor.transpose(ps[:, 5, c * P:(c + 1) * P], hb[par][:, c * P:(c + 1) * P], ident[:, :])
                ins.then_inc(hT_psum, 1)

            def down(j, e):
                pe_.wait_ge(hT_ready, j + 1)
                pe_.wait_ge(y_ready, j)
                for c in range(MC):
                    ins = nc.tensor.matmul(ps[:, 6, 0:D], hT[:, c * P:(c + 1) * P],
                                           wdn[:, bass.ds(e * (MC * D) + c * D, D)],
                                           start=(c == 0), stop=(c == MC - 1))
                ins.then_inc(d_done, 1)

            def expert_of(j, first):
                if first == 0:
                    return E
                return block_expert(pe_, j)

            scores(PAIRS - 1, 1)
            context(B - 2, 0, PAIRS - 1, (PAIRS - 1) % 2)
            mT_of(NT - 4)
            pe_.wait_ge(shifted, B)
            pe_.wait_ge(s_shared, 16 * 3)
            pe_.wait_ge(s_w3, 16 * 3 * E)
            gate_up(0, 0, True, True)
            oT_of(B - 2)
            pe_.wait_ge(mT_ready, NT - 3)
            context(B - 1, 1, PAIRS - 1, (PAIRS - 1) % 2)
            mT_of(NT - 3)
            gate_up(1, 1, True, True, (0,))
            oT_of(B - 1)
            gate_up(1, 1, True, True, (1,))
            wo_of(B - 1)
            pe_.wait_ge(oT_ready, B)
            for t in range(NT - 3):
                logits(t)
            h_transpose(0, 0)
            gate_up(2, 0, True)
            logits(NT - 3)
            mT_of(NT - 2)
            h_transpose(1, 1)
            pe_.wait_ge(resid_done, B)
            down(0, E)
            pe_.wait_ge(mT_ready, NT - 1)
            mT_of(NT - 1)
            gate_up(3, 1, True, parts=(0,))
            logits(NT - 2)
            logits(NT - 1)
            gate_up(3, 1, True, parts=(1,))
            h_transpose(2, 0)
            down(1, E)
            gate_up(4, 0, True)
            ranks()
            h_transpose(3, 1)
            down(2, E)

            def run(first, n):
                def x_T(j, k):
                    if first:
                        x_transpose(j, k % 2, (j - (first + k % 2)) * 8 + 16)

                def full(j, k, t=True, g=True, h=True, d=True):
                    if t:
                        x_T(j + 1, k + 1)
                    if g:
                        gate_up(j, (first + k) % 2, first == 0)
                    if h:
                        h_transpose(j - 1, (first + k + 1) % 2)
                    if d:
                        down(j - 2, expert_of(j - 2, first))

                if first == 0:
                    peeled = 5
                else:
                    x_T(first, 0)
                    down(first - 1, E)
                    full(first, 0, h=False, d=False)
                    full(first + 1, 1, d=False)
                    peeled = 2
                rounds = (n - 1 - peeled) // 2
                with pe_.Fori(0, rounds) as r:
                    for o in range(2):
                        full(r * 2 + (first + peeled + o), peeled + o)
                for k in range(peeled + 2 * rounds, n + (2 if first else 1)):
                    full(first + k, k, t=k + 1 < n, g=k < n, h=k - 1 < n)

            run(0, NT)
            pe_.wait_ge(experts_known, 1)
            run(NT, NB)

        @block.vector
        def _(dve):
            link = Chain(dve, dve_step)

            def moments(src, rows, width, st, out_mv):
                half = width // 512 + 1
                w = width // half
                for i in range(half):
                    ins = nc.vector.bn_stats(st[0:rows, 6 * i:6 * i + 6], src[:, i * w:(i + 1) * w])
                link(ins)
                return nc.vector.bn_aggr(out_mv, st[0:rows, 0:6 * half])

            def normed(dst, src, mean, inv):
                return nc.vector.tensor_scalar(dst, src, mean, inv, ALU.subtract, ALU.mult)

            nc.vector.memset(eps[:, :], EPS).then_inc(eps_made, 1)
            nc.vector.memset(m12z[:, 0:TE - E], 0.0)
            link(nc.vector.memset(var_t[:, :], 1.0))
            nc.vector.memset(empty[:, :], 0.0)
            dve.wait_ge(s_w1, 16 * 3)
            nc.vector.tensor_copy(ln1b.rearrange("p (c n) -> p c n", c=PDC),
                                  bc(ln1gb[:, PDC:].unsqueeze(2), [P, PDC, P])).then_inc(ln1b_ready, 1)
            for par in range(2):
                dve.wait_ge(xp_in[par], 16)
                ins = moments(xp[:, par * PD:(par + 1) * PD], P, PD, stats, mv[0:P, 2 * par:2 * par + 2])
                if par == 0:
                    link(ins)
            ins.then_inc(moved, 1)
            dve.wait_ge(deviated, 1)
            link(nc.vector.reciprocal(rstd[:, :], dev[:, :]))
            for par in range(2):
                normed(xn[par], xp[:, par * PD:(par + 1) * PD], mv[0:P, 2 * par:2 * par + 1],
                       rstd[0:P, par:par + 1]).then_inc(x_normed, 1)
            dve.wait_ge(ln1b_done, 1)
            w_v = wpatch.rearrange("p (c n) -> p c n", c=PDC)
            nc.vector.tensor_tensor(w_v, w_v, bc(ln1gb[:, 0:PDC].unsqueeze(2), [P, PDC, D]), ALU.mult).then_inc(gained, 1)
            dve.wait_ge(s_c, 16 * 4)
            link(nc.vector.tensor_tensor(rowp[:, 0:D], rowp[:, 0:D], ps[0:P, 3, 0:D], ALU.add))
            nc.vector.tensor_tensor(pe.rearrange("p (t d) -> p t d", t=NPT), pe.rearrange("p (t d) -> p t d", t=NPT),
                                    bc(rowp[:, 2 * D:3 * D].unsqueeze(1), [P, NPT, D]), ALU.add).then_inc(pe_made, 1)
            dve.wait_ge(s_cls, 32)
            nc.vector.tensor_tensor(cls[0:1, 0:D], cls[0:1, 0:D], cls[0:1, D:2 * D], ALU.add).then_inc(s_clsadd, 1)

            def patch_step(i):
                par, rows, ahead = i % 2, prows(i), i + 2 < NPT
                y = yt[par][0:rows, :]
                if ahead:
                    x_rows = prows(i + 2)
                    dve.wait_ge(xp_in[i + 2], 16)
                    x_in_ = xp[0:x_rows, (i + 2) * PD:(i + 3) * PD]
                    link(moments(x_in_, x_rows, PD, stats, mv[0:x_rows, 2:4]))
                dve.wait_ge(patch_mm, i + 1)
                if i >= 2:
                    dve.wait_ge(patch_stored[par], (i - par) * 8)
                nc.vector.tensor_tensor(y, ps[0:rows, 2, 0:D], rowp[0:rows, 0:D], ALU.add).then_inc(patch_read, 1)
                dve.wait_ge(patch_read, i + 1)
                moments(y, rows, D, stats, mv[0:rows, 0:2]).then_inc(moved, 1)
                dve.wait_ge(deviated, i + 2)
                link(nc.vector.reciprocal(rstd[:, :], dev[:, :]))
                if ahead:
                    normed(xn[par][0:x_rows, :], x_in_, mv[0:x_rows, 2:3], rstd[0:x_rows, 1:2]).then_inc(x_normed, 1)
                normed(y, y, mv[0:rows, 0:1], rstd[0:rows, 0:1]).then_inc(y_normed, 1)

            def image_stats(b0, b1):
                for b in range(b0, b1):
                    ins = nc.vector.bn_stats(stats_all[0:S, 6 * b:6 * b + 6], h_all[:, b * D:(b + 1) * D])
                link(ins)

            def image_moments(g):
                b0, b1 = GROUPS[g]
                for b in range(b0, b1):
                    ins = nc.vector.bn_aggr(mv_all[0:S, 2 * b:2 * b + 2], stats_all[0:S, 6 * b:6 * b + 6])
                ins.then_inc(image_moved, 1)

            for i in range(NPT - 2):
                patch_step(i)
            dve.wait_ge(h_in[0], 16)
            dve.wait_ge(s_txt, 32)
            image_stats(*GROUPS[0])
            image_moments(0)
            patch_step(NPT - 2)
            def ln_pair(p, first=False):
                if not first:
                    dve.wait_ge(nT_psum, p)
                for b in range(2):
                    n = p * 2 + b
                    normed(n_t[:, b * D:(b + 1) * D], h_all[:, bass.ds(n * D, D)], mv_all[0:S, bass.ds(n * 2, 1)],
                           rstd_all[0:S, bass.ds(n, 1)]).then_inc(n_ready, 1)

            dve.wait_ge(patch_T, NPT)
            dve.wait_ge(image_rstd, 1)
            ln_pair(0, True)
            patch_step(NPT - 1)

            def weights_lo(j, e, pieces, shared=False):
                for q in pieces:
                    dve.wait_ge(w_hi_ready, q + 1 if shared else (j - (NT - 1)) * PIECES + (q + 1))
                    nc.vector.tensor_tensor(w_lo[:, piece(q)], w_piece(e, q), w_hi[:, piece(q)],
                                            ALU.subtract).then_inc(w_lo_ready, 1)

            def rows_lo(j, shared):
                dve.wait_ge(x_hi_ready, j + 1)
                src = mT_all[:, bass.ds(j * D, D)] if shared else ps[:, 4, 0:D]
                nc.vector.tensor_tensor(x_lo[:, :], src, x_hi[:, :], ALU.subtract).then_inc(x_lo_ready, 1)

            swap = [i ^ 1 for i in range(32)]

            def rope_dve(p, first=False):
                dve.wait_ge(qk_done, p + 1)
                if not first:
                    dve.wait_ge(qk_ready, p)
                nc.vector.tensor_tensor(qc[:, :], ps_q, rope[:, 0:W2], ALU.mult)
                nc.vector.stream_shuffle(qs[:, :], ps_q, swap)
                nc.vector.tensor_tensor(kc[:, :], ps_k, rope[:, 0:W2], ALU.mult)
                nc.vector.stream_shuffle(ks[:, :], ps_k, swap).then_inc(rope_in, 1)

            mx_v = mx[:, :].rearrange("p (g h) -> p g h", g=4)

            def row_max(n):
                dve.wait_ge(scores_done, n + 1)
                link(nc.vector.tensor_reduce(mx_v, ps_s, AX_X, ALU.max))

            def shift(n, b, first=False):
                if not first:
                    dve.wait_ge(probT_psum, n * 4 - 4)
                nc.vector.tensor_tensor(prob[b][:, :].rearrange("p (g h k) -> p g h k", g=4, h=QH), ps_s,
                                        bc(mx_v.unsqueeze(3), [S, 4, QH, S]), ALU.subtract).then_inc(shifted, 1)

            def spread(p, first=False):
                dve.wait_ge(kr_ready, p + 1)
                if not first:
                    dve.wait_ge(scores_done, p * 2)
                spread_keys(nc.vector, 1).then_inc(kbd1_ready, 1)

            def norm_o(n, first=False):
                dve.wait_ge(pv_done, n * 4 + 4)
                o_v = ps_o.rearrange("p (h d) -> p h d", h=NH)
                link(nc.vector.reciprocal(rs[:, :], o_v[:, :, HD]))
                if not first:
                    dve.wait_ge(oT_psum, n)
                nc.vector.tensor_tensor(on[:, :].rearrange("p (h d) -> p h d", h=NH), o_v[:, :, 0:HD],
                                        bc(rs[:, :].unsqueeze(2), [S, NH, HD]), ALU.mult).then_inc(o_normed, 1)

            def resid(n):
                dve.wait_ge(wo_done, n + 1)
                h = h_all[:, bass.ds(n * D, D)]
                nc.vector.tensor_tensor(h, ps_wo, h, ALU.add).then_inc(resid_done, 1)

            def tile_stats(t, rows=P):
                dve.wait_ge(h1_in, t * 16 + 16)
                link(nc.vector.bn_stats(stats[0:rows, 0:6], acc[0:rows, bass.ds(t * D, D)]))

            def tile_centre(t, rows=P, free=None):
                link(nc.vector.bn_aggr(mv[0:rows, 0:2], stats[0:rows, 0:6]))
                nc.vector.tensor_copy(mean_t[0:rows, bass.ds(t, 1)], mv[0:rows, 0:1])
                nc.vector.tensor_scalar(var_t[0:rows, bass.ds(t, 1)], mv[0:rows, 1:2], EPS, None,
                                        ALU.add).then_inc(tile_moved, 1)
                if free is not None:
                    dve.wait_ge(mT_psum, free)
                if rows < P:
                    link(nc.vector.memset(mc[64:P, :], 0.0))
                nc.vector.tensor_scalar(mc[0:rows, :], acc[0:rows, bass.ds(t * D, D)], mv[0:rows, 0:1], None,
                                        ALU.subtract).then_inc(centred, 1)

            def slot_even(p, following=True, tile=True):
                n = p * 2
                row_max(n)
                resid(n - 2)
                shift(n, 0)
                norm_o(n - 1)
                if tile:
                    tile_stats(p - 2)
                if following:
                    rope_dve(p + 1)
                if tile:
                    tile_centre(p - 2)

            def slot_odd(p, following=True, ln=True, first=False):
                n = p * 2 + 1
                row_max(n)
                if not first:
                    resid(n - 2)
                shift(n, 1, first)
                if following:
                    spread(p + 1)
                norm_o(n - 1, first)
                if ln:
                    ln_pair(p + 2)

            dve.wait_ge(s_w2, 16 * 9)
            nc.vector.tensor_copy(empty[:, D:D + 1], route[:, NR + TE + NT:]).then_inc(s_zero, 1)
            ln_pair(1)
            rope_dve(0, True)
            image_stats(GROUPS[1][0], EARLY)
            spread(0, True)
            dve.wait_ge(h_in[1], 16)
            image_stats(EARLY, B)
            image_moments(1)
            row_max(0)
            shift(0, 0, True)
            rope_dve(1)
            dve.wait_ge(image_rstd, 2)
            slot_odd(0, first=True)
            dve.wait_ge(s_shared, 16 * 3)
            weights_lo(0, E, range(PIECES), shared=True)
            slot_even(1, tile=False)
            slot_odd(1)
            with dve.Fori(2, PAIRS - 2) as p:
                link.enter(p - 2, 6)
                slot_even(p)
                slot_odd(p)
                link.leave(PAIRS - 4)
            slot_even(PAIRS - 2)
            slot_odd(PAIRS - 2, ln=False)
            rows_lo(0, True)
            slot_even(PAIRS - 1, following=False)
            slot_odd(PAIRS - 1, following=False, ln=False)
            r_first, r_steps = route[:, 0:TE], route[:, TE:2 * TE]
            r_lower, r_blocks = route[:, 2 * TE:2 * TE + E * E], route[:, 2 * TE + E * E:NR]
            r_valid = route[:, NR:NR + TE]

            def te(ap):
                return ap.rearrange("p (t e) -> p t e", e=E)

            biased, eq, wt, one, two, tmp = (rt[:, i * TE:(i + 1) * TE] for i in range(6))
            tops = [rsm[:, i * NT:(i + 1) * NT] for i in range(K)]
            m_tags = m_all.rearrange("p (t w) -> p t w", w=RW)[:, :, D:]
            nblk, base, upto, start = (nb[:, i * E:(i + 1) * E] for i in range(4))

            def scaled_logits():
                dve.wait_ge(tile_rstd, NT)
                dve.wait_ge(logits_done, NT)
                link(nc.vector.tensor_tensor(te(lg[:, :]), te(ps[:, 7, 0:TE]),
                                             bc(rstd_t[:, :].unsqueeze(2), [P, NT, E]), ALU.mult))
                link(nc.vector.tensor_tensor(te(biased), te(lg[:, :]), bc(beta[:, :].unsqueeze(1), [P, NT, E]), ALU.add))

            def choose(sel, top, last=False):
                link(nc.vector.tensor_reduce(top, te(biased), AX_X, ALU.max))
                link(nc.vector.tensor_tensor(te(eq), te(biased), bc(top.unsqueeze(2), [P, NT, E]), ALU.is_equal))
                link(nc.vector.tensor_tensor(wt, eq, r_first, ALU.mult))
                link(nc.vector.tensor_reduce(top, te(wt), AX_X, ALU.max))
                link(nc.vector.tensor_tensor(te(sel), te(r_first), bc(top.unsqueeze(2), [P, NT, E]), ALU.is_equal))
                if last:
                    link(nc.vector.tensor_tensor(tmp, one, two, ALU.add))
                    nc.vector.tensor_tensor(m12[:, :], tmp, r_valid, ALU.mult).then_inc(chosen, 1)
                else:
                    link(nc.vector.scalar_tensor_tensor(out=biased, in0=sel, scalar=-3.0e38, in1=biased,
                                                        op0=ALU.mult, op1=ALU.add))

            def expert_blocks():
                dve.wait_ge(ranked, 1)
                en = wide[:, 0:TE].rearrange("p (e s) -> p e s", e=E)
                link(nc.vector.tensor_tensor(en, bc(ps[:, 7, 2 * P:2 * P + E].unsqueeze(2), [P, E, NT]),
                                             r_steps.rearrange("p (e s) -> p e s", e=E), ALU.is_gt))
                link(nc.vector.tensor_reduce(nblk, en, AX_X, ALU.add))
                ee = wide[:, 0:E * E].rearrange("p (e s) -> p e s", e=E)
                link(nc.vector.tensor_tensor(ee, bc(nblk.unsqueeze(1), [P, E, E]),
                                             r_lower.rearrange("p (e s) -> p e s", e=E), ALU.mult))
                link(nc.vector.tensor_reduce(base, ee, AX_X, ALU.add))

            def block_experts():
                link(nc.vector.tensor_tensor(upto, base, nblk, ALU.add))
                be = wide[:, :].rearrange("p (j e) -> p j e", e=E)
                link(nc.vector.tensor_tensor(be, r_blocks.rearrange("p (j e) -> p j e", e=E),
                                             bc(upto.unsqueeze(1), [P, NB, E]), ALU.is_ge))
                link(nc.vector.tensor_reduce(eidf[:, :], be, AX_X, ALU.add))
                nc.vector.tensor_scalar(eid[:, :], eidf[:, :], float(E - 1), None, ALU.min).then_inc(experts_known, 1)

            def token_slots():
                link(nc.vector.tensor_scalar(start, base, float(P), None, ALU.mult))
                link(nc.vector.tensor_tensor(te(wt), te(ps[:, 7, P:P + TE]), bc(start.unsqueeze(1), [P, NT, E]), ALU.add))
                for i, sel in enumerate((one, two)):
                    link(nc.vector.tensor_tensor(tmp, sel, wt, ALU.mult))
                    link(nc.vector.tensor_reduce(rsm[:, (2 + i) * NT:(3 + i) * NT], te(tmp), AX_X, ALU.add))
                nc.vector.tensor_copy(slot[0][:, :], rsm[:, 2 * NT:3 * NT])
                nc.vector.tensor_copy(slot[1][:, :], rsm[:, 3 * NT:4 * NT]).then_inc(slots_ready, 1)

            def chosen_logits():
                dve.wait_ge(chosen, 1)
                for i, sel in enumerate((one, two)):
                    link(nc.vector.tensor_tensor(tmp, sel, lg[:, :], ALU.mult))
                    ins = nc.vector.tensor_reduce(rsm[:, (4 + i) * NT:(5 + i) * NT], te(tmp), AX_X, ALU.add)
                    if i == 0:
                        link(ins)
                ins.then_inc(picked, 1)
                nc.vector.tensor_copy(m_tags[:, :, 0], route[:, NR + TE:NR + TE + NT])
                nc.vector.tensor_copy(m_tags[:, :, 3], tops[0])

            def token_weights():
                dve.wait_ge(c_ready, 1)
                nc.vector.reciprocal(m_tags[:, :, 1:3],
                                     csel[:, :].rearrange("p (k t) -> p t k", k=K)).then_inc(rows_tagged, 1)

            def block_weights():
                dve.wait_ge(tags_in, 16)
                t_v = tags.rearrange("p (j w) -> p w j", w=RW - D)
                is_first, w_first, w_second = (wide[:, i * NB:(i + 1) * NB] for i in range(3))
                nc.vector.tensor_copy(tok[:, :], t_v[:, 0, :])
                link(nc.vector.tensor_scalar(eidf[:, :], eidf[:, :], -1.0, float(E), ALU.mult, ALU.add))
                link(nc.vector.tensor_scalar(eidf[:, :], eidf[:, :], 1.0, None, ALU.max))
                link(nc.vector.tensor_tensor(is_first, t_v[:, 3, :], eidf[:, :], ALU.is_equal))
                nc.vector.tensor_tensor(w_first, t_v[:, 1, :], is_first, ALU.mult)
                link(nc.vector.tensor_tensor(w_second, t_v[:, 2, :], is_first, ALU.mult))
                link(nc.vector.tensor_tensor(w_second, t_v[:, 2, :], w_second, ALU.subtract))
                nc.vector.tensor_tensor(cblk[:, :], w_first, w_second, ALU.add).then_inc(weighed, 1)

            def h_mult(j, par, shared, first=False):
                dve.wait_ge(silu_done, j + 1)
                dve.wait_ge(u_done, j + 1)
                if not first:
                    dve.wait_ge(hT_psum, j - 1)
                if shared:
                    ins = nc.vector.scalar_tensor_tensor(out=hb[par], in0=ps[:, 2 * par + 1, :],
                                                         scalar=rstd_t[:, bass.ds(j, 1)], in1=sg[par][:, :],
                                                         op0=ALU.mult, op1=ALU.mult)
                else:
                    ins = nc.vector.tensor_tensor(hb[par], sg[par][:, :], ps[:, 2 * par + 1, :], ALU.mult)
                ins.then_inc(h_ready, 1)

            def hT_copy(j):
                dve.wait_ge(hT_psum, j + 1)
                dve.wait_ge(d_done, j)
                nc.vector.tensor_copy(hT[:, :], ps[:, 5, :]).then_inc(hT_ready, 1)

            def shared_y(j):
                dve.wait_ge(d_done, j + 1)
                dve.wait_ge(m_ready, j + 1)
                rows = LAST if isinstance(j, int) and j == NT - 1 else P
                at = acc[0:rows, bass.ds(j * D, D)]
                nc.vector.tensor_tensor(at, ps[0:rows, 6, 0:D], at, ALU.add).then_inc(y_ready, 1)

            resid(B - 2)
            tile_stats(NT - 3)
            tile_centre(NT - 3, free=NT - 3)
            rows_lo(1, True)
            norm_o(B - 1)
            h_mult(0, 0, True, True)
            resid(B - 1)
            tile_stats(NT - 2)
            tile_centre(NT - 2, free=NT - 2)
            h_mult(1, 1, True, True)
            rows_lo(2, True)
            hT_copy(0)
            tile_stats(NT - 1, LAST)
            tile_centre(NT - 1, LAST, free=NT - 1)

            def run(first, n):
                shared = first == 0

                def step(j, k, t=True, g=True, h=True, d=True):
                    if t and not shared:
                        e = block_expert(dve, j + 1)
                        weights_lo(j + 1, e, (0, 1))
                    if g:
                        h_mult(j, (first + k) % 2, shared)
                    if t:
                        rows_lo(j + 1, shared)
                    if t and not shared:
                        weights_lo(j + 1, e, (2, 3))
                    if h:
                        hT_copy(j - 1)
                    if d and shared:
                        shared_y(j - 2)

                if shared:
                    step(2, 2)
                    scaled_logits()
                    choose(one, tops[0])
                    h_mult(3, 1, True)
                    rows_lo(4, True)
                    choose(two, tops[1], last=True)
                    hT_copy(2)
                    shared_y(1)
                    chosen_logits()
                    h_mult(4, 0, True)
                    rows_lo(5, True)
                    expert_blocks()
                    token_slots()
                    token_weights()
                    hT_copy(3)
                    shared_y(2)
                    block_experts()
                    peeled = 5
                else:
                    weights_lo(first, block_expert(dve, first), range(PIECES))
                    rows_lo(first, False)
                    block_weights()
                    step(first, 0, h=False, d=False)
                    shared_y(first - 1)
                    step(first + 1, 1, d=False)
                    peeled = 2
                rounds = (n - 1 - peeled) // 2
                with dve.Fori(0, rounds) as r:
                    for o in range(2):
                        step(r * 2 + (first + peeled + o), peeled + o)
                for k in range(peeled + 2 * rounds, n + (1 if shared else 2)):
                    step(first + k, k, t=k + 1 < n, g=k < n, h=k - 1 < n)

            run(0, NT)
            run(NT, NB)


def kernel(**inputs):
    import concourse.bacc as bacc
    from concourse.bass_utils import run_bass_kernel_spmd

    x = np.asarray(inputs["x"])
    patches = x.reshape(B, C, HP, PS, HP, PS).transpose(0, 2, 4, 3, 5, 1).reshape(B * NPATCH, PD)
    cols = [np.asarray(inputs[n]).reshape(PDC, P).T for n in ("L0_tok_ln1_g", "L0_tok_ln1_b")]
    arrays = {
        "patches": patches, "ln1gb": np.concatenate(cols, axis=1), "txt": inputs["txt"],
        "cls_token": np.asarray(inputs["L0_tok_cls_token"]).reshape(1, D),
        "cls_pos": np.asarray(inputs["L0_tok_cls_pos_embedding"]).reshape(1, D),
        "W": inputs["L0_tok_W"],
        "bias": np.asarray(inputs["L0_tok_bias"]).reshape(1, D),
        "ln2_g": np.asarray(inputs["L0_tok_ln2_g"]).reshape(1, D),
        "ln2_b": np.asarray(inputs["L0_tok_ln2_b"]).reshape(1, D),
        "wqT": np.asarray(inputs["L0_attn_wq"]).T, "wkT": np.asarray(inputs["L0_attn_wk"]).T,
        "wvT": np.asarray(inputs["L0_attn_wv"]).T, "woT": np.asarray(inputs["L0_attn_wo"]).T,
        "gateT": np.asarray(inputs["L0_ffn_gate_w"]).T,
        "beta": np.asarray(inputs["L0_ffn_beta"]).reshape(1, E),
        "gate_w": inputs["L0_ffn_gate_proj_w"], "up_w": inputs["L0_ffn_up_proj_w"],
        "down_w": inputs["L0_ffn_down_proj_w"], "sgate_w": inputs["L0_ffn_shared_gate_w"],
        "sup_w": inputs["L0_ffn_shared_up_w"], "sdown_w": inputs["L0_ffn_shared_down_w"],
        **shape_constants(),
    }
    arrays = {n: np.ascontiguousarray(v) for n, v in arrays.items()}
    nc = bacc.Bacc("TRN2", target_bir_lowering=False, num_devices=1)
    aps = {n: nc.dram_tensor(f"in_{n}", v.shape, mybir.dt.from_np(v.dtype), kind="ExternalInput").ap()
           for n, v in arrays.items()}
    out = nc.dram_tensor("out", (TOK + P, D), F32, kind="ExternalOutput").ap()
    build(nc, aps, out)
    r = run_bass_kernel_spmd(nc, [{f"in_{n}": v for n, v in arrays.items()}], core_ids=[0])
    return r.results[0]["out"][:TOK].reshape(B, S, D)
```
